# Optimizing a Trainium2 kernel written in Bass

```python
import numpy as np
import jax
import jax.numpy as jnp

def _softmax(x, axis=-1):
    return jax.nn.softmax(x, axis=axis)

def _gelu(x):
    return jax.nn.gelu(x, approximate=True)

def _silu(x):
    return jax.nn.silu(x)

def _sigmoid(x):
    return jax.nn.sigmoid(x)

def _layernorm(x, axis=-1, eps=1e-05):
    m = jnp.mean(x, axis=axis, keepdims=True)
    v = jnp.var(x, axis=axis, keepdims=True)
    return (x - m) / jnp.sqrt(v + eps)

def _scatter_add(tgt, idx, src, axis=0):
    return tgt.at[idx].add(src)

def _segment_sum(src, seg, n):
    return jax.ops.segment_sum(src, seg, n)
kernel_name = 'mk_decoder_preln_d1_seqx_r4_202f73'

def setup_inputs(seed: int=0):
    np.random.seed(seed)
    _w = jnp.asarray

    def _rec_inputs():
        import jax
        import jax.numpy as jnp
        _rk = jax.random.key(seed)
        x = -0.0002928 + 1 * jax.random.normal(jax.random.fold_in(_rk, 1), (8, 512, 256), jnp.float32)
        _lenS = 512 - jax.random.randint(jax.random.fold_in(_rk, 7), (8,), 0, max(1, 512 // 4) + 1, jnp.int32)
        _lenS2 = 512 - jax.random.randint(jax.random.fold_in(_rk, 8), (8,), 0, max(1, 512 // 4) + 1, jnp.int32)
        _ctx_1024P = jax.random.normal(jax.random.fold_in(_rk, 11), (8, 16, 256), jnp.float32)
        _ctx_1024c = jax.random.dirichlet(jax.random.fold_in(_rk, 511), 0.3 * jnp.ones((16,), jnp.float32), (8, 512))
        _ctx_1024t = jnp.einsum('bsk,bkd->bsd', _ctx_1024c, _ctx_1024P)
        _ctx_1024t = _ctx_1024t * jax.lax.rsqrt(jnp.mean(jnp.square(_ctx_1024t)) + 1e-12) * 0.953939
        ctx_1024 = -1.39393e-06 + 0.999914 * (_ctx_1024t + 0.3 * jax.random.normal(jax.random.fold_in(_rk, 611), (8, 512, 256), jnp.float32))
        return (x, ctx_1024)
    x, ctx_1024 = _rec_inputs()

    def _L0_attn_setup():
        import math
        import jax, jax.numpy as jnp
        import numpy as np
        from jax.scipy.special import logsumexp
        B, L, D_MODEL = (2, 256, 256)
        H = 16
        DH = D_MODEL // H
        M = 24
        WINDOW = 128
        MASK_VAL = -10000.0
        EPS = 0.0001
        SCALE = 1.0 / math.sqrt(DH)

        def _sb_features(x, proj, is_query):
            xh = x * math.sqrt(SCALE)
            x_dash = jnp.einsum('bhld,md->bhlm', xh, proj)
            diag = 0.5 * jnp.sum(xh * xh, axis=-1, keepdims=True)
            log_feat = x_dash - diag
            if is_query:
                stab = jax.lax.stop_gradient(jnp.max(log_feat, axis=-1, keepdims=True))
            else:
                stab = jax.lax.stop_gradient(jnp.max(log_feat, axis=(-2, -1), keepdims=True))
            prime = jnp.exp(log_feat - stab) + EPS
            return (prime, stab)

        def _local_mask(L):
            i = jnp.arange(L)[:, None]
            j = jnp.arange(L)[None, :]
            keep = (j <= i) & (j >= i - WINDOW)
            return jnp.where(keep, 0.0, MASK_VAL).astype(jnp.float32)
        if __name__ == '__main__':
            o = reference(**setup_inputs())
            print(o.shape, o.dtype)
        key = jax.random.key(seed)
        ks = jax.random.split(key, 4)
        x = jax.random.normal(ks[0], (B, L, D_MODEL), dtype=jnp.float32)
        Wqkv_w = jax.random.normal(ks[1], (3 * D_MODEL, D_MODEL), dtype=jnp.float32) * D_MODEL ** (-0.5)
        Wqkv_b = jnp.zeros((3 * D_MODEL,), dtype=jnp.float32)
        proj = jax.random.normal(ks[2], (M, DH), dtype=jnp.float32)
        out_w = jax.random.normal(ks[3], (D_MODEL, D_MODEL), dtype=jnp.float32) * D_MODEL ** (-0.5)
        out_b = jnp.zeros((D_MODEL,), dtype=jnp.float32)
        return {'x': x, 'Wqkv_w': Wqkv_w, 'Wqkv_b': Wqkv_b, 'proj': proj, 'out_w': out_w, 'out_b': out_b}
    _L0_attn_all = _L0_attn_setup()
    _L0_attn_in = {k: v for k, v in _L0_attn_all.items() if k in ('Wqkv_w', 'Wqkv_b', 'proj', 'out_w', 'out_b')}
    del _L0_attn_all

    def _L0_xattn_setup():
        import jax, jax.numpy as jnp
        import numpy as np
        EPS_BACKEND = 1e-06
        NORM_EPS = 1e-06
        NUM_HEADS = 4

        def _mlstm_forward(q, k, v, ig_kernel, ig_bias, fg_kernel, fg_bias, outnorm_weight):
            B, S, E = q.shape
            NH = ig_bias.shape[0]
            DH = E // NH
            gate_input = jnp.concatenate([q, k, v], axis=-1)
            igate = gate_input @ ig_kernel + ig_bias
            fgate = gate_input @ fg_kernel + fg_bias
            qh = q.reshape(B, S, NH, DH).transpose(0, 2, 1, 3)
            kh = k.reshape(B, S, NH, DH).transpose(0, 2, 1, 3)
            vh = v.reshape(B, S, NH, DH).transpose(0, 2, 1, 3)
            ig = igate.transpose(0, 2, 1)
            fg = fgate.transpose(0, 2, 1)
            log_fg = jax.nn.log_sigmoid(fg)
            cums = jnp.concatenate([jnp.zeros((B, NH, 1), log_fg.dtype), jnp.cumsum(log_fg, axis=-1)], axis=-1)
            fg_mat = cums[..., :, None] - cums[..., None, :]
            mask = jnp.tril(jnp.ones((S + 1, S + 1), bool))
            fg_mat = jnp.where(mask, fg_mat, -jnp.inf)[..., 1:, 1:]
            log_D = fg_mat + ig[..., None, :]
            max_log_D = jnp.max(log_D, axis=-1, keepdims=True)
            D = jnp.exp(log_D - max_log_D)
            qk = jnp.einsum('bnsd,bntd->bnst', qh, kh) / jnp.sqrt(jnp.float32(DH))
            C = qk * D
            normalizer = jnp.maximum(jnp.abs(C.sum(-1, keepdims=True)), jnp.exp(-max_log_D))
            h = jnp.einsum('bnst,bntd->bnsd', C / (normalizer + EPS_BACKEND), vh)
            h = h.transpose(0, 2, 1, 3)
            mean = h.mean(-1, keepdims=True)
            var = h.var(-1, keepdims=True)
            hn = (h - mean) * jax.lax.rsqrt(var + NORM_EPS) * outnorm_weight
            return hn.reshape(B, S, E)
        key = jax.random.key(seed)
        ks = jax.random.split(key, 8)
        B, S, E, NH = (2, 512, 256, NUM_HEADS)
        DH = E // NH
        q = jax.random.normal(ks[0], (B, S, E), jnp.float32)
        k = jax.random.normal(ks[1], (B, S, E), jnp.float32)
        v = jax.random.normal(ks[2], (B, S, E), jnp.float32)
        ig_kernel = jax.random.normal(ks[3], (3 * E, NH), jnp.float32) * 0.02
        fg_kernel = jax.random.normal(ks[4], (3 * E, NH), jnp.float32) * 0.02
        ig_bias = jax.random.normal(ks[5], (NH,), jnp.float32) * 0.1
        fg_bias = jnp.linspace(3.0, 6.0, NH, dtype=jnp.float32)
        outnorm_weight = jnp.ones((NH, DH), jnp.float32)
        return {'q': q, 'k': k, 'v': v, 'ig_kernel': ig_kernel, 'ig_bias': ig_bias, 'fg_kernel': fg_kernel, 'fg_bias': fg_bias, 'outnorm_weight': outnorm_weight}
    _L0_xattn_all = _L0_xattn_setup()
    _L0_xattn_in = {k: v for k, v in _L0_xattn_all.items() if k in ('ig_kernel', 'ig_bias', 'fg_kernel', 'fg_bias', 'outnorm_weight')}
    del _L0_xattn_all

    def _L0_ffn_setup():
        import jax, jax.numpy as jnp
        import numpy as np
        B, S, D, H, E = (4, 512, 256, 1024, 8)
        THRESHOLD = 0.5
        key = jax.random.key(seed)
        ks = jax.random.split(key, 7)
        s_in = 1.0 / np.sqrt(D)
        s_h = 1.0 / np.sqrt(H)
        return {'x': jax.random.normal(ks[0], (B, S, D), dtype=jnp.float32), 'Wg': jax.random.uniform(ks[1], (D, E), jnp.float32, -s_in, s_in), 'bg': jax.random.uniform(ks[2], (E,), jnp.float32, -s_in, s_in), 'W1': jax.random.uniform(ks[3], (E, D, H), jnp.float32, -s_in, s_in), 'b1': jax.random.uniform(ks[4], (E, H), jnp.float32, -s_in, s_in), 'W2': jax.random.uniform(ks[5], (E, H, D), jnp.float32, -s_h, s_h), 'b2': jax.random.uniform(ks[6], (E, D), jnp.float32, -s_h, s_h)}
    _L0_ffn_all = _L0_ffn_setup()
    _L0_ffn_in = {k: v for k, v in _L0_ffn_all.items() if k in ('Wg', 'bg', 'W1', 'b1', 'W2', 'b2')}
    del _L0_ffn_all
    return {'x': x, 'ctx_1024': ctx_1024, 'L0_attn_Wqkv_w': _L0_attn_in['Wqkv_w'], 'L0_attn_Wqkv_b': _L0_attn_in['Wqkv_b'], 'L0_attn_proj': _L0_attn_in['proj'], 'L0_attn_out_w': _L0_attn_in['out_w'], 'L0_attn_out_b': _L0_attn_in['out_b'], 'L0_xattn_ig_kernel': _L0_xattn_in['ig_kernel'], 'L0_xattn_ig_bias': _L0_xattn_in['ig_bias'], 'L0_xattn_fg_kernel': _L0_xattn_in['fg_kernel'], 'L0_xattn_fg_bias': _L0_xattn_in['fg_bias'], 'L0_xattn_outnorm_weight': _L0_xattn_in['outnorm_weight'], 'L0_ffn_Wg': _L0_ffn_in['Wg'], 'L0_ffn_bg': _L0_ffn_in['bg'], 'L0_ffn_W1': _L0_ffn_in['W1'], 'L0_ffn_b1': _L0_ffn_in['b1'], 'L0_ffn_W2': _L0_ffn_in['W2'], 'L0_ffn_b2': _L0_ffn_in['b2']}

def reference(x, ctx_1024, L0_attn_Wqkv_w, L0_attn_Wqkv_b, L0_attn_proj, L0_attn_out_w, L0_attn_out_b, L0_xattn_ig_kernel, L0_xattn_ig_bias, L0_xattn_fg_kernel, L0_xattn_fg_bias, L0_xattn_outnorm_weight, L0_ffn_Wg, L0_ffn_bg, L0_ffn_W1, L0_ffn_b1, L0_ffn_W2, L0_ffn_b2):
    import jax
    import jax.numpy as jnp

    def _L0_attn_ref(x, Wqkv_w, Wqkv_b, proj, out_w, out_b):
        import math
        import jax, jax.numpy as jnp
        import numpy as np
        from jax.scipy.special import logsumexp
        B, L, D_MODEL = (2, 256, 256)
        H = 16
        DH = D_MODEL // H
        M = 24
        WINDOW = 128
        MASK_VAL = -10000.0
        EPS = 0.0001
        SCALE = 1.0 / math.sqrt(DH)

        def _sb_features(x, proj, is_query):
            xh = x * math.sqrt(SCALE)
            x_dash = jnp.einsum('bhld,md->bhlm', xh, proj)
            diag = 0.5 * jnp.sum(xh * xh, axis=-1, keepdims=True)
            log_feat = x_dash - diag
            if is_query:
                stab = jax.lax.stop_gradient(jnp.max(log_feat, axis=-1, keepdims=True))
            else:
                stab = jax.lax.stop_gradient(jnp.max(log_feat, axis=(-2, -1), keepdims=True))
            prime = jnp.exp(log_feat - stab) + EPS
            return (prime, stab)

        def _local_mask(L):
            i = jnp.arange(L)[:, None]
            j = jnp.arange(L)[None, :]
            keep = (j <= i) & (j >= i - WINDOW)
            return jnp.where(keep, 0.0, MASK_VAL).astype(jnp.float32)
        if __name__ == '__main__':
            o = reference(**setup_inputs())
            print(o.shape, o.dtype)
        b, l, dm = x.shape
        qkv = (x @ Wqkv_w.T + Wqkv_b).reshape(b, l, 3, H, DH)
        q = jnp.transpose(qkv[:, :, 0], (0, 2, 1, 3))
        k = jnp.transpose(qkv[:, :, 1], (0, 2, 1, 3))
        v = jnp.transpose(qkv[:, :, 2], (0, 2, 1, 3))
        q_prime, q_ls = _sb_features(q, proj, is_query=True)
        k_prime, k_ls = _sb_features(k, proj, is_query=False)
        global_scale = q_ls + k_ls
        global_out_cumsum = jnp.einsum('bhnm,bhnm->bhn', q_prime, jnp.cumsum(k_prime, axis=-2))
        kv = jnp.cumsum(k_prime[..., :, :, None] * v[..., :, None, :], axis=-3)
        global_out = jnp.einsum('bhlm,bhlmd->bhld', q_prime, kv)
        mask = _local_mask(l)
        g_scores = jnp.einsum('bhmd,bhnd->bhmn', q_prime, k_prime) * SCALE + mask
        global_qk = jnp.where(g_scores <= 0, 0.0, g_scores)
        l_scores = jnp.einsum('bhmd,bhnd->bhmn', q, k) * SCALE + mask
        QK_lse = logsumexp(l_scores, axis=-1, keepdims=True)
        gqk_sum = jnp.sum(global_qk, axis=-1, keepdims=True)
        g_log_norm = jnp.log(jnp.clip(global_out_cumsum[..., None] - gqk_sum, 1e-24)) + global_scale
        log_norm = jnp.logaddexp(QK_lse, g_log_norm)
        g_prime_scale = jnp.exp(global_scale - log_norm)
        local_score = jax.nn.softmax(l_scores - log_norm, axis=-1) - global_qk * g_prime_scale
        out = jnp.einsum('bhmn,bhnd->bhmd', local_score, v) + global_out * g_prime_scale
        ctx = jnp.transpose(out, (0, 2, 1, 3)).reshape(b, l, dm)
        return ctx @ out_w.T + out_b

    def _L0_xattn_ref(q, k, v, ig_kernel, ig_bias, fg_kernel, fg_bias, outnorm_weight):
        import jax, jax.numpy as jnp
        import numpy as np
        EPS_BACKEND = 1e-06
        NORM_EPS = 1e-06
        NUM_HEADS = 4

        def _mlstm_forward(q, k, v, ig_kernel, ig_bias, fg_kernel, fg_bias, outnorm_weight):
            B, S, E = q.shape
            NH = ig_bias.shape[0]
            DH = E // NH
            gate_input = jnp.concatenate([q, k, v], axis=-1)
            igate = gate_input @ ig_kernel + ig_bias
            fgate = gate_input @ fg_kernel + fg_bias
            qh = q.reshape(B, S, NH, DH).transpose(0, 2, 1, 3)
            kh = k.reshape(B, S, NH, DH).transpose(0, 2, 1, 3)
            vh = v.reshape(B, S, NH, DH).transpose(0, 2, 1, 3)
            ig = igate.transpose(0, 2, 1)
            fg = fgate.transpose(0, 2, 1)
            log_fg = jax.nn.log_sigmoid(fg)
            cums = jnp.concatenate([jnp.zeros((B, NH, 1), log_fg.dtype), jnp.cumsum(log_fg, axis=-1)], axis=-1)
            fg_mat = cums[..., :, None] - cums[..., None, :]
            mask = jnp.tril(jnp.ones((S + 1, S + 1), bool))
            fg_mat = jnp.where(mask, fg_mat, -jnp.inf)[..., 1:, 1:]
            log_D = fg_mat + ig[..., None, :]
            max_log_D = jnp.max(log_D, axis=-1, keepdims=True)
            D = jnp.exp(log_D - max_log_D)
            qk = jnp.einsum('bnsd,bntd->bnst', qh, kh) / jnp.sqrt(jnp.float32(DH))
            C = qk * D
            normalizer = jnp.maximum(jnp.abs(C.sum(-1, keepdims=True)), jnp.exp(-max_log_D))
            h = jnp.einsum('bnst,bntd->bnsd', C / (normalizer + EPS_BACKEND), vh)
            h = h.transpose(0, 2, 1, 3)
            mean = h.mean(-1, keepdims=True)
            var = h.var(-1, keepdims=True)
            hn = (h - mean) * jax.lax.rsqrt(var + NORM_EPS) * outnorm_weight
            return hn.reshape(B, S, E)
        return _mlstm_forward(q, k, v, ig_kernel, ig_bias, fg_kernel, fg_bias, outnorm_weight)

    def _L0_ffn_ref(x, Wg, bg, W1, b1, W2, b2):
        import jax, jax.numpy as jnp
        import numpy as np
        B, S, D, H, E = (4, 512, 256, 1024, 8)
        THRESHOLD = 0.5
        b, s, d = x.shape
        x_flat = x.reshape(-1, d)
        probs = jax.nn.sigmoid(x_flat @ Wg + bg)
        mask = (probs > THRESHOLD).astype(x_flat.dtype)
        weights = probs * mask
        h = jax.nn.relu(jnp.einsum('td,edh->eth', x_flat, W1) + b1[:, None, :])
        expert_out = jnp.einsum('eth,ehd->etd', h, W2) + b2[:, None, :]
        combined = jnp.einsum('te,etd->td', weights, expert_out)
        return combined.reshape(b, s, d)
    x = x + _L0_attn_ref(_layernorm(x, axis=-1), L0_attn_Wqkv_w, L0_attn_Wqkv_b, L0_attn_proj, L0_attn_out_w, L0_attn_out_b)
    x = x + _L0_xattn_ref(_layernorm(x, axis=-1), ctx_1024, ctx_1024, L0_xattn_ig_kernel, L0_xattn_ig_bias, L0_xattn_fg_kernel, L0_xattn_fg_bias, L0_xattn_outnorm_weight)
    x = x + _L0_ffn_ref(_layernorm(x, axis=-1), L0_ffn_Wg, L0_ffn_bg, L0_ffn_W1, L0_ffn_b1, L0_ffn_W2, L0_ffn_b2)
    return x

_drawn_inputs = setup_inputs


def setup_inputs(seed=0):
    import zlib

    import numpy as np

    out = dict(_drawn_inputs(seed))
    spreads = {'L0_attn_Wqkv_b': (0.0, 0.1),
     'L0_attn_out_b': (0.0, 0.1),
     'L0_xattn_outnorm_weight': (1.0, 0.2)}
    factors = {'L0_xattn_ig_bias': 8.0, 'L0_ffn_b1': 5.733, 'L0_ffn_b2': 4.587}
    for name, (base, spread) in spreads.items():
        noise = np.random.default_rng([zlib.crc32(name.encode()), seed]).standard_normal(out[name].shape)
        drawn = base * np.exp(spread * noise) if base else spread * noise
        out[name] = jnp.asarray(drawn.astype(out[name].dtype))
    for name, factor in factors.items():
        out[name] = (out[name] * factor).astype(out[name].dtype)
    return out
```

```python
import concourse.bass as bass
from concourse import mybir
from contextlib import ExitStack

F32 = mybir.dt.float32
F32R = mybir.dt.float32r
ALU = mybir.AluOpType
ACT = mybir.ActivationFunctionType
AX = mybir.AxisListType

P = 128
NB = 8
L = 512
D = 256
NT = L // P
KC = D // P
H = 16
DH = D // H
M = 24
MP = 32
HG = 4
NG = H // HG
QROWS = 80
FROWS = 3 * M
NH = 4
XD = D // NH
NE = 8
HID = 1024
NK = HID // P
NTOK = NB * L
NGRP = NTOK // L
SCALE = DH ** -0.5
FEAT_EPS = 1e-4
MASK_VAL = -10000.0
LN_EPS = 1e-5
X_EPS = 1e-6


def pe_groups():
    g = [(("x1T", t), "C%d" % (t % 2)) for t in range(NT)]
    for s in range(NT + 2):
        if s < NT:
            g += [(("qk", s), "A%d" % (s % 2)), (("v", s), "B%d" % (s % 2))]
        if 1 <= s <= NT:
            g.append((("qkT", s - 1), "C%d" % ((s - 1) % 2)))
        if 2 <= s:
            g += [(("xdq", s - 2), "D"), (("xdk", s - 2), "E")]
    g += [(("mkT",), "A0"), (("mkB",), "A1")]
    g += [(("qfT", 0), "C0"), (("kfT", 0), "C1")]
    for c in range(NT):
        g.append((("u", c), "E"))
        if c >= 2:
            g += [(("kv", c), "D"), (("st", c), "E")]
        g += [(("s", c, u), "A%d" % (u % 2)) for u in range(H // 2)]
        if c + 1 < NT:
            g += [(("qfT", c + 1), "C0"), (("kfT", c + 1), "C1")]
        for s in range(H // 2 + 2):
            if s < H // 2:
                g.append((("sg", c, s), "B%d" % (s % 2)))
            if 1 <= s <= H // 2:
                g.append((("pT", c, s - 1), "C%d" % ((s - 1) % 2)))
            if s == 2:
                g.append((("pv", c), "D"))
        g += [(("oT", c), "A0"), (("cT", c), "A1"), (("proj", c), "B0")]
    g += [(("cxT", t), "B%d" % (t % 2)) for t in range(NT)]
    g += [(("x2T", t), "C%d" % (t % 2)) for t in range(NT)]
    g += [(("gate",), "D"), (("rowT",), "E")]
    for h in range(NH):
        g.append((("mB", h), "A%d" % (h % 2)))
        g += [(("qkm", h, tc), ("B0", "B1", "C0", "C1")[tc]) for tc in range(NT)]
    g += [(("h", sc), "DE"[sc % 2]) for sc in range(NT)]
    g += [(("x3T", t), "C%d" % (t % 2)) for t in range(NT)]
    g += [(("z",), "A0"), (("wT",), "A1")]
    g += [(("b2", t), "B%d" % (t % 2)) for t in range(NT)]
    return g


BANKS = ("A0", "A1", "B0", "B1", "C0", "C1", "D", "E")
GROUPS = pe_groups()
BANK_OF = dict(GROUPS)
USES = {x: [n for n, bank in GROUPS if bank == x] for x in BANKS}

CONST_DMA = 16 * 22
CONSTS_READY = 8

LINKS = {"dve": 60, "act": 2, "pool": 4}


def hold(eng, held):
    eng.sem_inc(held, 1)


def decoder_kernel(nc, x, ctx, wqkv, bqkv, proj, wo, bo, igk, igb, fgk, fgb, onw, wg, bg, w1, b1, w2, b2, out):
    x2_dram = nc.dram_tensor("x2_dram", [NB, P, NT, D], F32, kind="Internal").ap()
    x3_dram = nc.dram_tensor("x3_dram", [NB, 2, P, KC, L], F32, kind="Internal").ap()
    qk_dram = nc.dram_tensor("qk_dram", [NT, 2, 4, P, P], F32, kind="Internal").ap()
    f_dram = nc.dram_tensor("f_dram", [2, 2, 2, NG, P, P], F32, kind="Internal").ap()

    with ExitStack() as stack:
        def sem(name):
            return stack.enter_context(nc.semaphore(name))

        def sb0(name, shape, dt=F32):
            return stack.enter_context(nc.sbuf_tensor(name, shape, dt))

        banks = {x: stack.enter_context(nc.psum_tensor("bank" + x, [P, 512], F32)) for x in BANKS}
        wtok = sb0("wtok", [P, NB * NT, NE])
        attention_phase(nc, sem, banks, wtok, x, ctx, wqkv, bqkv, proj, wo, bo, igk, igb, fgk, fgb,
                        onw, wg, bg, b2, x2_dram, x3_dram, qk_dram, f_dram)
        ffn_phase(nc, sem, banks, wtok, w1, b1, w2, x2_dram, x3_dram, out)


def attention_phase(nc, sem, banks, wtok, x, ctx, wqkv, bqkv, proj, wo, bo, igk, igb, fgk, fgb,
                    onw, wg, bg, b2, x2_dram, x3_dram, qk_dram, f_dram):
    full = {b: sem("full_" + b) for b in BANKS}
    evac = {b: sem("evac_" + b) for b in BANKS}
    consts_loaded, consts_made, consts_ready = sem("consts_loaded"), sem("consts_made"), sem("consts_ready")
    x_loaded, x_free, xb_ready = sem("x_loaded"), sem("x_free"), sem("xb_ready")
    ctx_loaded, ctx_free = sem("ctx_loaded"), sem("ctx_free")
    ln_stats, ln_rstd, xhat_ready = sem("ln_stats"), sem("ln_rstd"), sem("xhat_ready")
    sq_ready, sq_read, qkh_ready = sem("sq_ready"), sem("sq_read"), sem("qkh_ready")
    qk_stored = [sem("qk_stored%d" % i) for i in range(2)]
    f_stored, qs_loaded, fs_loaded = sem("f_stored"), sem("qs_loaded"), sem("fs_loaded")
    qf_exp, qf_ready, kf_sub, kf_exp, kf_ready = sem("qf_exp"), sem("qf_ready"), sem("kf_sub"), sem("kf_exp"), sem("kf_ready")
    mk_ready, kmax_diag = sem("mk_ready"), sem("kmax_diag")
    fh_ready = sem("fh_ready")
    nmx_ready, t_ready, e1_ready = sem("nmx_ready"), sem("t_ready"), sem("e1_ready")
    p_ready, c_ready = sem("p_ready"), sem("c_ready")
    lsig_ready, nm_ready, negm_ready, expn_ready = sem("lsig_ready"), sem("nm_ready"), sem("negm_ready"), sem("expn_ready")
    d_ready, dmask_ready = sem("d_ready"), sem("dmask_ready")
    x3h_ready, w_ready, x2_stored, x3_stored = sem("x3h_ready"), sem("w_ready"), sem("x2_stored"), sem("x3_stored")
    held = {e: sem("held_" + e) for e in ("pe", "dve", "pool", "sp")}
    dve_link, act_link, pool_link = sem("dve_link"), sem("act_link"), sem("pool_link")

    with ExitStack() as stack:
        def sb(name, shape, dt=F32):
            return stack.enter_context(nc.sbuf_tensor(name, shape, dt))

        wqkv_sb = sb("wqkv_sb", [P, KC, 3 * D])
        bqkv_bc = sb("bqkv_bc", [P, 3 * D])
        wo_sb = sb("wo_sb", [P, KC, D])
        bo_bc = sb("bo_bc", [P, D])
        pd = sb("pd", [P, H // 2, MP])
        pdh = sb("pdh", [P, H // 2, MP], F32R)
        pdl = sb("pdl", [P, H // 2, MP], F32R)
        win = sb("win", [P, 3, 2, P])
        maskf = sb("maskf", [P, 3, 2, P])
        maskr = sb("maskr", [P, 3, 2, P], F32R)
        ident = sb("ident", [P, P])
        identr = sb("identr", [P, P], F32R)
        wdT = sb("wdT", [P, P])
        wpT = sb("wpT", [P, P])
        ones = sb("ones", [P, P])
        blk = sb("blk", [P, HG * DH])
        gk = sb("gk", [P, 2 * KC, 36])
        gkv = sb("gkv", [P, KC, 36])
        igb_sb = sb("igb_sb", [4, 1])
        fgb_sb = sb("fgb_sb", [36, 1])
        onw_bc = sb("onw_bc", [P, D])
        sel = sb("sel", [4, NH, P])
        ones_row = sb("ones_row", [36, L])
        wg_sb = sb("wg_sb", [P, KC, NE])
        wgh = sb("wgh", [P, KC, NE], F32R)
        wgl = sb("wgl", [P, KC, NE], F32R)
        nbg = sb("nbg", [NE, 1])
        b2_sb = sb("b2_sb", [NE, D])
        mhalf = sb("mhalf", [P, H])

        x_in = sb("x_in", [P, NT, D])
        x1 = sb("x1", [P, NT, D])
        ctx_in = sb("ctx_in", [P, NT, NH, XD + 1])
        xh = sb("xh", [P, NT, D])
        xT = sb("xT", [P, KC, L])
        st6 = sb("st6", [P, NT * NH, 6])
        mv = sb("mv", [P, NT * NH, 2])
        rstd = sb("rstd", [P, NT * NH])
        rstd_in = sb("rstd_in", [P, NT * NH])
        qk_tm = sb("qk_tm", [P, 2, 2 * D])
        v_tm = sb("v_tm", [P, NT, H, MP])
        sqt = sb("sqt", [P, 2, 2 * D])
        sq = sb("sq", [P, NT, 2 * H])
        qkhl = sb("qkhl", [P, 2, 2, 4, P], F32R)
        qf = sb("qf", [P, NT, H, MP])
        kf = sb("kf", [P, NT, H, MP])
        mq = sb("mq", [P, NT, H])
        mk = sb("mk", [P, NT, H])
        mk1 = sb("mk1", [P, H])
        kmx = sb("kmx", [H, 1])
        kdg = sb("kdg", [H, H])
        kb = sb("kb", [P, H])
        gs = sb("gs", [P, NT, H])
        fhl = sb("fhl", [P, 2, 2, NG, P], F32R)
        qf32 = sb("qf32", [P, NG, P])
        qs = sb("qs", [QROWS, H, P], F32R)
        ks = sb("ks", [QROWS, H, 2, P], F32R)
        qfs = sb("qfs", [FROWS, H, P], F32R)
        kfs = sb("kfs", [FROWS, H, 2, P], F32R)
        E = sb("E", [P, H, 2, P])
        GP = sb("GP", [P, 2, 2, 2, 2, P])
        GW, PT = GP[:, 0, :, :, :, :], GP[:, 1, :, :, :, :]
        OT = sb("OT", [P, NG, P])
        nmx = sb("nmx", [P, H])
        sume = sb("sume", [P, H])
        gsum = sb("gsum", [P, H])
        tt = sb("tt", [P, H])
        e1 = sb("e1", [P, H])
        gps = sb("gps", [P, H])
        aa = sb("aa", [P, H])
        rs = sb("rs", [P, H])
        ut = sb("ut", [P, H, M])
        kvs = sb("kvs", [P, NG, HG * DH])
        stt = sb("stt", [P, H, DH])
        cc = sb("cc", [P, H, DH])
        cT = sb("cT", [P, KC, P])
        ctx_t = sqt[:, :, :].rearrange("p a n -> p (a n)").rearrange("p (t d) -> p t d", t=NT)
        cxT = sb("cxT", [P, KC, L])
        rows = sb("rows", [36, 6, L])
        gT = sb("gT", [P, NT, 2, NH])
        Dm = sb("Dm", [P, 2, L])
        nrm = sb("nrm", [P, 2, NH])
        x3h, x3l = (fhl[:, i, :, :, :].rearrange("p s g n -> p (s g n)").rearrange("p (k n) -> p k n", k=KC)
                    for i in range(2))
        zr = rows[0:NE, 0:3, :]

        R_ABS, R_MIN, R_F, R_G, R_M, R_NM = range(6)
        CT_LEN = sum(L - tc * P for tc in range(NT))
        GP_row = GP[:, :, :, :, :, :].rearrange("p w a b c n -> p (w a b c n)")
        E_row = E[:, :, :, :].rearrange("p a b c -> p (a b c)")

        def ct(h, tc, a, b):
            o = h * CT_LEN + sum(L - i * P for i in range(tc))
            if h < 3:
                return E_row[:, o + a:o + b]
            o -= 3 * CT_LEN
            return GP_row[:, o + a:o + b]

        def variant(c):
            return 2 if c == 0 else c % 2

        def at(b, name):
            bank = BANK_OF[name]
            return b * len(USES[bank]) + USES[bank].index(name) + 1

        def wait_full(eng, b, *name):
            eng.wait_ge(full[BANK_OF[name]], at(b, name))

        def wait_evac(eng, b, *name):
            eng.wait_ge(evac[BANK_OF[name]], at(b, name) + 1)

        def wait_bank(pe, b, *name):
            pe.wait_ge(evac[BANK_OF[name]], at(b, name))

        def bank(*name):
            return banks[BANK_OF[name]]

        def evac_of(*name):
            return evac[BANK_OF[name]]

        def full_of(*name):
            return full[BANK_OF[name]]

        def linker(eng, link_sem, b, key):
            n = [0]

            def link(ins):
                n[0] += 1
                ins.then_inc(link_sem, 1)
                eng.wait_ge(link_sem, b * LINKS[key] + n[0])
            return link, n

        block = stack.enter_context(nc.Block())

        @block.sync
        def _(sp):
            for dst, src in (
                (wqkv_sb[:, :, :], wqkv.rearrange("(k p) n -> p k n", p=P)),
                (bqkv_bc[:, :], bqkv.partition_broadcast(P)),
                (wo_sb[:, :, :], wo.rearrange("(k p) n -> p k n", p=P)),
                (bo_bc[:, :], bo.partition_broadcast(P)),
                (igb_sb[:, :], igb), (fgb_sb[32:36, :], fgb),
                (onw_bc[:, :], onw.partition_broadcast(P)),
                (wg_sb[:, :, :], wg.rearrange("(k p) n -> p k n", p=P)),
                (nbg[:, :], bg), (b2_sb[:, :], b2),
            ):
                sp.dma_start(dst, src).then_inc(consts_loaded, 16)
            sp.wait_ge(consts_made, 3)
            for h in range(H // 2):
                sp.dma_start(pd[DH * h:DH * h + DH, h, 0:M], proj).then_inc(consts_loaded, 16)
            for (kern, at) in ((igk, 0), (fgk, 32)):
                v = kern.rearrange("(k p) n -> p k n", p=P)
                sp.dma_start(gk[:, 0:2 * KC, at:at + NH], v[:, 0:2 * KC, :]).then_inc(consts_loaded, 16)
                sp.dma_start(gkv[:, :, at:at + NH], v[:, 2 * KC:3 * KC, :]).then_inc(consts_loaded, 16)
            with sp.Fori(0, NB) as b:
                sp.wait_ge(x_free, b + 1)
                hold(sp, held["sp"])
                sp.dma_start(x_in[:, :, :], x[bass.ds(b, 1), :, :].rearrange("o (t p) d -> p (o t) d", p=P))\
                  .then_inc(x_loaded, 16)
                sp.wait_ge(ctx_free, b + 1)
                hold(sp, held["sp"])
                for t in range(NT):
                    src = ctx[bass.ds(b, 1), t * P:(t + 1) * P, :].rearrange("o p (h d) -> p (o h) d", h=NH)
                    sp.dma_start(ctx_in[:, t, :, 0:XD], src).then_inc(ctx_loaded, 16)
                for t in range(NT):
                    wait_evac(sp, b, "qkT", t)
                    for s in range(2):
                        sp.dma_start(qk_dram[t, s, :, :, :].rearrange("j p n -> p j n"),
                                     qkhl[:, t % 2, s, :, :].bitcast(F32)).then_inc(qk_stored[t % 2], 16)

                sp.wait_ge(sq_read, b * NT + NT)
                hold(sp, held["sp"])
                sp.dma_start(ctx_t, ctx[bass.ds(b, 1), :, :].rearrange("o (t p) d -> p (o t) d", p=P)).then_inc(ctx_loaded, 16)

                def load_dots(c):
                    for stored in qk_stored:
                        sp.wait_ge(stored, b * 16 * NT + 16 * NT)
                        hold(sp, held["sp"])
                    if c:
                        wait_full(sp, b, "s", c - 1, H // 2 - 1)
                    for r, s in ((0, 0), (1, 1), (2, 0), (3, 1)):
                        sp.dma_start(qs[DH * r:DH * r + DH, :, :].bitcast(F32),
                                     qk_dram[c, s, 0:2, :, :].rearrange("j (h d) n -> d (j h) n", d=DH))\
                          .then_inc(qs_loaded, 16)
                    for r, s in ((0, 0), (1, 0), (2, 1), (3, 1)):
                        sp.dma_start(ks[DH * r:DH * r + DH, :, c % 2, :].bitcast(F32),
                                     qk_dram[c, s, 2:4, :, :].rearrange("j (h d) n -> d (j h) n", d=DH))\
                          .then_inc(qs_loaded, 16)

                def move_features(c):
                    wait_evac(sp, b, "kfT", c)
                    for w in range(2):
                        for s in range(2):
                            sp.dma_start(f_dram[c % 2, w, s, :, :, :].rearrange("g p n -> p g n"),
                                         fhl[:, w, s, :, :].bitcast(F32)).then_inc(f_stored, 16)
                    sp.wait_ge(f_stored, b * 64 * NT + 64 * (c + 1))
                    hold(sp, held["sp"])
                    if c:
                        wait_full(sp, b, "sg", c - 1, H // 2 - 1)
                    for w, dst, parts in ((0, qfs[:, :, :], (0, 1, 0)), (1, kfs[:, :, c % 2, :], (0, 0, 1))):
                        for r, s in enumerate(parts):
                            sp.dma_start(dst[M * r:M * r + M, :, :].bitcast(F32),
                                         f_dram[c % 2, w, s, :, :, :].rearrange("g (h m) n -> m (g h) n", m=MP)[0:M, :, :])\
                              .then_inc(fs_loaded, 16)

                load_dots(0)
                move_features(0)
                for c in range(1, NT):
                    load_dots(c)
                    move_features(c)
                wait_evac(sp, b, "x3T", NT - 1)
                hold(sp, held["sp"])
                for s, part in enumerate((x3h, x3l)):
                    sp.dma_start(x3_dram[bass.ds(b, 1), s, :, :, :].rearrange("o p k n -> p (o k) n"),
                                 part[:, :, :].bitcast(F32)).then_inc(x3_stored, 16)
                wait_evac(sp, b, "b2", NT - 1)
                hold(sp, held["sp"])
                sp.dma_start(x2_dram[bass.ds(b, 1), :, :, :].rearrange("o p t d -> p (o t) d"),
                             x1[:, :, :]).then_inc(x2_stored, 16)
            sp.wait_ge(x2_stored, 16 * NB + 16)
            sp.wait_ge(x3_stored, 32 * NB + 32)

        @block.gpsimd
        def _(pool):
            def make(ins):
                ins.then_inc(consts_made, 1)
                n_made[0] += 1

            n_made = [0]
            make(nc.gpsimd.memset(pd[:, :, :], 0.0))
            make(nc.gpsimd.memset(gk[:, :, :], 0.0))
            make(nc.gpsimd.memset(gkv[:, :, :], 0.0))
            make(nc.gpsimd.memset(ident[:, :], 0.0))
            make(nc.gpsimd.memset(ones[:, :], 1.0))
            make(nc.gpsimd.memset(maskf[:, :, :, :], 0.0))
            make(nc.gpsimd.memset(blk[:, :], 1.0))
            make(nc.gpsimd.memset(sel[:, :, :], 0.0))
            make(nc.gpsimd.memset(mhalf[:, :], -0.5))
            make(nc.gpsimd.memset(ones_row[:, :], 1.0))
            make(nc.gpsimd.memset(v_tm[:, :, :, :], 0.0))
            make(nc.gpsimd.memset(qf[:, :, :, :], 0.0))
            make(nc.gpsimd.memset(kf[:, :, :, :], 0.0))
            make(nc.gpsimd.memset(ctx_in[:, :, :, XD:XD + 1], 1.0))
            make(nc.gpsimd.memset(qs[:, :, :].bitcast(F32), 0.0))
            make(nc.gpsimd.memset(ks[:, :, :, :].bitcast(F32), 0.0))
            make(nc.gpsimd.memset(kfs[:, :, :, :].bitcast(F32), 0.0))
            pool.wait_ge(consts_made, n_made[0])

            def select(out, src, pattern, op, fill, base, mult):
                make(nc.gpsimd.affine_select(out=out, in_=src, pattern=pattern, compare_op=op, fill=fill,
                                             base=base, channel_multiplier=mult))
                pool.wait_ge(consts_made, n_made[0])

            select(ident[:, :], ident[:, :], [[-1, P]], ALU.not_equal, 1.0, 0, 1)
            bv = blk[:, :].rearrange("p (h d) -> p h d", h=HG)
            select(bv, bv, [[-MP, HG], [0, DH]], ALU.is_ge, 0.0, 0, 1)
            select(bv, bv, [[MP, HG], [0, DH]], ALU.is_ge, 0.0, MP - 1, -1)
            select(sel[:, :, :], sel[:, :, :], [[-1, NH], [0, P]], ALU.not_equal, 1.0, 0, 1)
            for v, (cur, prev) in enumerate(((0, 1), (1, 0), (0, 1))):
                w = win[:, v, cur, :]
                make(nc.gpsimd.memset(w, 1.0 - SCALE))
                pool.wait_ge(consts_made, n_made[0])
                select(w, w, [[-1, P]], ALU.is_ge, 0.0, 0, 1)
                f = maskf[:, v, cur, :]
                select(f, f, [[-1, P]], ALU.is_ge, MASK_VAL, 0, 1)
                w, f = win[:, v, prev, :], maskf[:, v, prev, :]
                make(nc.gpsimd.memset(w, 0.0 if v == 2 else 1.0 - SCALE))
                pool.wait_ge(consts_made, n_made[0])
                if v == 2:
                    make(nc.gpsimd.memset(f, MASK_VAL))
                    pool.wait_ge(consts_made, n_made[0])
                else:
                    select(w, w, [[1, P]], ALU.is_ge, 1.0, 0, -1)
                    select(f, f, [[1, P]], ALU.is_ge, MASK_VAL, 0, -1)
            make(nc.gpsimd.memset(wdT[:, :], 1.0 - SCALE))
            make(nc.gpsimd.memset(wpT[:, :], 1.0 - SCALE))
            pool.wait_ge(consts_made, n_made[0])
            select(wdT[:, :], wdT[:, :], [[1, P]], ALU.is_ge, 0.0, 0, -1)
            select(wpT[:, :], wpT[:, :], [[-1, P]], ALU.is_ge, 1.0, 0, 1)
            pool.wait_ge(consts_loaded, 16 * 22)
            nc.gpsimd.tensor_tensor(gk[:, KC:2 * KC, :], gk[:, KC:2 * KC, :], gkv[:, :, :], ALU.add)\
              .then_inc(consts_ready, 1)
            nc.gpsimd.tensor_scalar(nbg[:, :], nbg[:, :], -1.0, None, ALU.mult).then_inc(consts_ready, 1)
            pool.sem_inc(x_free, 1)
            pool.sem_inc(ctx_free, 1)
            pool.sem_inc(x2_stored, 16)
            pool.sem_inc(x3_stored, 32)
            for k in BANKS:
                pool.sem_inc(evac[k], 1)

            with pool.Fori(0, NB) as b:
                link, n_links = linker(pool, pool_link, b, "pool")

                def rsqrt(k, n, eps):
                    pool.wait_ge(ln_stats, b * 4 + k + 1)
                    hold(pool, held["pool"])
                    link(nc.gpsimd.tensor_scalar(rstd_in[:, 0:n], mv[:, 0:n, 1], eps, None, ALU.add))
                    nc.gpsimd.tensor_tensor(rstd[:, 0:n], rstd_in[:, 0:n], mhalf[:, 0:n], ALU.pow)\
                      .then_inc(ln_rstd, 1)

                rsqrt(0, NT, LN_EPS)
                pool.wait_ge(xhat_ready, b * 3 * NT + NT)
                nc.gpsimd.tensor_tensor(x_in[:, :, :], x_in[:, :, :],
                                        bo_bc[:, :].unsqueeze(1).to_broadcast([P, NT, D]), ALU.add)\
                  .then_inc(xb_ready, 1)

                def add_eps_q(t):
                    pool.wait_ge(qf_exp, b * NT + t + 1)
                    hold(pool, held["pool"])
                    nc.gpsimd.tensor_scalar(qf[:, t, :, 0:M], qf[:, t, :, 0:M], FEAT_EPS, None, ALU.add)\
                      .then_inc(qf_ready, 1)

                for t in range(NT):
                    wait_evac(pool, b, "qk", t)
                    if t >= 2:
                        pool.wait_ge(sq_read, b * NT + t - 1)
                    nc.gpsimd.tensor_tensor(sqt[:, t % 2, :], qk_tm[:, t % 2, :], qk_tm[:, t % 2, :], ALU.mult)\
                      .then_inc(sq_ready, 1)
                    if t >= 2:
                        add_eps_q(t - 2)
                add_eps_q(NT - 2)
                add_eps_q(NT - 1)
                for t in range(NT):
                    pool.wait_ge(kf_exp, b * NT + t + 1)
                    hold(pool, held["pool"])
                    nc.gpsimd.tensor_scalar(kf[:, t, :, 0:M], kf[:, t, :, 0:M], FEAT_EPS, None, ALU.add)\
                      .then_inc(kf_ready, 1)
                for c in range(NT):
                    for u in range(H // 2):
                        wait_evac(pool, b, "s", c, u)
                        wait_evac(pool, b, "sg", c, u)
                        nc.gpsimd.tensor_tensor(E[:, 2 * u:2 * u + 2, :, :], E[:, 2 * u:2 * u + 2, :, :],
                                                GW[:, u % 2, :, :, :], ALU.add).then_inc(p_ready, 1)
                rsqrt(1, NT, LN_EPS)
                for h in range(NH):
                    for tc in range(NT):
                        if tc < NT - 1:
                            pool.wait_ge(d_ready, b * NH * (NT - 1) + h * (NT - 1) + tc + 1)
                        else:
                            wait_evac(pool, b, "mB", h)
                        hold(pool, held["pool"])
                        nc.gpsimd.affine_select(out=Dm[:, tc % 2, 0:P], in_=Dm[:, tc % 2, 0:P], pattern=[[1, P]],
                                                compare_op=ALU.is_ge, fill=0.0, base=0, channel_multiplier=-1)\
                          .then_inc(dmask_ready, 1)
                rsqrt(2, NT * NH, X_EPS)
                rsqrt(3, NT, LN_EPS)
            assert n_links[0] == LINKS["pool"], ("pool", n_links)

        @block.scalar
        def _(act):
            act.wait_ge(consts_ready, CONSTS_READY)
            with act.Fori(0, NB) as b:
                link, n_links = linker(act, act_link, b, "act")

                def copy_xT(name, t):
                    wait_full(act, b, name, t)
                    src = bank(name, t)[:, 0:D].rearrange("p (k n) -> p k n", k=KC)
                    nc.scalar.activation(xT[:, :, t * P:(t + 1) * P], src, ACT.Copy).then_inc(evac_of(name, t), 1)

                def qk_high(t):
                    wait_full(act, b, "qkT", t)
                    if t >= 2:
                        wait_full(act, b, "xdk", t - 2)
                        act.wait_ge(qk_stored[t % 2], b * 16 * NT + 32 * (t // 2))
                    nc.scalar.activation(qkhl[:, t % 2, 0, :, :], bank("qkT", t)[:, :].rearrange("p (j n) -> p j n", j=4),
                                         ACT.Copy, scale=SCALE ** 0.5).then_inc(qkh_ready, 1)

                def q_exp(t):
                    wait_evac(act, b, "xdq", t)
                    nc.scalar.activation(qf[:, t, :, 0:M], qf[:, t, :, 0:M], ACT.Exp).then_inc(qf_exp, 1)

                for t in range(NT):
                    copy_xT("x1T", t)
                for t in range(NT):
                    qk_high(t)
                    if t >= 1:
                        q_exp(t - 1)
                q_exp(NT - 1)
                for t in range(NT):
                    act.wait_ge(kf_sub, b * NT + t + 1)
                    nc.scalar.activation(kf[:, t, :, 0:M], kf[:, t, :, 0:M], ACT.Exp).then_inc(kf_exp, 1)

                def features_high(c):
                    for w, name in enumerate(("qfT", "kfT")):
                        wait_full(act, b, name, c)
                        src = bank(name, c)[:, :].rearrange("p (g n) -> p g n", g=NG)
                        if w == 0:
                            if c:
                                act.wait_ge(f_stored, b * 64 * NT + 64 * c)
                            else:
                                act.wait_ge(x3_stored, b * 32 + 32)
                        if w == 0 and c >= 2:
                            nc.scalar.activation(qf32[:, :, :], src, ACT.Copy)
                        nc.scalar.activation(fhl[:, w, 0, :, :], src, ACT.Copy).then_inc(fh_ready, 1)

                features_high(0)
                for c in range(NT):
                    for u in range(H // 2):
                        act.wait_ge(nmx_ready, b * NT * (H // 2) + c * (H // 2) + u + 1)
                        for i in range(2):
                            h = 2 * u + i
                            ins = nc.scalar.activation(
                                E[:, h, :, :], bank("s", c, u)[:, i * 2 * P:(i + 1) * 2 * P].rearrange("p (s n) -> p s n", s=2),
                                ACT.Exp, bias=nmx[:, h:h + 1], accum_out=sume[:, h:h + 1])
                        ins.then_inc(evac_of("s", c, u), 1)
                    act.wait_ge(t_ready, b * NT + c + 1)
                    nc.scalar.activation(e1[:, :], tt[:, :], ACT.Exp).then_inc(e1_ready, 1)
                    if c + 1 < NT:
                        features_high(c + 1)
                    for u in range(H // 2):
                        wait_full(act, b, "pT", c, u)
                        a = 1 if c == 0 else 2
                        src = bank("pT", c, u)[:, 0:2 * a * P].rearrange("p (h s n) -> p h s n", h=2, s=a)
                        nc.scalar.activation(PT[:, u % 2, :, 0:a, :], src, ACT.Copy).then_inc(evac_of("pT", c, u), 1)
                    wait_full(act, b, "pv", c)
                    nc.scalar.activation(OT[:, :, :], bank("pv", c)[:, :].rearrange("p (g n) -> p g n", g=NG), ACT.Copy)\
                      .then_inc(evac_of("pv", c), 1)
                    wait_full(act, b, "cT", c)
                    nc.scalar.activation(cT[:, :, :], bank("cT", c)[:, 0:D].rearrange("p (k n) -> p k n", k=KC), ACT.Copy)\
                      .then_inc(evac_of("cT", c), 1)
                for t in range(NT):
                    wait_full(act, b, "cxT", t)
                    nc.scalar.activation(cxT[:, :, t * P:(t + 1) * P],
                                         bank("cxT", t)[:, 0:D].rearrange("p (k n) -> p k n", k=KC), ACT.Copy)\
                      .then_inc(evac_of("cxT", t), 1)
                for t in range(NT):
                    copy_xT("x2T", t)
                wait_full(act, b, "gate")
                r = rows[32:36, R_ABS, :]
                link(nc.scalar.activation(r, bank("gate")[32:36, :], ACT.Abs, bias=fgb_sb[32:36, :]))
                link(nc.scalar.activation(r, r, ACT.Exp, scale=-1.0))
                nc.scalar.activation(r, r, ACT.Ln, bias=1.0).then_inc(lsig_ready, 1)
                act.wait_ge(negm_ready, b + 1)
                nc.scalar.activation(rows[0:4, R_ABS, :], rows[0:4, R_MIN, :], ACT.Exp).then_inc(expn_ready, 1)
                wait_evac(act, b, "rowT")
                for h in range(NH):
                    wait_full(act, b, "mB", h)
                    for tc in range(NT):
                        n = L - tc * P
                        if tc >= 2:
                            wait_evac(act, b, "qkm", h, tc - 2)
                        elif h:
                            wait_evac(act, b, "qkm", h - 1, tc + 2)
                        ins = nc.scalar.activation(Dm[:, tc % 2, 0:n], bank("mB", h)[:, tc * P:L], ACT.Exp,
                                                   bias=gT[:, tc, 0, h:h + 1])
                        ins.then_inc(d_ready if tc < NT - 1 else evac_of("mB", h), 1)
                act.wait_ge(f_stored, b * 64 * NT + 64 * NT)
                for t in range(NT):
                    wait_full(act, b, "x3T", t)
                    nc.scalar.activation(x3h[:, :, t * P:(t + 1) * P],
                                         bank("x3T", t)[:, 0:D].rearrange("p (k n) -> p k n", k=KC), ACT.Copy)\
                      .then_inc(x3h_ready, 1)
                wait_full(act, b, "z")
                nc.scalar.activation(zr[:, 0, :], bank("z")[0:NE, :], ACT.Exp, bias=nbg[:, :], scale=-1.0)\
                  .then_inc(evac_of("z"), 1)
            assert n_links[0] == LINKS["act"], ("act", n_links)

        @block.vector
        def _(dve):
            dve.wait_ge(consts_ready, 2)
            dve.wait_ge(consts_loaded, CONST_DMA)
            for hi, lo, src in ((pdh, pdl, pd), (wgh, wgl, wg_sb)):
                nc.vector.tensor_copy(hi[:, :, :], src[:, :, :]).then_inc(consts_ready, 1)
                dve.wait_ge(consts_ready, 3 if hi is pdh else 5)
                nc.vector.tensor_tensor(lo[:, :, :], src[:, :, :], hi[:, :, :].bitcast(F32), ALU.subtract)\
                  .then_inc(consts_ready, 1)
            nc.vector.tensor_copy(identr[:, :], ident[:, :]).then_inc(consts_ready, 1)
            nc.vector.tensor_copy(maskr[:, :, :, :], maskf[:, :, :, :]).then_inc(consts_ready, 1)
            dve.wait_ge(consts_ready, CONSTS_READY)

            with dve.Fori(0, NB) as b:
                link, n_links = linker(dve, dve_link, b, "dve")
                n_xhat = [0]

                def stats(src, n, first, done=None):
                    for i in range(n):
                        ins = nc.vector.bn_stats(st6[:, first + i, :], src(i))
                        if i == 0 and done is not None:
                            ins.then_inc(done, 1)
                    link(ins)
                    hold(dve, held["dve"])
                    for i in range(n):
                        ins = nc.vector.bn_aggr(mv[:, first + i, :], st6[:, first + i, :])
                    return ins

                def normalize(k, dst, src, n):
                    dve.wait_ge(ln_rstd, b * 4 + k + 1)
                    for i in range(n):
                        ins = nc.vector.tensor_scalar(dst(i), src(i), mv[:, i, 0:1], rstd[:, i:i + 1],
                                                      ALU.subtract, ALU.mult)
                        if k != 2:
                            ins.then_inc(xhat_ready, 1)
                    return ins

                dve.wait_ge(x_loaded, b * 16 + 16)
                stats(lambda t: x_in[:, t, :], NT, 0).then_inc(ln_stats, 1)
                normalize(0, lambda t: xh[:, t, :], lambda t: x_in[:, t, :], NT)

                def add_bias(t):
                    wait_full(dve, b, "qk", t)
                    if t >= 2:
                        dve.wait_ge(sq_ready, b * NT + t - 1)
                        wait_full(dve, b, "qkT", t - 2)
                    nc.vector.tensor_tensor(qk_tm[:, t % 2, :], bank("qk", t)[:, :], bqkv_bc[:, 0:2 * D], ALU.add)\
                      .then_inc(evac_of("qk", t), 1)
                    wait_full(dve, b, "v", t)
                    nc.vector.tensor_tensor(v_tm[:, t, :, 0:DH], bank("v", t)[:, 0:D].rearrange("p (h d) -> p h d", h=H),
                                            bqkv_bc[:, 2 * D:3 * D].rearrange("p (h d) -> p h d", h=H), ALU.add)\
                      .then_inc(evac_of("v", t), 1)

                def qk_low(t):
                    dve.wait_ge(qkh_ready, b * NT + t + 1)
                    nc.vector.scalar_tensor_tensor(
                        qkhl[:, t % 2, 1, :, :], bank("qkT", t)[:, :].rearrange("p (j n) -> p j n", j=4), SCALE ** 0.5,
                        qkhl[:, t % 2, 0, :, :].bitcast(F32), ALU.mult, ALU.subtract).then_inc(evac_of("qkT", t), 1)
                    dve.wait_ge(sq_ready, b * NT + t + 1)
                    nc.vector.tensor_reduce(sq[:, t, :], sqt[:, t % 2, :].rearrange("p (h d) -> p h d", d=DH),
                                            AX.X, ALU.add).then_inc(sq_read, 1)

                def logits(t):
                    xq = bank("xdq", t)[:, :].rearrange("p (h m) -> p h m", m=MP)[:, :, 0:M]
                    xk = bank("xdk", t)[:, :].rearrange("p (h m) -> p h m", m=MP)[:, :, 0:M]
                    wait_full(dve, b, "xdq", t)
                    link(nc.vector.tensor_reduce(mq[:, t, :], xq, AX.X, ALU.max))
                    nc.vector.tensor_tensor(qf[:, t, :, 0:M], xq, mq[:, t, :].unsqueeze(2).to_broadcast([P, H, M]),
                                            ALU.subtract).then_inc(evac_of("xdq", t), 1)
                    wait_full(dve, b, "xdk", t)
                    dve.wait_ge(sq_read, b * NT + t + 1)
                    nc.vector.scalar_tensor_tensor(kf[:, t, :, 0:M],
                                                   sq[:, t, H:2 * H].unsqueeze(2).to_broadcast([P, H, M]), -0.5 * SCALE,
                                                   xk, ALU.mult, ALU.add).then_inc(evac_of("xdk", t), 1)
                    nc.vector.scalar_tensor_tensor(gs[:, t, :], sq[:, t, 0:H], -0.5 * SCALE, mq[:, t, :],
                                                   ALU.mult, ALU.add)
                    wait_evac(dve, b, "xdk", t)
                    link(nc.vector.tensor_reduce(mk[:, t, :], kf[:, t, :, 0:M], AX.X, ALU.max))

                for s in range(NT + 2):
                    if s < NT:
                        add_bias(s)
                    if 1 <= s <= NT:
                        qk_low(s - 1)
                    if 2 <= s:
                        logits(s - 2)
                nc.vector.tensor_reduce(mk1[:, :], mk[:, :, :].rearrange("p t h -> p h t"), AX.X, ALU.max)\
                  .then_inc(mk_ready, 1)
                wait_full(dve, b, "mkT")
                nc.vector.tensor_reduce(kmx[:, :], bank("mkT")[0:H, 0:P], AX.X, ALU.max).then_inc(evac_of("mkT"), 1)
                wait_evac(dve, b, "mkT")
                nc.vector.tensor_scalar(kdg[:, :], ident[0:H, 0:H], kmx[:, 0:1], None, ALU.mult).then_inc(kmax_diag, 1)
                wait_full(dve, b, "mkB")
                nc.vector.tensor_copy(kb[:, :], bank("mkB")[:, 0:H]).then_inc(evac_of("mkB"), 1)
                wait_evac(dve, b, "mkB")
                for t in range(NT):
                    nc.vector.tensor_tensor(kf[:, t, :, 0:M], kf[:, t, :, 0:M],
                                            kb[:, :].unsqueeze(2).to_broadcast([P, H, M]), ALU.subtract)\
                      .then_inc(kf_sub, 1)
                link(nc.vector.tensor_tensor(gs[:, :, :], gs[:, :, :], kb[:, :].unsqueeze(1).to_broadcast([P, NT, H]),
                                             ALU.add))

                def features_low(c):
                    for w, name in enumerate(("qfT", "kfT")):
                        dve.wait_ge(fh_ready, b * 2 * NT + 2 * c + w + 1)
                        nc.vector.tensor_tensor(fhl[:, w, 1, :, :], bank(name, c)[:, :].rearrange("p (g n) -> p g n", g=NG),
                                                fhl[:, w, 0, :, :].bitcast(F32), ALU.subtract)\
                          .then_inc(evac_of(name, c), 1)

                features_low(0)
                for c in range(NT):
                    wait_full(dve, b, "u", c)
                    nc.vector.tensor_tensor(ut[:, :, :], bank("u", c)[:, :].rearrange("p (h m) -> p h m", m=MP)[:, :, 0:M],
                                            qf[:, c, :, 0:M], ALU.mult).then_inc(evac_of("u", c), 1)
                    wait_evac(dve, b, "u", c)
                    link(nc.vector.tensor_reduce(gsum[:, :], ut[:, :, :], AX.X, ALU.add))
                    if c >= 2:
                        wait_full(dve, b, "kv", c)
                        nc.vector.tensor_tensor(kvs[:, :, :], bank("kv", c)[:, 0:NG * HG * DH].rearrange("p (g n) -> p g n", g=NG),
                                                blk[:, :].unsqueeze(1).to_broadcast([P, NG, HG * DH]), ALU.mult)\
                          .then_inc(evac_of("kv", c), 1)
                    for u in range(H // 2):
                        wait_full(dve, b, "s", c, u)
                        nc.vector.tensor_reduce(nmx[:, 2 * u:2 * u + 2], bank("s", c, u)[:, :].rearrange("p (h n) -> p h n", h=2),
                                                AX.X, ALU.max, negate=True).then_inc(nmx_ready, 1)
                    dve.wait_ge(nmx_ready, b * NT * (H // 2) + (c + 1) * (H // 2))
                    nc.vector.scalar_tensor_tensor(tt[:, :], nmx[:, :], -1.0, gs[:, c, :], ALU.mult, ALU.subtract)\
                      .then_inc(t_ready, 1)
                    dve.wait_ge(e1_ready, b * NT + c + 1)
                    wait_evac(dve, b, "s", c, H // 2 - 1)
                    wait_evac(dve, b, "s", c, H // 2 - 2)
                    link(nc.vector.tensor_tensor(tt[:, :], e1[:, :], sume[:, :], ALU.mult))
                    link(nc.vector.scalar_tensor_tensor(tt[:, :], gsum[:, :], 1e-24, tt[:, :], ALU.max, ALU.add))
                    link(nc.vector.reciprocal(gps[:, :], tt[:, :]))
                    nc.vector.reciprocal(rs[:, :], sume[:, :])
                    link(nc.vector.tensor_tensor(aa[:, :], gps[:, :], sume[:, :], ALU.mult))
                    if c + 1 < NT:
                        features_low(c + 1)
                    for u in range(H // 2):
                        wait_full(dve, b, "sg", c, u)
                        if u >= 2:
                            dve.wait_ge(p_ready, b * NT * (H // 2) + c * (H // 2) + u - 1)
                        for i in range(2):
                            h = 2 * u + i
                            ins = nc.vector.scalar_tensor_tensor(
                                GW[:, u % 2, i, :, :], bank("sg", c, u)[:, i * 2 * P:(i + 1) * 2 * P].rearrange("p (s n) -> p s n", s=2),
                                aa[:, h:h + 1], win[:, variant(c), :, :], ALU.mult, ALU.mult)
                        ins.then_inc(evac_of("sg", c, u), 1)
                    if c >= 2:
                        wait_full(dve, b, "st", c)
                        nc.vector.tensor_tensor(stt[:, :, :], bank("st", c)[:, 0:D].rearrange("p (h d) -> p h d", h=H),
                                                gps[:, :].unsqueeze(2).to_broadcast([P, H, DH]), ALU.mult)\
                          .then_inc(evac_of("st", c), 1)
                    wait_full(dve, b, "oT", c)
                    nc.vector.tensor_tensor(cc[:, :, :], bank("oT", c)[:, :].rearrange("p (h d) -> p h d", d=MP)[:, :, 0:DH],
                                            rs[:, :].unsqueeze(2).to_broadcast([P, H, DH]), ALU.mult)\
                      .then_inc(evac_of("oT", c), 1)
                    wait_evac(dve, b, "oT", c)
                    if c >= 2:
                        wait_evac(dve, b, "st", c)
                        nc.vector.tensor_tensor(cc[:, :, :], cc[:, :, :], stt[:, :, :], ALU.add).then_inc(c_ready, 1)
                    if c == 0:
                        dve.wait_ge(x2_stored, b * 16 + 16)
                        dve.wait_ge(xb_ready, b + 1)
                    wait_full(dve, b, "proj", c)
                    nc.vector.tensor_tensor(x1[:, c, :], bank("proj", c)[:, 0:D], x_in[:, c, :], ALU.add)\
                      .then_inc(evac_of("proj", c), 1)

                wait_evac(dve, b, "proj", NT - 1)
                stats(lambda t: x1[:, t, :], NT, 0, x_free).then_inc(ln_stats, 1)
                normalize(1, lambda t: xh[:, t, :], lambda t: x1[:, t, :], NT)
                wait_full(dve, b, "gate")
                dve.wait_ge(lsig_ready, b + 1)
                link(nc.vector.tensor_scalar(rows[32:36, R_MIN, :], bank("gate")[32:36, :], fgb_sb[32:36, :], 0.0,
                                             ALU.add, ALU.min))
                link(nc.vector.tensor_tensor(rows[32:36, R_MIN, :], rows[32:36, R_MIN, :], rows[32:36, R_ABS, :], ALU.subtract))
                link(nc.vector.tensor_tensor_scan(rows[0:4, R_F, :], ones_row[32:36, :], rows[32:36, R_MIN, :], 0.0,
                                                  ALU.mult, ALU.add))
                nc.vector.scalar_tensor_tensor(rows[0:4, R_G, :], bank("gate")[0:4, :], igb_sb[:, :], rows[0:4, R_F, :],
                                               ALU.add, ALU.subtract).then_inc(evac_of("gate"), 1)
                wait_evac(dve, b, "gate")
                link(nc.vector.tensor_tensor_scan(rows[0:4, R_M, :], rows[0:4, R_G, :], rows[0:4, R_G, :], -3.0e38,
                                                  ALU.max, ALU.max))
                nc.vector.scalar_tensor_tensor(rows[0:4, R_MIN, :], rows[0:4, R_F, :], -1.0, rows[0:4, R_M, :],
                                               ALU.mult, ALU.subtract).then_inc(negm_ready, 1)
                nc.vector.tensor_scalar(rows[0:4, R_NM, :], rows[0:4, R_M, :], -1.0, None, ALU.mult).then_inc(nm_ready, 1)
                wait_full(dve, b, "rowT")
                nc.vector.tensor_copy(gT[:, :, :, :], bank("rowT")[:, 0:NT * 2 * NH].rearrange("p (t w h) -> p t w h", t=NT, w=2))\
                  .then_inc(evac_of("rowT"), 1)
                for h in range(NH):
                    for tc in range(NT):
                        n = L - tc * P
                        wait_full(dve, b, "qkm", h, tc)
                        dve.wait_ge(dmask_ready, b * NH * NT + h * NT + tc + 1)
                        nc.vector.scalar_tensor_tensor(ct(h, tc, 0, n), bank("qkm", h, tc)[:, 0:n], XD ** -0.5,
                                                       Dm[:, tc % 2, 0:n], ALU.mult, ALU.mult)\
                          .then_inc(evac_of("qkm", h, tc), 1)
                wait_evac(dve, b, "rowT")
                for sc in range(NT):
                    wait_full(dve, b, "h", sc)
                    hv = bank("h", sc)[:, 0:NH * (XD + 1)].rearrange("p (h d) -> p h d", h=NH)
                    nr = nrm[:, sc % 2, :]
                    link(nc.vector.tensor_reduce(nr, hv[:, :, XD:XD + 1], AX.X, ALU.max, apply_absolute_value=True))
                    link(nc.vector.tensor_tensor(nr, nr, gT[:, sc, 1, :], ALU.max))
                    link(nc.vector.tensor_scalar(nr, nr, X_EPS, None, ALU.add))
                    link(nc.vector.reciprocal(nr, nr))
                    nc.vector.tensor_tensor(xh[:, sc, :].rearrange("p (h d) -> p h d", h=NH), hv[:, :, 0:XD],
                                            nr.unsqueeze(2).to_broadcast([P, NH, XD]), ALU.mult)\
                      .then_inc(evac_of("h", sc), 1)
                    wait_evac(dve, b, "h", sc)
                    ins = stats(lambda h: xh[:, sc, h * XD:(h + 1) * XD], NH, sc * NH)
                ins.then_inc(ln_stats, 1)
                link(normalize(2, lambda i: xh[:, i // NH, (i % NH) * XD:(i % NH + 1) * XD],
                               lambda i: xh[:, i // NH, (i % NH) * XD:(i % NH + 1) * XD], NT * NH))
                link(nc.vector.tensor_tensor(xh[:, :, :], xh[:, :, :], onw_bc[:, :].unsqueeze(1).to_broadcast([P, NT, D]),
                                             ALU.mult))
                nc.vector.tensor_tensor(x1[:, :, :], x1[:, :, :], xh[:, :, :], ALU.add).then_inc(ctx_free, 1)
                dve.wait_ge(ctx_free, b + 2)
                stats(lambda t: x1[:, t, :], NT, 0).then_inc(ln_stats, 1)
                normalize(3, lambda t: xh[:, t, :], lambda t: x1[:, t, :], NT)
                for t in range(NT):
                    dve.wait_ge(x3h_ready, b * NT + t + 1)
                    nc.vector.tensor_tensor(x3l[:, :, t * P:(t + 1) * P],
                                            bank("x3T", t)[:, 0:D].rearrange("p (k n) -> p k n", k=KC),
                                            x3h[:, :, t * P:(t + 1) * P].bitcast(F32), ALU.subtract)\
                      .then_inc(evac_of("x3T", t), 1)
                wait_evac(dve, b, "z")
                link(nc.vector.tensor_scalar(zr[:, 1, :], zr[:, 0, :], 1.0, None, ALU.add))
                link(nc.vector.reciprocal(zr[:, 1, :], zr[:, 1, :]))
                nc.vector.scalar_tensor_tensor(zr[:, 2, :], zr[:, 1, :], 0.5, zr[:, 1, :], ALU.is_gt, ALU.mult)\
                  .then_inc(w_ready, 1)
                wait_full(dve, b, "wT")
                nc.vector.tensor_copy(wtok[:, bass.ds(b * NT, NT), :],
                                      bank("wT")[:, 0:NT * NE].rearrange("p (t e) -> p t e", t=NT))\
                  .then_inc(evac_of("wT"), 1)
                for t in range(NT):
                    wait_full(dve, b, "b2", t)
                    nc.vector.tensor_tensor(x1[:, t, :], x1[:, t, :], bank("b2", t)[:, 0:D], ALU.add)\
                      .then_inc(evac_of("b2", t), 1)
            assert n_links[0] == LINKS["dve"], ("dve", n_links)

        @block.tensor
        def _(pe):
            pe.wait_ge(consts_ready, CONSTS_READY)
            with pe.Fori(0, NB) as b:
                emitted = []

                def begin(*name):
                    emitted.append((name, BANK_OF[name]))
                    wait_bank(pe, b, *name)
                    return bank(*name)

                def end(ins, *name):
                    ins.then_inc(full_of(*name), 1)

                def turn(name, t, src, base):
                    dst = begin(name, t)
                    for k in range(KC):
                        ins = nc.tensor.transpose(dst[:, k * P:(k + 1) * P], src(k), ident[:, :])
                    end(ins, name, t)

                for t in range(NT):
                    pe.wait_ge(xhat_ready, b * 3 * NT + t + 1)
                    turn("x1T", t, lambda k: xh[:, t, k * P:(k + 1) * P], 0)

                def project(t):
                    wait_evac(pe, b, "x1T", t)
                    dst = begin("qk", t)
                    for k in range(KC):
                        ins = nc.tensor.matmul(dst[:, :], xT[:, k, t * P:(t + 1) * P], wqkv_sb[:, k, 0:2 * D],
                                               start=k == 0, stop=k == KC - 1)
                    end(ins, "qk", t)
                    dst = begin("v", t)
                    for k in range(KC):
                        ins = nc.tensor.matmul(dst[:, 0:D], xT[:, k, t * P:(t + 1) * P], wqkv_sb[:, k, 2 * D:3 * D],
                                               start=k == 0, stop=k == KC - 1)
                    end(ins, "v", t)

                def turn_qk(t):
                    wait_evac(pe, b, "qk", t)
                    dst = begin("qkT", t)
                    for j in range(4):
                        ins = nc.tensor.transpose(dst[:, j * P:(j + 1) * P], qk_tm[:, t % 2, j * P:(j + 1) * P], ident[:, :])
                    end(ins, "qkT", t)

                def random_features(t):
                    wait_evac(pe, b, "qkT", t)
                    for name, j0 in (("xdq", 0), ("xdk", 2)):
                        dst = begin(name, t)
                        for j in range(2):
                            parts = ((0, pdh), (0, pdl), (1, pdh))
                            for i, (s, w) in enumerate(parts):
                                ins = nc.tensor.matmul(dst[:, j * 256:(j + 1) * 256], qkhl[:, t % 2, s, j0 + j, :],
                                                       w[:, :, :].rearrange("p h m -> p (h m)"),
                                                       start=i == 0, stop=i == len(parts) - 1)
                        end(ins, name, t)

                for s in range(NT + 2):
                    if s < NT:
                        project(s)
                    if 1 <= s <= NT:
                        turn_qk(s - 1)
                    if 2 <= s:
                        random_features(s - 2)
                pe.wait_ge(mk_ready, b + 1)
                dst = begin("mkT")
                end(nc.tensor.transpose(dst[0:H, 0:P], mk1[:, :], ident[:, :]), "mkT")
                pe.wait_ge(kmax_diag, b + 1)
                dst = begin("mkB")
                end(nc.tensor.matmul(dst[:, 0:H], ones[0:H, :], kdg[:, :], start=True, stop=True), "mkB")

                def turn_features(c):
                    for name, f, ready in (("qfT", qf, qf_ready), ("kfT", kf, kf_ready)):
                        pe.wait_ge(ready, b * NT + c + 1)
                        dst = begin(name, c)
                        for g in range(NG):
                            ins = nc.tensor.transpose(dst[:, g * P:(g + 1) * P],
                                                      f[:, c, g * HG:(g + 1) * HG, :].rearrange("p h m -> p (h m)"), ident[:, :])
                        end(ins, name, c)

                turn_features(0)
                for c in range(NT):
                    v = variant(c)
                    dst = begin("u", c)
                    for j in range(c + 1):
                        w = wdT if j == c else wpT if j == c - 1 else ones
                        ins = nc.tensor.matmul(dst[:, :], w[:, :], kf[:, j, :, :].rearrange("p h m -> p (h m)"),
                                               start=j == 0, stop=j == c)
                    end(ins, "u", c)
                    if c >= 2:
                        dst = begin("kv", c)
                        for g in range(NG):
                            for j in range(c - 1):
                                ins = nc.tensor.matmul(dst[:, g * 64:(g + 1) * 64],
                                                       kf[:, j, g * HG:(g + 1) * HG, :].rearrange("p h m -> p (h m)"),
                                                       v_tm[:, j, g * HG:(g + 1) * HG, 0:DH], start=j == 0, stop=j == c - 2)
                        end(ins, "kv", c)
                        wait_evac(pe, b, "kv", c)
                        pe.wait_ge(fh_ready, b * 2 * NT + 2 * c + 1)
                        dst = begin("st", c)
                        for g in range(NG):
                            ins = nc.tensor.matmul(dst[:, g * 64:(g + 1) * 64], qf32[:, g, :], kvs[:, g, :],
                                                   start=True, stop=True)
                        end(ins, "st", c)
                    pe.wait_ge(qs_loaded, b * 128 * NT + 128 * (c + 1))
                    for u in range(H // 2):
                        dst = begin("s", c, u)
                        nc.tensor.matmul(dst[:, :], identr[:, :],
                                         maskr[:, v, :, :].unsqueeze(1).to_broadcast([P, 2, 2, P]),
                                         start=True, stop=False, skip_group_check=True)
                        for i in range(2):
                            h = 2 * u + i
                            ins = nc.tensor.matmul(dst[:, i * 256:(i + 1) * 256], qs[:, h, :],
                                                   ks[:, h, :, :].rearrange("p s n -> p (s n)"),
                                                   start=False, stop=i == 1, skip_group_check=True)
                        end(ins, "s", c, u)
                    if c + 1 < NT:
                        turn_features(c + 1)
                    pe.wait_ge(fs_loaded, b * 96 * NT + 96 * (c + 1))
                    dst_pv = None
                    for s in range(H // 2 + 2):
                        if s < H // 2:
                            dst = begin("sg", c, s)
                            for i in range(2):
                                h = 2 * s + i
                                ins = nc.tensor.matmul(dst[:, i * 256:(i + 1) * 256], qfs[:, h, :],
                                                       kfs[:, h, :, :].rearrange("p s n -> p (s n)"), start=True, stop=True)
                            end(ins, "sg", c, s)
                        slots = (0,) if c == 0 else (0, 1)
                        if 1 <= s <= H // 2:
                            u = s - 1
                            pe.wait_ge(p_ready, b * NT * (H // 2) + c * (H // 2) + u + 1)
                            dst = begin("pT", c, u)
                            for i in range(2):
                                for k in slots:
                                    at_ = (i * len(slots) + k) * P
                                    ins = nc.tensor.transpose(dst[:, at_:at_ + P], E[:, 2 * u + i, k, :], ident[:, :])
                            end(ins, "pT", c, u)
                        if s >= 2:
                            u = s - 2
                            wait_evac(pe, b, "pT", c, u)
                            if u == 0:
                                dst_pv = begin("pv", c)
                            for i in range(2):
                                h = 2 * u + i
                                q = h % HG
                                for k in slots:
                                    chunk = c if k == c % 2 else c - 1
                                    ins = nc.tensor.matmul(dst_pv[MP * q:MP * q + MP, (h // HG) * P:(h // HG + 1) * P],
                                                           v_tm[:, chunk, h, :], PT[:, u % 2, i, k, :],
                                                           start=k == 0, stop=k == slots[-1])
                    end(ins, "pv", c)
                    wait_evac(pe, b, "pv", c)
                    dst = begin("oT", c)
                    for g in range(NG):
                        ins = nc.tensor.transpose(dst[:, g * P:(g + 1) * P], OT[:, g, :], ident[:, :])
                    end(ins, "oT", c)
                    if c >= 2:
                        pe.wait_ge(c_ready, b * 2 + c - 1)
                    else:
                        wait_evac(pe, b, "oT", c)
                    dst = begin("cT", c)
                    cr = cc[:, :, :].rearrange("p h d -> p (h d)")
                    for k in range(KC):
                        ins = nc.tensor.transpose(dst[:, k * P:(k + 1) * P], cr[:, k * P:(k + 1) * P], ident[:, :])
                    end(ins, "cT", c)
                    wait_evac(pe, b, "cT", c)
                    dst = begin("proj", c)
                    for k in range(KC):
                        ins = nc.tensor.matmul(dst[:, 0:D], cT[:, k, :], wo_sb[:, k, :], start=k == 0, stop=k == KC - 1)
                    end(ins, "proj", c)

                pe.wait_ge(ctx_loaded, b * 16 * (NT + 1) + 16 * (NT + 1))
                for t in range(NT):
                    turn("cxT", t, lambda k: ctx_t[:, t, k * P:(k + 1) * P], 0)
                for t in range(NT):
                    pe.wait_ge(xhat_ready, b * 3 * NT + NT + t + 1)
                    turn("x2T", t, lambda k: xh[:, t, k * P:(k + 1) * P], 0)
                for t in range(NT):
                    wait_evac(pe, b, "cxT", t)
                    wait_evac(pe, b, "x2T", t)
                dst = begin("gate")
                for k in range(2 * KC):
                    src = xT[:, k, :] if k < KC else cxT[:, k - KC, :]
                    ins = nc.tensor.matmul(dst[0:36, :], gk[:, k, :], src, start=k == 0, stop=k == 2 * KC - 1)
                end(ins, "gate")
                pe.wait_ge(expn_ready, b + 1)
                dst = begin("rowT")
                hold(pe, held["pe"])
                for t in range(NT):
                    for w, r in enumerate((R_G, R_ABS)):
                        o = (t * 2 + w) * NH
                        ins = nc.tensor.transpose(dst[:, o:o + NH], rows[0:4, r, t * P:(t + 1) * P], ident[0:4, 0:4])
                end(ins, "rowT")
                pe.wait_ge(nm_ready, b + 1)
                for h in range(NH):
                    dst = begin("mB", h)
                    end(nc.tensor.matmul(dst[:, :], sel[:, h, :], rows[0:4, R_NM, :], start=True, stop=True), "mB", h)
                    r = (h % 2) * XD
                    for tc in range(NT):
                        dst = begin("qkm", h, tc)
                        end(nc.tensor.matmul(dst[:, 0:L - tc * P], cxT[r:r + XD, h // 2, tc * P:(tc + 1) * P],
                                             xT[r:r + XD, h // 2, tc * P:L], start=True, stop=True), "qkm", h, tc)
                wait_evac(pe, b, "qkm", NH - 1, NT - 1)
                for sc in range(NT):
                    dst = begin("h", sc)
                    for h in range(NH):
                        for tc in range(sc + 1):
                            ins = nc.tensor.matmul(dst[:, h * (XD + 1):(h + 1) * (XD + 1)],
                                                   ct(h, tc, (sc - tc) * P, (sc - tc + 1) * P), ctx_in[:, tc, h, :],
                                                   start=tc == 0, stop=tc == sc)
                    end(ins, "h", sc)
                for t in range(NT):
                    pe.wait_ge(xhat_ready, b * 3 * NT + 2 * NT + t + 1)
                    turn("x3T", t, lambda k: xh[:, t, k * P:(k + 1) * P], 0)
                wait_evac(pe, b, "x3T", NT - 1)
                wait_evac(pe, b, "x3T", NT - 2)
                dst = begin("z")
                zp = [(k, a, w) for k in range(KC) for a, w in ((x3h, wgh), (x3l, wgh), (x3h, wgl))]
                for i, (k, a, w) in enumerate(zp):
                    ins = nc.tensor.matmul(dst[0:NE, :], w[:, k, :], a[:, k, :], start=i == 0, stop=i == len(zp) - 1)
                end(ins, "z")
                pe.wait_ge(w_ready, b + 1)
                dst = begin("wT")
                hold(pe, held["pe"])
                for t in range(NT):
                    ins = nc.tensor.transpose(dst[:, t * NE:(t + 1) * NE], zr[:, 2, t * P:(t + 1) * P], ident[0:NE, 0:NE])
                end(ins, "wT")
                for t in range(NT):
                    dst = begin("b2", t)
                    end(nc.tensor.matmul(dst[:, 0:D], zr[:, 2, t * P:(t + 1) * P], b2_sb[:, :], start=True, stop=True), "b2", t)
                assert emitted == GROUPS


def ffn_phase(nc, sem, banks, wtok, w1, b1, w2, x2_dram, x3_dram, out):
    w_loaded = [sem("w_loaded%d" % i) for i in range(2)]
    b1_loaded = [sem("b1_loaded%d" % i) for i in range(2)]
    held_sp, held_pool = sem("held_sp2"), sem("held_pool2")
    w_high, w_split = sem("w_high"), sem("w_split")
    group_loaded = sem("group_loaded")
    up_full, hid_ready, hid_split = sem("up_full"), sem("hid_ready"), sem("hid_split")
    down_full, gate_copied, acc_done, out_stored = sem("down_full"), sem("gate_copied"), sem("acc_done"), sem("out_stored")
    PIECES = 4
    PCOLS = KC * HID // 2
    RING = 4
    CREDIT = 2 * NGRP
    with ExitStack() as stack:
        def sb(name, shape, dt=F32):
            return stack.enter_context(nc.sbuf_tensor(name, shape, dt))

        x3 = sb("x3", [P, NGRP, 2, KC, L], F32R)
        acc = sb("acc", [P, NB * NT, D])
        wraw = sb("wraw", [P, 2, PCOLS])
        w1p = sb("w1p", [P, 2, 2, KC, HID], F32R)
        w2p = sb("w2p", [P, 2, 2, NK, D], F32R)
        b1p = sb("b1p", [P, 2, NK])
        hid = sb("hid", [P, RING, L])
        hidr = sb("hidr", [P, RING, 2, L], F32R)
        gate = sb("gate", [P, 2, NT])
        up = [banks[k] for k in ("A0", "A1", "B0", "B1")]
        down = [banks[k] for k in ("C0", "C1", "D", "E")]

        def piece(parity, part, j):
            if j < KC:
                return w1p[:, parity, part, j, :]
            j -= KC
            return w2p[:, parity, part, j * NK // 2:(j + 1) * NK // 2, :].rearrange("p k n -> p (k n)")

        def over_groups(eng, body):
            with eng.Fori(0, NGRP // 2 - 1) as j:
                body(2 * j, 0, False)
                body(2 * j + 1, 1, False)
            body(NGRP - 2, 0, False)
            body(NGRP - 1, 1, True)

        block = stack.enter_context(nc.Block())

        @block.sync
        def _(sp):
            def load_piece(e, parity, j):
                sp.wait_ge(w_split, PIECES * e + j + 1)
                hold(sp, held_sp)
                dst = wraw[:, j % 2, :]
                if j < KC:
                    src = w1[bass.ds(e, 1), j * P:(j + 1) * P, :].rearrange("o p n -> p (o n)")
                else:
                    src = w2[bass.ds(e, 1), (j - KC) * HID // 2:(j - KC + 1) * HID // 2, :]\
                        .rearrange("o (k p) n -> p (o k) n", p=P)
                    dst = dst.rearrange("p (k n) -> p k n", n=D)
                sp.dma_start(dst, src).then_inc(w_loaded[j % 2], 16)

            def load_expert(e, parity):
                load_piece(e, parity, 0)
                load_piece(e, parity, 1)
                sp.wait_ge(acc_done, NGRP * e + NGRP)
                hold(sp, held_sp)
                sp.dma_start(b1p[:, parity, :], b1[bass.ds(e, 1), :, :].rearrange("o p k -> p (o k)")).then_inc(b1_loaded[parity], 16)
                load_piece(e, parity, 2)
                load_piece(e, parity, 3)

            def load_group(g):
                for s in range(2):
                    sp.dma_start(x3[:, g, s, :, :].bitcast(F32), x3_dram[g, s, :, :, :]).then_inc(group_loaded, 16)
                sp.dma_start(acc[:, g * NT:(g + 1) * NT, :], x2_dram[g, :, :, :]).then_inc(group_loaded, 16)

            load_group(0)
            load_expert(0, 0)
            for g in range(1, NGRP):
                sp.wait_ge(group_loaded, 48 * g)
                load_group(g)
            load_expert(1, 1)
            with sp.Fori(1, NE // 2) as i:
                load_expert(2 * i, 0)
                load_expert(2 * i + 1, 1)
            with sp.Fori(0, NGRP) as g:
                sp.wait_ge(acc_done, g + (CREDIT + (NE - 1) * NGRP + 1))
                hold(sp, held_sp)
                sp.dma_start(out[bass.ds(g, 1), :, :].rearrange("o (t p) d -> p (o t) d", p=P),
                             acc[:, bass.ds(g * NT, NT), :]).then_inc(out_stored, 16)
            sp.wait_ge(out_stored, 16 * NGRP)

        @block.gpsimd
        def _(pool):
            pool.sem_inc(w_split, 2)
            pool.sem_inc(acc_done, CREDIT)
            with pool.Fori(0, NE // 2) as i:
                for parity in range(2):
                    e = 2 * i + parity
                    pool.wait_ge(acc_done, NGRP * e + NGRP)
                    for j in range(PIECES):
                        pool.wait_ge(w_loaded[j % 2], 16 * (PIECES // 2) * e + 16 * (j // 2 + 1))
                        hold(pool, held_pool)
                        high, low = piece(parity, 0, j), piece(parity, 1, j)
                        nc.gpsimd.tensor_copy(high, wraw[:, j % 2, :]).then_inc(w_high, 1)
                        pool.wait_ge(w_high, PIECES * e + j + 1)
                        nc.gpsimd.tensor_tensor(low, wraw[:, j % 2, :], high.bitcast(F32), ALU.subtract)\
                          .then_inc(w_split, 1)

        @block.scalar
        def _(act):
            with act.Fori(0, NE // 2) as i:
                for parity in range(2):
                    e = 2 * i + parity
                    act.wait_ge(b1_loaded[parity], 16 * i + 16)

                    def group(g, gp, last):
                        for k in range(NK):
                            n = (e * NGRP + g) * NK + k
                            act.wait_ge(up_full, n + 1)
                            b = b1p[:, parity, k:k + 1]
                            nc.scalar.activation(hidr[:, k % RING, 0, :], up[k % RING][:, :], ACT.Relu, bias=b)
                            nc.scalar.activation(hid[:, k % RING, :], up[k % RING][:, :], ACT.Relu, bias=b)\
                              .then_inc(hid_ready, 1)

                    over_groups(act, group)

        @block.vector
        def _(dve):
            with dve.Fori(0, NE // 2) as i:
                for parity in range(2):
                    e = 2 * i + parity

                    def group(g, gp, last):
                        nc.vector.tensor_copy(gate[:, gp, :], wtok[:, bass.ds(g * NT, NT), bass.ds(e, 1)]
                                              .rearrange("p t o -> p (t o)")).then_inc(gate_copied, 1)
                        for k in range(NK):
                            n = (e * NGRP + g) * NK + k
                            dve.wait_ge(hid_ready, n + 1)
                            nc.vector.tensor_tensor(hidr[:, k % RING, 1, :], hid[:, k % RING, :],
                                                    hidr[:, k % RING, 0, :].bitcast(F32), ALU.subtract)\
                              .then_inc(hid_split, 1)
                        dve.wait_ge(gate_copied, e * NGRP + g + 1)
                        dve.wait_ge(group_loaded, 48 * g + 48)
                        dve.wait_ge(down_full, e * NGRP + g + 1)
                        for t in range(NT):
                            a = acc[:, bass.ds(g * NT + t, 1), :].rearrange("p o d -> p (o d)")
                            ins = nc.vector.scalar_tensor_tensor(a, down[2 * gp + t // 2][:, (t % 2) * D:(t % 2 + 1) * D],
                                                                 gate[:, gp, t:t + 1], a, ALU.mult, ALU.add)
                        ins.then_inc(acc_done, 1)

                    over_groups(dve, group)

        @block.tensor
        def _(pe):
            def x3_part(g, s, k):
                return x3[:, bass.ds(g, 1), s, k, :].rearrange("p o n -> p (o n)")

            with pe.Fori(0, NE // 2) as i:
                for parity in range(2):
                    e = 2 * i + parity

                    def up_step(g, k):
                        dst = up[k % RING]
                        prods = [(s, w, c) for c in range(KC) for s, w in ((0, 0), (0, 1), (1, 0))]
                        for m, (s, w, c) in enumerate(prods):
                            ins = nc.tensor.matmul(dst[:, :], w1p[:, parity, w, c, k * P:(k + 1) * P], x3_part(g, s, c),
                                                   start=m == 0, stop=m == len(prods) - 1)
                        ins.then_inc(up_full, 1)

                    pe.wait_ge(w_split, PIECES * e + KC + 2)
                    if parity == 0:
                        pe.wait_ge(group_loaded, 48)
                    up_step(0, 0)

                    def group(g, gp, last):
                        G = e * NGRP + g
                        for k in range(NK):
                            if k + 1 < NK:
                                up_step(g, k + 1)
                            elif not last:
                                pe.wait_ge(group_loaded, 48 * (g + 1) + 48)
                                up_step(g + 1, 0)
                            pe.wait_ge(hid_split, G * NK + k + 1)
                            if k == 0:
                                pe.wait_ge(w_split, PIECES * e + PIECES + 2)
                                pe.wait_ge(acc_done, G + CREDIT - 1)
                            for t in range(NT):
                                dst = down[2 * gp + t // 2][:, (t % 2) * D:(t % 2 + 1) * D]
                                for m, (s, w) in enumerate(((0, 0), (0, 1), (1, 0))):
                                    ins = nc.tensor.matmul(dst, hidr[:, k % RING, s, t * P:(t + 1) * P], w2p[:, parity, w, k, :],
                                                           start=k == 0 and m == 0 and t % 2 == 0, stop=k == NK - 1 and m == 2,
                                                           skip_group_check=True)
                        ins.then_inc(down_full, 1)

                    over_groups(pe, group)


_OUT = (NB, L, D)


def kernel(x, ctx_1024, L0_attn_Wqkv_w, L0_attn_Wqkv_b, L0_attn_proj, L0_attn_out_w, L0_attn_out_b,
           L0_xattn_ig_kernel, L0_xattn_ig_bias, L0_xattn_fg_kernel, L0_xattn_fg_bias, L0_xattn_outnorm_weight,
           L0_ffn_Wg, L0_ffn_bg, L0_ffn_W1, L0_ffn_b1, L0_ffn_W2, L0_ffn_b2):
    import numpy as np
    import concourse.bacc as bacc
    from concourse.bass_utils import run_bass_kernel_spmd

    layout = {
        "x": x, "ctx": ctx_1024, "wqkv": np.asarray(L0_attn_Wqkv_w).T, "bqkv": L0_attn_Wqkv_b,
        "proj": np.asarray(L0_attn_proj).T, "wo": np.asarray(L0_attn_out_w).T, "bo": L0_attn_out_b,
        "igk": L0_xattn_ig_kernel, "igb": np.asarray(L0_xattn_ig_bias).reshape(NH, 1),
        "fgk": L0_xattn_fg_kernel, "fgb": np.asarray(L0_xattn_fg_bias).reshape(NH, 1),
        "onw": np.asarray(L0_xattn_outnorm_weight).reshape(D),
        "wg": L0_ffn_Wg, "bg": np.asarray(L0_ffn_bg).reshape(NE, 1), "w1": L0_ffn_W1,
        "b1": np.asarray(L0_ffn_b1).reshape(NE, NK, P).transpose(0, 2, 1), "w2": L0_ffn_W2, "b2": L0_ffn_b2,
    }
    nc = bacc.Bacc("TRN2", target_bir_lowering=False, num_devices=1)
    arrays, aps = {}, {}
    for name, a in layout.items():
        a = np.ascontiguousarray(a)
        arrays["in_" + name] = a
        aps[name] = nc.dram_tensor("in_" + name, a.shape, mybir.dt.from_np(a.dtype), kind="ExternalInput").ap()
    out = nc.dram_tensor("out_dram", _OUT, F32, kind="ExternalOutput").ap()
    decoder_kernel(nc, out=out, **aps)
    r = run_bass_kernel_spmd(nc, [arrays], core_ids=[0])
    return r.results[0]["out_dram"]
```

```python
import concourse.bass as bass
from concourse import mybir
from contextlib import ExitStack

F32 = mybir.dt.float32
F32R = mybir.dt.float32r
ALU = mybir.AluOpType
ACT = mybir.ActivationFunctionType
AX = mybir.AxisListType

P = 128
NB = 8
L = 512
D = 256
NT = L // P
KC = D // P
H = 16
DH = D // H
M = 24
MP = 32
HG = 4
NG = H // HG
QROWS = 80
FROWS = 3 * M
NH = 4
XD = D // NH
NE = 8
HID = 1024
NK = HID // P
NTOK = NB * L
NGRP = NTOK // L
SCALE = DH ** -0.5
FEAT_EPS = 1e-4
MASK_VAL = -10000.0
LN_EPS = 1e-5
X_EPS = 1e-6


def pe_groups():
    g = [(("x1T", t), "C%d" % (t % 2)) for t in range(NT)]
    for s in range(NT + 2):
        if s < NT:
            g += [(("qk", s), "A%d" % (s % 2)), (("v", s), "B%d" % (s % 2))]
        if 1 <= s <= NT:
            g.append((("qkT", s - 1), "C%d" % ((s - 1) % 2)))
        if 2 <= s:
            g += [(("xdq", s - 2), "D"), (("xdk", s - 2), "E")]
    g += [(("mkT",), "A0"), (("mkB",), "A1")]
    g += [(("qfT", 0), "E"), (("kfT", 0), "C1"), (("u", 0), "E")]
    g += [(("s", 0, u), "A%d" % (u % 2)) for u in range(H // 2)]
    for c in range(NT):
        for s in range(H // 2 + 3):
            if s < H // 2:
                if c + 1 < NT:
                    g.append((("s", c + 1, s), "A%d" % (s % 2)))
                g.append((("sg", c, s), "B%d" % (s % 2)))
            if 2 <= s < H // 2 + 2:
                g.append((("pT", c, s - 2), "C%d" % (s % 2)))
            if s == 3:
                g.append((("pv", c), "D"))
            if s == 0 and c:
                g.append((("oT", c - 1), "D"))
            if s == 0 and c >= 2:
                g.append((("kv", c), "E"))
            if s == 1 and c >= 2:
                g.append((("st", c), "E"))
            if s == 2 and c + 1 < NT:
                g.append((("qfT", c + 1), "E"))
            if s == 3 and c + 1 < NT:
                g.append((("kfT", c + 1), "E"))
            if s == 4 and c:
                g.append((("cT", c - 1), "E"))
            if s == 5 and c:
                g.append((("proj", c - 1), "E"))
            if s == 6 and c + 1 < NT:
                g.append((("u", c + 1), "E"))
    g += [(("oT", NT - 1), "D"), (("cT", NT - 1), "E"), (("proj", NT - 1), "D")]
    g += [(("cxT", t), "B%d" % (t % 2)) for t in range(NT)]
    g += [(("x2T", t), "C%d" % (t % 2)) for t in range(NT)]
    g += [(("gate",), "D"), (("rowT",), "E")]
    for h in range(NH):
        g.append((("mB", h), "A%d" % (h % 2)))
        g += [(("qkm", h, tc), ("B0", "B1", "C0", "C1")[tc]) for tc in range(NT)]
    g += [(("h", sc), "DE"[sc % 2]) for sc in range(NT)]
    g += [(("x3T", t), "C%d" % (t % 2)) for t in range(NT)]
    g += [(("z",), "A0"), (("wT",), "A1")]
    g += [(("b2", t), "B%d" % (t % 2)) for t in range(NT)]
    return g


BANKS = ("A0", "A1", "B0", "B1", "C0", "C1", "D", "E")
GROUPS = pe_groups()
BANK_OF = dict(GROUPS)
USES = {x: [n for n, bank in GROUPS if bank == x] for x in BANKS}

CONST_DMA = 16 * 22
CONSTS_READY = 8

LINKS = {"dve": 56, "act": 2, "pool": 4}


def hold(eng, held):
    eng.sem_inc(held, 1)


def decoder_kernel(nc, x, ctx, wqkv, bqkv, proj, wo, bo, igk, igb, fgk, fgb, onw, wg, bg, w1, b1, w2, b2, out):
    x2_dram = nc.dram_tensor("x2_dram", [NB, P, NT, D], F32, kind="Internal").ap()
    x3_dram = nc.dram_tensor("x3_dram", [NB, 2, P, KC, L], F32, kind="Internal").ap()
    qk_dram = nc.dram_tensor("qk_dram", [NT, 2, 4, P, P], F32, kind="Internal").ap()
    f_dram = nc.dram_tensor("f_dram", [2, 2, 2, NG, P, P], F32, kind="Internal").ap()

    with ExitStack() as stack:
        def sem(name):
            return stack.enter_context(nc.semaphore(name))

        def sb0(name, shape, dt=F32):
            return stack.enter_context(nc.sbuf_tensor(name, shape, dt))

        banks = {x: stack.enter_context(nc.psum_tensor("bank" + x, [P, 512], F32)) for x in BANKS}
        wtok = sb0("wtok", [P, NB * NT, NE])
        attention_phase(nc, sem, banks, wtok, x, ctx, wqkv, bqkv, proj, wo, bo, igk, igb, fgk, fgb,
                        onw, wg, bg, b2, x2_dram, x3_dram, qk_dram, f_dram)
        ffn_phase(nc, sem, banks, wtok, w1, b1, w2, x2_dram, x3_dram, out)


def attention_phase(nc, sem, banks, wtok, x, ctx, wqkv, bqkv, proj, wo, bo, igk, igb, fgk, fgb,
                    onw, wg, bg, b2, x2_dram, x3_dram, qk_dram, f_dram):
    full = {b: sem("full_" + b) for b in BANKS}
    evac = {b: sem("evac_" + b) for b in BANKS}
    consts_loaded, consts_made, consts_ready = sem("consts_loaded"), sem("consts_made"), sem("consts_ready")
    x_loaded, x_free, xb_ready = sem("x_loaded"), sem("x_free"), sem("xb_ready")
    ctx_loaded, ctx_free = sem("ctx_loaded"), sem("ctx_free")
    ln_stats, ln_rstd, xhat_ready = sem("ln_stats"), sem("ln_rstd"), sem("xhat_ready")
    sq_ready, sq_read, qkh_ready = sem("sq_ready"), sem("sq_read"), sem("qkh_ready")
    qk_stored = [sem("qk_stored%d" % i) for i in range(NT)]
    f_stored = sem("f_stored")
    qs_loaded, fs_loaded = ([sem("%s_loaded%d" % (n, i)) for i in range(2)] for n in ("qs", "fs"))
    qf_exp, qf_ready, kf_sub, kf_exp, kf_ready = sem("qf_exp"), sem("qf_ready"), sem("kf_sub"), sem("kf_exp"), sem("kf_ready")
    mk_ready, kmax_diag = sem("mk_ready"), sem("kmax_diag")
    fh_ready = sem("fh_ready")
    nmx_ready, t_ready, e1_ready = sem("nmx_ready"), sem("t_ready"), sem("e1_ready")
    p_ready, c_ready = sem("p_ready"), sem("c_ready")
    lsig_ready, nm_ready, negm_ready, expn_ready = sem("lsig_ready"), sem("nm_ready"), sem("negm_ready"), sem("expn_ready")
    d_ready, dmask_ready = sem("d_ready"), sem("dmask_ready")
    x3h_ready, w_ready, x2_stored, x3_stored = sem("x3h_ready"), sem("w_ready"), sem("x2_stored"), sem("x3_stored")
    held = {e: sem("held_" + e) for e in ("pe", "dve", "pool", "sp")}
    dve_link, act_link, pool_link = sem("dve_link"), sem("act_link"), sem("pool_link")

    with ExitStack() as stack:
        def sb(name, shape, dt=F32):
            return stack.enter_context(nc.sbuf_tensor(name, shape, dt))

        wqkv_sb = sb("wqkv_sb", [P, KC, 3 * D])
        bqkv_bc = sb("bqkv_bc", [P, 3 * D])
        wo_sb = sb("wo_sb", [P, KC, D])
        bo_bc = sb("bo_bc", [P, D])
        pdh = sb("pdh", [P, H // 2, MP], F32R)
        pdl = sb("pdl", [P, H // 2, MP], F32R)
        win = sb("win", [P, 3, P])
        maskr = sb("maskr", [P, 3, P], F32R)
        ident = sb("ident", [P, P])
        identr = sb("identr", [P, P], F32R)
        wdT = sb("wdT", [P, P])
        wpT = sb("wpT", [P, P])
        ones = sb("ones", [P, P])
        blk = sb("blk", [P, HG * DH])
        gk = sb("gk", [P, 2 * KC, 36])
        gkv = sb("gkv", [P, KC, 36])
        igb_sb = sb("igb_sb", [4, 1])
        fgb_sb = sb("fgb_sb", [36, 1])
        onw_bc = sb("onw_bc", [P, D])
        sel = sb("sel", [4, NH, P])
        ones_row = sb("ones_row", [36, L])
        wg_sb = sb("wg_sb", [P, KC, NE])
        wgh = sb("wgh", [P, KC, NE], F32R)
        wgl = sb("wgl", [P, KC, NE], F32R)
        nbg = sb("nbg", [NE, 1])
        b2_sb = sb("b2_sb", [NE, D])
        mhalf = sb("mhalf", [P, H])

        x_in = sb("x_in", [P, NT, D])
        x1 = sb("x1", [P, NT, D])
        ctx_in = sb("ctx_in", [P, NT, NH, XD + 1])
        xh = sb("xh", [P, NT, D])
        xT = sb("xT", [P, KC, L])
        st6 = sb("st6", [P, NT * NH, 6])
        mv = sb("mv", [P, NT * NH, 2])
        rstd = sb("rstd", [P, NT * NH])
        rstd_in = sb("rstd_in", [P, NT * NH])
        qk_tm = sb("qk_tm", [P, 2, 2 * D])
        v_tm = sb("v_tm", [P, NT, H, MP])
        sqt = sb("sqt", [P, 2, 2 * D])
        sq = sb("sq", [P, NT, 2 * H])
        qkhl = sb("qkhl", [P, 2, 2, 4, P], F32R)
        qf = sb("qf", [P, NT, H, MP])
        kf = sb("kf", [P, NT, H, MP])
        mq = sb("mq", [P, NT, H])
        mk = sb("mk", [P, NT, H])
        mk1 = sb("mk1", [P, H])
        kmx = sb("kmx", [H, 1])
        kdg = sb("kdg", [H, H])
        kb = sb("kb", [P, H])
        gs = sb("gs", [P, NT, H])
        fhl = sb("fhl", [P, 2, 2, NG, P], F32R)
        qf32 = sb("qf32", [P, NG, P])
        qs = sb("qs", [QROWS, H, P], F32R)
        ks = sb("ks", [QROWS, H, 2, P], F32R)
        qfs = sb("qfs", [FROWS, H, P], F32R)
        kfs = sb("kfs", [FROWS, H, 2, P], F32R)
        E2 = [sb("E%d" % i, [P, H, 2, P]) for i in range(2)]
        GP = sb("GP", [P, 2, 2, 2, 2, P])
        GW, PT = GP[:, 0, :, :, :, :], GP[:, 1, :, :, :, :]
        OT = sb("OT", [P, NG, P])
        maskf = E2[0][:, 0:2, :, :].rearrange("p h s n -> p (h s) n")[:, 0:3, :]
        pd = E2[0][:, 2, :, :].rearrange("p s n -> p (s n)").rearrange("p (h m) -> p h m", m=MP)
        nmx = sb("nmx", [P, H])
        sume = sb("sume", [P, H])
        gsum = sb("gsum", [P, H])
        tt = sb("tt", [P, H])
        e1 = sb("e1", [P, H])
        gps = sb("gps", [P, H])
        aa = sb("aa", [P, H])
        rs = sb("rs", [P, 2, H])
        ut = sb("ut", [P, H, M])
        kvs = sb("kvs", [P, NG, HG * DH])
        stt = sb("stt", [P, H, DH])
        cc = sb("cc", [P, H, DH])
        cT = sb("cT", [P, KC, P])
        ctx_t = sqt[:, :, :].rearrange("p a n -> p (a n)").rearrange("p (t d) -> p t d", t=NT)
        cxT = sb("cxT", [P, KC, L])
        E1_row = E2[1][:, :, :, :].rearrange("p a b c -> p (a b c)")
        rows = E1_row[0:36, 0:6 * L].rearrange("p (r n) -> p r n", r=6)
        Dm = E1_row[:, 6 * L:8 * L].rearrange("p (i n) -> p i n", i=2)
        gT = sb("gT", [P, NT, 2, NH])
        nrm = sb("nrm", [P, 2, NH])
        x3h, x3l = (fhl[:, i, :, :, :].rearrange("p s g n -> p (s g n)").rearrange("p (k n) -> p k n", k=KC)
                    for i in range(2))
        zr = rows[0:NE, 0:3, :]

        R_ABS, R_MIN, R_F, R_G, R_M, R_NM = range(6)
        CT_LEN = sum(L - tc * P for tc in range(NT))
        GP_row = GP[:, :, :, :, :, :].rearrange("p w a b c n -> p (w a b c n)")
        E_row = E2[0][:, :, :, :].rearrange("p a b c -> p (a b c)")

        def ct(h, tc, a, b):
            o = h * CT_LEN + sum(L - i * P for i in range(tc))
            if h < 3:
                return E_row[:, o + a:o + b]
            o -= 3 * CT_LEN
            return GP_row[:, o + a:o + b]

        def slots(c):
            return 1 if c == 0 else 2

        def at(b, name):
            bank = BANK_OF[name]
            return b * len(USES[bank]) + USES[bank].index(name) + 1

        def wait_full(eng, b, *name):
            eng.wait_ge(full[BANK_OF[name]], at(b, name))

        def wait_evac(eng, b, *name):
            eng.wait_ge(evac[BANK_OF[name]], at(b, name) + 1)

        def wait_bank(pe, b, *name):
            pe.wait_ge(evac[BANK_OF[name]], at(b, name))

        def bank(*name):
            return banks[BANK_OF[name]]

        def evac_of(*name):
            return evac[BANK_OF[name]]

        def full_of(*name):
            return full[BANK_OF[name]]

        def linker(eng, link_sem, b, key):
            n = [0]

            def link(ins):
                n[0] += 1
                ins.then_inc(link_sem, 1)
                eng.wait_ge(link_sem, b * LINKS[key] + n[0])
            return link, n

        block = stack.enter_context(nc.Block())

        @block.sync
        def _(sp):
            for dst, src in (
                (wqkv_sb[:, :, :], wqkv.rearrange("(k p) n -> p k n", p=P)),
                (bqkv_bc[:, :], bqkv.partition_broadcast(P)),
                (wo_sb[:, :, :], wo.rearrange("(k p) n -> p k n", p=P)),
                (bo_bc[:, :], bo.partition_broadcast(P)),
                (igb_sb[:, :], igb), (fgb_sb[32:36, :], fgb),
                (onw_bc[:, :], onw.partition_broadcast(P)),
                (wg_sb[:, :, :], wg.rearrange("(k p) n -> p k n", p=P)),
                (nbg[:, :], bg), (b2_sb[:, :], b2),
            ):
                sp.dma_start(dst, src).then_inc(consts_loaded, 16)
            sp.wait_ge(consts_made, 3)
            for h in range(H // 2):
                sp.dma_start(pd[DH * h:DH * h + DH, h, 0:M], proj).then_inc(consts_loaded, 16)
            for (kern, at) in ((igk, 0), (fgk, 32)):
                v = kern.rearrange("(k p) n -> p k n", p=P)
                sp.dma_start(gk[:, 0:2 * KC, at:at + NH], v[:, 0:2 * KC, :]).then_inc(consts_loaded, 16)
                sp.dma_start(gkv[:, :, at:at + NH], v[:, 2 * KC:3 * KC, :]).then_inc(consts_loaded, 16)
            with sp.Fori(0, NB) as b:
                sp.wait_ge(x_free, b + 1)
                hold(sp, held["sp"])
                sp.dma_start(x_in[:, :, :], x[bass.ds(b, 1), :, :].rearrange("o (t p) d -> p (o t) d", p=P))\
                  .then_inc(x_loaded, 16)
                sp.wait_ge(ctx_free, b + 1)
                hold(sp, held["sp"])
                for t in range(NT):
                    src = ctx[bass.ds(b, 1), t * P:(t + 1) * P, :].rearrange("o p (h d) -> p (o h) d", h=NH)
                    sp.dma_start(ctx_in[:, t, :, 0:XD], src).then_inc(ctx_loaded, 16)
                for t in range(NT):
                    wait_evac(sp, b, "qkT", t)
                    for s in range(2):
                        sp.dma_start(qk_dram[t, s, :, :, :].rearrange("j p n -> p j n"),
                                     qkhl[:, t % 2, s, :, :].bitcast(F32)).then_inc(qk_stored[t], 16)

                sp.wait_ge(sq_read, b * NT + NT)
                hold(sp, held["sp"])
                sp.dma_start(ctx_t, ctx[bass.ds(b, 1), :, :].rearrange("o (t p) d -> p (o t) d", p=P)).then_inc(ctx_loaded, 16)

                def load_dots(c, half):
                    if half == 0:
                        sp.wait_ge(qk_stored[c], b * 32 + 32)
                        hold(sp, held["sp"])
                    if c:
                        wait_full(sp, b, "s", c - 1, H // 4 * (half + 1) - 1)
                    hs = slice(H // 2 * half, H // 2 * (half + 1))
                    for j, dst, parts in ((0, qs[:, hs, :], (0, 1, 0)), (2, ks[:, hs, c % 2, :], (0, 0, 1))):
                        for r, s in enumerate(parts):
                            sp.dma_start(dst[DH * r:DH * r + DH, :, :].bitcast(F32),
                                         qk_dram[c, s, j + half, :, :].rearrange("(h d) n -> d h n", d=DH))\
                              .then_inc(qs_loaded[half], 16)

                def store_features(c):
                    wait_evac(sp, b, "kfT", c)
                    for w in range(2):
                        for s in range(2):
                            sp.dma_start(f_dram[c % 2, w, s, :, :, :].rearrange("g p n -> p g n"),
                                         fhl[:, w, s, :, :].bitcast(F32)).then_inc(f_stored, 16)

                def load_features(c, half):
                    if half == 0:
                        sp.wait_ge(f_stored, b * 64 * NT + 64 * (c + 1))
                        hold(sp, held["sp"])
                    if c:
                        wait_full(sp, b, "sg", c - 1, H // 4 * (half + 1) - 1)
                    hs = slice(H // 2 * half, H // 2 * (half + 1))
                    gr = slice(NG // 2 * half, NG // 2 * (half + 1))
                    for w, dst, parts in ((0, qfs[:, hs, :], (0, 1, 0)), (1, kfs[:, hs, c % 2, :], (0, 0, 1))):
                        for r, s in enumerate(parts):
                            sp.dma_start(dst[M * r:M * r + M, :, :].bitcast(F32),
                                         f_dram[c % 2, w, s, gr, :, :].rearrange("g (h m) n -> m (g h) n", m=MP)[0:M, :, :])\
                              .then_inc(fs_loaded[half], 16)

                load_dots(0, 0)
                load_dots(0, 1)
                store_features(0)
                load_dots(1, 0)
                load_features(0, 0)
                load_features(0, 1)
                load_dots(1, 1)
                for c in range(NT - 1):
                    if c + 2 < NT:
                        load_dots(c + 2, 0)
                    store_features(c + 1)
                    load_features(c + 1, 0)
                    if c + 2 < NT:
                        load_dots(c + 2, 1)
                    load_features(c + 1, 1)
                wait_evac(sp, b, "x3T", NT - 1)
                hold(sp, held["sp"])
                for s, part in enumerate((x3h, x3l)):
                    sp.dma_start(x3_dram[bass.ds(b, 1), s, :, :, :].rearrange("o p k n -> p (o k) n"),
                                 part[:, :, :].bitcast(F32)).then_inc(x3_stored, 16)
                wait_evac(sp, b, "b2", NT - 1)
                hold(sp, held["sp"])
                sp.dma_start(x2_dram[bass.ds(b, 1), :, :, :].rearrange("o p t d -> p (o t) d"),
                             x1[:, :, :]).then_inc(x2_stored, 16)
            sp.wait_ge(x2_stored, 16 * NB + 16)
            sp.wait_ge(x3_stored, 32 * NB + 32)

        @block.gpsimd
        def _(pool):
            def make(ins):
                ins.then_inc(consts_made, 1)
                n_made[0] += 1

            n_made = [0]
            make(nc.gpsimd.memset(pd, 0.0))
            make(nc.gpsimd.memset(gk[:, :, :], 0.0))
            make(nc.gpsimd.memset(gkv[:, :, :], 0.0))
            make(nc.gpsimd.memset(ident[:, :], 0.0))
            make(nc.gpsimd.memset(ones[:, :], 1.0))
            make(nc.gpsimd.memset(maskf, 0.0))
            make(nc.gpsimd.memset(win[:, :, :], 1.0 - SCALE))
            make(nc.gpsimd.memset(blk[:, :], 1.0))
            make(nc.gpsimd.memset(sel[:, :, :], 0.0))
            make(nc.gpsimd.memset(mhalf[:, :], -0.5))
            make(nc.gpsimd.memset(ones_row[:, :], 1.0))
            make(nc.gpsimd.memset(v_tm[:, :, :, :], 0.0))
            make(nc.gpsimd.memset(qf[:, :, :, :], 0.0))
            make(nc.gpsimd.memset(kf[:, :, :, :], 0.0))
            make(nc.gpsimd.memset(ctx_in[:, :, :, XD:XD + 1], 1.0))
            make(nc.gpsimd.memset(qs[:, :, :].bitcast(F32), 0.0))
            make(nc.gpsimd.memset(ks[:, :, :, :].bitcast(F32), 0.0))
            make(nc.gpsimd.memset(kfs[:, :, :, :].bitcast(F32), 0.0))
            pool.wait_ge(consts_made, n_made[0])

            def select(out, src, pattern, op, fill, base, mult):
                make(nc.gpsimd.affine_select(out=out, in_=src, pattern=pattern, compare_op=op, fill=fill,
                                             base=base, channel_multiplier=mult))
                pool.wait_ge(consts_made, n_made[0])

            select(ident[:, :], ident[:, :], [[-1, P]], ALU.not_equal, 1.0, 0, 1)
            bv = blk[:, :].rearrange("p (h d) -> p h d", h=HG)
            select(bv, bv, [[-MP, HG], [0, DH]], ALU.is_ge, 0.0, 0, 1)
            select(bv, bv, [[MP, HG], [0, DH]], ALU.is_ge, 0.0, MP - 1, -1)
            select(sel[:, :, :], sel[:, :, :], [[-1, NH], [0, P]], ALU.not_equal, 1.0, 0, 1)
            for i in (0, 2):
                select(win[:, i, :], win[:, i, :], [[-1, P]], ALU.is_ge, 0.0, 0, 1)
                select(maskf[:, i, :], maskf[:, i, :], [[-1, P]], ALU.is_ge, MASK_VAL, 0, 1)
            select(win[:, 1, :], win[:, 1, :], [[1, P]], ALU.is_ge, 1.0, 0, -1)
            select(maskf[:, 1, :], maskf[:, 1, :], [[1, P]], ALU.is_ge, MASK_VAL, 0, -1)
            make(nc.gpsimd.memset(wdT[:, :], 1.0 - SCALE))
            make(nc.gpsimd.memset(wpT[:, :], 1.0 - SCALE))
            pool.wait_ge(consts_made, n_made[0])
            select(wdT[:, :], wdT[:, :], [[1, P]], ALU.is_ge, 0.0, 0, -1)
            select(wpT[:, :], wpT[:, :], [[-1, P]], ALU.is_ge, 1.0, 0, 1)
            pool.wait_ge(consts_loaded, 16 * 22)
            nc.gpsimd.tensor_tensor(gk[:, KC:2 * KC, :], gk[:, KC:2 * KC, :], gkv[:, :, :], ALU.add)\
              .then_inc(consts_ready, 1)
            nc.gpsimd.tensor_scalar(nbg[:, :], nbg[:, :], -1.0, None, ALU.mult).then_inc(consts_ready, 1)
            pool.sem_inc(x_free, 1)
            pool.sem_inc(ctx_free, 1)
            pool.sem_inc(x2_stored, 16)
            pool.sem_inc(x3_stored, 32)
            for k in BANKS:
                pool.sem_inc(evac[k], 1)

            with pool.Fori(0, NB) as b:
                link, n_links = linker(pool, pool_link, b, "pool")

                def rsqrt(k, n, eps):
                    pool.wait_ge(ln_stats, b * 4 + k + 1)
                    hold(pool, held["pool"])
                    link(nc.gpsimd.tensor_scalar(rstd_in[:, 0:n], mv[:, 0:n, 1], eps, None, ALU.add))
                    nc.gpsimd.tensor_tensor(rstd[:, 0:n], rstd_in[:, 0:n], mhalf[:, 0:n], ALU.pow)\
                      .then_inc(ln_rstd, 1)

                rsqrt(0, NT, LN_EPS)
                pool.wait_ge(xhat_ready, b * 3 * NT + NT)
                nc.gpsimd.tensor_tensor(x_in[:, :, :], x_in[:, :, :],
                                        bo_bc[:, :].unsqueeze(1).to_broadcast([P, NT, D]), ALU.add)\
                  .then_inc(xb_ready, 1)

                def add_eps_q(t):
                    pool.wait_ge(qf_exp, b * NT + t + 1)
                    hold(pool, held["pool"])
                    nc.gpsimd.tensor_scalar(qf[:, t, :, 0:M], qf[:, t, :, 0:M], FEAT_EPS, None, ALU.add)\
                      .then_inc(qf_ready, 1)

                for t in range(NT):
                    wait_evac(pool, b, "qk", t)
                    if t >= 2:
                        pool.wait_ge(sq_read, b * NT + t - 1)
                    nc.gpsimd.tensor_tensor(sqt[:, t % 2, :], qk_tm[:, t % 2, :], qk_tm[:, t % 2, :], ALU.mult)\
                      .then_inc(sq_ready, 1)
                    if t >= 2:
                        add_eps_q(t - 2)
                add_eps_q(NT - 2)
                add_eps_q(NT - 1)
                for t in range(NT):
                    pool.wait_ge(kf_exp, b * NT + t + 1)
                    hold(pool, held["pool"])
                    nc.gpsimd.tensor_scalar(kf[:, t, :, 0:M], kf[:, t, :, 0:M], FEAT_EPS, None, ALU.add)\
                      .then_inc(kf_ready, 1)
                for c in range(NT):
                    for u in range(H // 2):
                        wait_evac(pool, b, "s", c, u)
                        wait_evac(pool, b, "sg", c, u)
                        e = E2[c % 2][:, 2 * u:2 * u + 2, 0:slots(c), :]
                        nc.gpsimd.tensor_tensor(e, e, GW[:, u % 2, :, 0:slots(c), :], ALU.add).then_inc(p_ready, 1)
                rsqrt(1, NT, LN_EPS)
                for h in range(NH):
                    for tc in range(NT):
                        if tc < NT - 1:
                            pool.wait_ge(d_ready, b * NH * (NT - 1) + h * (NT - 1) + tc + 1)
                        else:
                            wait_evac(pool, b, "mB", h)
                        hold(pool, held["pool"])
                        nc.gpsimd.affine_select(out=Dm[:, tc % 2, 0:P], in_=Dm[:, tc % 2, 0:P], pattern=[[1, P]],
                                                compare_op=ALU.is_ge, fill=0.0, base=0, channel_multiplier=-1)\
                          .then_inc(dmask_ready, 1)
                rsqrt(2, NT * NH, X_EPS)
                rsqrt(3, NT, LN_EPS)
            assert n_links[0] == LINKS["pool"], ("pool", n_links)

        @block.scalar
        def _(act):
            act.wait_ge(consts_ready, CONSTS_READY)
            with act.Fori(0, NB) as b:
                link, n_links = linker(act, act_link, b, "act")

                def copy_xT(name, t):
                    wait_full(act, b, name, t)
                    src = bank(name, t)[:, 0:D].rearrange("p (k n) -> p k n", k=KC)
                    nc.scalar.activation(xT[:, :, t * P:(t + 1) * P], src, ACT.Copy).then_inc(evac_of(name, t), 1)

                def qk_high(t):
                    wait_full(act, b, "qkT", t)
                    if t >= 2:
                        wait_full(act, b, "xdk", t - 2)
                        act.wait_ge(qk_stored[t - 2], b * 32 + 32)
                    nc.scalar.activation(qkhl[:, t % 2, 0, :, :], bank("qkT", t)[:, :].rearrange("p (j n) -> p j n", j=4),
                                         ACT.Copy, scale=SCALE ** 0.5).then_inc(qkh_ready, 1)

                def q_exp(t):
                    wait_evac(act, b, "xdq", t)
                    nc.scalar.activation(qf[:, t, :, 0:M], qf[:, t, :, 0:M], ACT.Exp).then_inc(qf_exp, 1)

                for t in range(NT):
                    copy_xT("x1T", t)
                for t in range(NT):
                    qk_high(t)
                    if t >= 1:
                        q_exp(t - 1)
                q_exp(NT - 1)
                for t in range(NT):
                    act.wait_ge(kf_sub, b * NT + t + 1)
                    nc.scalar.activation(kf[:, t, :, 0:M], kf[:, t, :, 0:M], ACT.Exp).then_inc(kf_exp, 1)

                def features_high(c, w):
                    name = ("qfT", "kfT")[w]
                    wait_full(act, b, name, c)
                    src = bank(name, c)[:, :].rearrange("p (g n) -> p g n", g=NG)
                    if w == 0:
                        if c:
                            act.wait_ge(f_stored, b * 64 * NT + 64 * c)
                        else:
                            act.wait_ge(x3_stored, b * 32 + 32)
                    if w == 0 and c >= 2:
                        nc.scalar.activation(qf32[:, :, :], src, ACT.Copy)
                    nc.scalar.activation(fhl[:, w, 0, :, :], src, ACT.Copy).then_inc(fh_ready, 1)

                def scores_exp(c, u):
                    act.wait_ge(nmx_ready, b * NT * (H // 2) + c * (H // 2) + u + 1)
                    if c >= 2:
                        wait_full(act, b, "pT", c - 2, u)
                    for i in range(2):
                        h = 2 * u + i
                        src = bank("s", c, u)[:, i * 2 * P:(i + 1) * 2 * P].rearrange("p (s n) -> p s n", s=2)
                        ins = nc.scalar.activation(E2[c % 2][:, h, 0:slots(c), :], src[:, 0:slots(c), :],
                                                   ACT.Exp, bias=nmx[:, h:h + 1], accum_out=sume[:, h:h + 1])
                    ins.then_inc(evac_of("s", c, u), 1)

                def scale_exp(c):
                    act.wait_ge(t_ready, b * NT + c + 1)
                    nc.scalar.activation(e1[:, :], tt[:, :], ACT.Exp).then_inc(e1_ready, 1)

                def copy_context(c):
                    wait_full(act, b, "cT", c)
                    nc.scalar.activation(cT[:, :, :], bank("cT", c)[:, 0:D].rearrange("p (k n) -> p k n", k=KC), ACT.Copy)\
                      .then_inc(evac_of("cT", c), 1)

                features_high(0, 0)
                features_high(0, 1)
                for u in range(H // 2):
                    scores_exp(0, u)
                scale_exp(0)
                for c in range(NT):
                    for s in range(H // 2 + 2):
                        if s in (3, 4) and c + 1 < NT:
                            features_high(c + 1, s - 3)
                        if s == 5 and c:
                            copy_context(c - 1)
                        if s < H // 2 and c + 1 < NT:
                            scores_exp(c + 1, s)
                        if s >= 2:
                            wait_full(act, b, "pT", c, s - 2)
                            a = slots(c)
                            src = bank("pT", c, s - 2)[:, 0:2 * a * P].rearrange("p (h s n) -> p h s n", h=2, s=a)
                            nc.scalar.activation(PT[:, s % 2, :, 0:a, :], src, ACT.Copy)\
                              .then_inc(evac_of("pT", c, s - 2), 1)
                    if c + 1 < NT:
                        scale_exp(c + 1)
                    wait_full(act, b, "pv", c)
                    nc.scalar.activation(OT[:, :, :], bank("pv", c)[:, :].rearrange("p (g n) -> p g n", g=NG), ACT.Copy)\
                      .then_inc(evac_of("pv", c), 1)
                copy_context(NT - 1)
                for t in range(NT):
                    wait_full(act, b, "cxT", t)
                    nc.scalar.activation(cxT[:, :, t * P:(t + 1) * P],
                                         bank("cxT", t)[:, 0:D].rearrange("p (k n) -> p k n", k=KC), ACT.Copy)\
                      .then_inc(evac_of("cxT", t), 1)
                for t in range(NT):
                    copy_xT("x2T", t)
                wait_full(act, b, "gate")
                r = rows[32:36, R_ABS, :]
                link(nc.scalar.activation(r, bank("gate")[32:36, :], ACT.Abs, bias=fgb_sb[32:36, :]))
                link(nc.scalar.activation(r, r, ACT.Exp, scale=-1.0))
                nc.scalar.activation(r, r, ACT.Ln, bias=1.0).then_inc(lsig_ready, 1)
                act.wait_ge(negm_ready, b + 1)
                nc.scalar.activation(rows[0:4, R_ABS, :], rows[0:4, R_MIN, :], ACT.Exp).then_inc(expn_ready, 1)
                wait_evac(act, b, "rowT")
                for h in range(NH):
                    wait_full(act, b, "mB", h)
                    for tc in range(NT):
                        n = L - tc * P
                        if tc >= 2:
                            wait_evac(act, b, "qkm", h, tc - 2)
                        elif h:
                            wait_evac(act, b, "qkm", h - 1, tc + 2)
                        ins = nc.scalar.activation(Dm[:, tc % 2, 0:n], bank("mB", h)[:, tc * P:L], ACT.Exp,
                                                   bias=gT[:, tc, 0, h:h + 1])
                        ins.then_inc(d_ready if tc < NT - 1 else evac_of("mB", h), 1)
                act.wait_ge(f_stored, b * 64 * NT + 64 * NT)
                for t in range(NT):
                    wait_full(act, b, "x3T", t)
                    nc.scalar.activation(x3h[:, :, t * P:(t + 1) * P],
                                         bank("x3T", t)[:, 0:D].rearrange("p (k n) -> p k n", k=KC), ACT.Copy)\
                      .then_inc(x3h_ready, 1)
                wait_full(act, b, "z")
                nc.scalar.activation(zr[:, 0, :], bank("z")[0:NE, :], ACT.Exp, bias=nbg[:, :], scale=-1.0)\
                  .then_inc(evac_of("z"), 1)
            assert n_links[0] == LINKS["act"], ("act", n_links)

        @block.vector
        def _(dve):
            dve.wait_ge(consts_ready, 2)
            dve.wait_ge(consts_loaded, CONST_DMA)
            for hi, lo, src in ((pdh, pdl, pd), (wgh, wgl, wg_sb[:, :, :])):
                nc.vector.tensor_copy(hi[:, :, :], src).then_inc(consts_ready, 1)
                dve.wait_ge(consts_ready, 3 if hi is pdh else 5)
                nc.vector.tensor_tensor(lo[:, :, :], src, hi[:, :, :].bitcast(F32), ALU.subtract)\
                  .then_inc(consts_ready, 1)
            nc.vector.tensor_copy(identr[:, :], ident[:, :]).then_inc(consts_ready, 1)
            nc.vector.tensor_copy(maskr[:, :, :], maskf).then_inc(consts_ready, 1)
            dve.wait_ge(consts_ready, CONSTS_READY)

            with dve.Fori(0, NB) as b:
                link, n_links = linker(dve, dve_link, b, "dve")
                n_xhat = [0]

                def stats(src, n, first, done=None):
                    for i in range(n):
                        ins = nc.vector.bn_stats(st6[:, first + i, :], src(i))
                        if i == 0 and done is not None:
                            ins.then_inc(done, 1)
                    link(ins)
                    hold(dve, held["dve"])
                    for i in range(n):
                        ins = nc.vector.bn_aggr(mv[:, first + i, :], st6[:, first + i, :])
                    return ins

                def normalize(k, dst, src, n):
                    dve.wait_ge(ln_rstd, b * 4 + k + 1)
                    for i in range(n):
                        ins = nc.vector.tensor_scalar(dst(i), src(i), mv[:, i, 0:1], rstd[:, i:i + 1],
                                                      ALU.subtract, ALU.mult)
                        if k != 2:
                            ins.then_inc(xhat_ready, 1)
                    return ins

                dve.wait_ge(x_loaded, b * 16 + 16)
                stats(lambda t: x_in[:, t, :], NT, 0).then_inc(ln_stats, 1)
                normalize(0, lambda t: xh[:, t, :], lambda t: x_in[:, t, :], NT)

                def add_bias(t):
                    wait_full(dve, b, "qk", t)
                    if t >= 2:
                        dve.wait_ge(sq_ready, b * NT + t - 1)
                        wait_full(dve, b, "qkT", t - 2)
                    nc.vector.tensor_tensor(qk_tm[:, t % 2, :], bank("qk", t)[:, :], bqkv_bc[:, 0:2 * D], ALU.add)\
                      .then_inc(evac_of("qk", t), 1)
                    wait_full(dve, b, "v", t)
                    nc.vector.tensor_tensor(v_tm[:, t, :, 0:DH], bank("v", t)[:, 0:D].rearrange("p (h d) -> p h d", h=H),
                                            bqkv_bc[:, 2 * D:3 * D].rearrange("p (h d) -> p h d", h=H), ALU.add)\
                      .then_inc(evac_of("v", t), 1)

                def qk_low(t):
                    dve.wait_ge(qkh_ready, b * NT + t + 1)
                    nc.vector.scalar_tensor_tensor(
                        qkhl[:, t % 2, 1, :, :], bank("qkT", t)[:, :].rearrange("p (j n) -> p j n", j=4), SCALE ** 0.5,
                        qkhl[:, t % 2, 0, :, :].bitcast(F32), ALU.mult, ALU.subtract).then_inc(evac_of("qkT", t), 1)
                    dve.wait_ge(sq_ready, b * NT + t + 1)
                    nc.vector.tensor_reduce(sq[:, t, :], sqt[:, t % 2, :].rearrange("p (h d) -> p h d", d=DH),
                                            AX.X, ALU.add).then_inc(sq_read, 1)

                def logits(t):
                    xq = bank("xdq", t)[:, :].rearrange("p (h m) -> p h m", m=MP)[:, :, 0:M]
                    xk = bank("xdk", t)[:, :].rearrange("p (h m) -> p h m", m=MP)[:, :, 0:M]
                    wait_full(dve, b, "xdq", t)
                    link(nc.vector.tensor_reduce(mq[:, t, :], xq, AX.X, ALU.max))
                    nc.vector.tensor_tensor(qf[:, t, :, 0:M], xq, mq[:, t, :].unsqueeze(2).to_broadcast([P, H, M]),
                                            ALU.subtract).then_inc(evac_of("xdq", t), 1)
                    wait_full(dve, b, "xdk", t)
                    dve.wait_ge(sq_read, b * NT + t + 1)
                    nc.vector.scalar_tensor_tensor(kf[:, t, :, 0:M],
                                                   sq[:, t, H:2 * H].unsqueeze(2).to_broadcast([P, H, M]), -0.5 * SCALE,
                                                   xk, ALU.mult, ALU.add).then_inc(evac_of("xdk", t), 1)
                    nc.vector.scalar_tensor_tensor(gs[:, t, :], sq[:, t, 0:H], -0.5 * SCALE, mq[:, t, :],
                                                   ALU.mult, ALU.add)
                    wait_evac(dve, b, "xdk", t)
                    link(nc.vector.tensor_reduce(mk[:, t, :], kf[:, t, :, 0:M], AX.X, ALU.max))

                for s in range(NT + 2):
                    if s < NT:
                        add_bias(s)
                    if 1 <= s <= NT:
                        qk_low(s - 1)
                    if 2 <= s:
                        logits(s - 2)
                nc.vector.tensor_reduce(mk1[:, :], mk[:, :, :].rearrange("p t h -> p h t"), AX.X, ALU.max)\
                  .then_inc(mk_ready, 1)
                wait_full(dve, b, "mkT")
                nc.vector.tensor_reduce(kmx[:, :], bank("mkT")[0:H, 0:P], AX.X, ALU.max).then_inc(evac_of("mkT"), 1)
                wait_evac(dve, b, "mkT")
                nc.vector.tensor_scalar(kdg[:, :], ident[0:H, 0:H], kmx[:, 0:1], None, ALU.mult).then_inc(kmax_diag, 1)
                wait_full(dve, b, "mkB")
                nc.vector.tensor_copy(kb[:, :], bank("mkB")[:, 0:H]).then_inc(evac_of("mkB"), 1)
                wait_evac(dve, b, "mkB")
                for t in range(NT):
                    nc.vector.tensor_tensor(kf[:, t, :, 0:M], kf[:, t, :, 0:M],
                                            kb[:, :].unsqueeze(2).to_broadcast([P, H, M]), ALU.subtract)\
                      .then_inc(kf_sub, 1)
                link(nc.vector.tensor_tensor(gs[:, :, :], gs[:, :, :], kb[:, :].unsqueeze(1).to_broadcast([P, NT, H]),
                                             ALU.add))

                def features_low(c, w):
                    name = ("qfT", "kfT")[w]
                    dve.wait_ge(fh_ready, b * 2 * NT + 2 * c + w + 1)
                    nc.vector.tensor_tensor(fhl[:, w, 1, :, :], bank(name, c)[:, :].rearrange("p (g n) -> p g n", g=NG),
                                            fhl[:, w, 0, :, :].bitcast(F32), ALU.subtract)\
                      .then_inc(evac_of(name, c), 1)

                def denominator(c):
                    wait_full(dve, b, "u", c)
                    nc.vector.tensor_tensor(ut[:, :, :], bank("u", c)[:, :].rearrange("p (h m) -> p h m", m=MP)[:, :, 0:M],
                                            qf[:, c, :, 0:M], ALU.mult).then_inc(evac_of("u", c), 1)
                    wait_evac(dve, b, "u", c)
                    nc.vector.tensor_reduce(gsum[:, :], ut[:, :, :], AX.X, ALU.add)

                def maxima(c, u):
                    wait_full(dve, b, "s", c, u)
                    src = bank("s", c, u)[:, :].rearrange("p (h n) -> p h n", h=2)[:, :, 0:slots(c) * P]
                    nc.vector.tensor_reduce(nmx[:, 2 * u:2 * u + 2], src, AX.X, ALU.max, negate=True).then_inc(nmx_ready, 1)

                def scales(c):
                    dve.wait_ge(nmx_ready, b * NT * (H // 2) + (c + 1) * (H // 2))
                    nc.vector.scalar_tensor_tensor(tt[:, :], nmx[:, :], -1.0, gs[:, c, :], ALU.mult, ALU.subtract)\
                      .then_inc(t_ready, 1)
                    dve.wait_ge(e1_ready, b * NT + c + 1)
                    wait_evac(dve, b, "s", c, H // 2 - 1)
                    wait_evac(dve, b, "s", c, H // 2 - 2)
                    link(nc.vector.tensor_tensor(tt[:, :], e1[:, :], sume[:, :], ALU.mult))
                    link(nc.vector.scalar_tensor_tensor(tt[:, :], gsum[:, :], 1e-24, tt[:, :], ALU.max, ALU.add))
                    link(nc.vector.reciprocal(gps[:, :], tt[:, :]))
                    nc.vector.reciprocal(rs[:, c % 2, :], sume[:, :])
                    link(nc.vector.tensor_tensor(aa[:, :], gps[:, :], sume[:, :], ALU.mult))

                def features_part(c, u):
                    wait_full(dve, b, "sg", c, u)
                    if u >= 2:
                        dve.wait_ge(p_ready, b * NT * (H // 2) + c * (H // 2) + u - 1)
                    for i in range(2):
                        h = 2 * u + i
                        src = bank("sg", c, u)[:, i * 2 * P:(i + 1) * 2 * P].rearrange("p (s n) -> p s n", s=2)
                        ins = nc.vector.scalar_tensor_tensor(
                            GW[:, u % 2, i, 0:slots(c), :], src[:, 0:slots(c), :],
                            aa[:, h:h + 1], win[:, c % 2:c % 2 + slots(c), :], ALU.mult, ALU.mult)
                    ins.then_inc(evac_of("sg", c, u), 1)

                def far_features(c):
                    wait_full(dve, b, "kv", c)
                    nc.vector.tensor_tensor(kvs[:, :, :], bank("kv", c)[:, 0:NG * HG * DH].rearrange("p (g n) -> p g n", g=NG),
                                            blk[:, :].unsqueeze(1).to_broadcast([P, NG, HG * DH]), ALU.mult)\
                      .then_inc(evac_of("kv", c), 1)

                def far_part(c):
                    wait_full(dve, b, "st", c)
                    nc.vector.tensor_tensor(stt[:, :, :], bank("st", c)[:, 0:D].rearrange("p (h d) -> p h d", h=H),
                                            gps[:, :].unsqueeze(2).to_broadcast([P, H, DH]), ALU.mult)\
                      .then_inc(evac_of("st", c), 1)

                def context(c):
                    wait_full(dve, b, "oT", c)
                    nc.vector.tensor_tensor(cc[:, :, :], bank("oT", c)[:, :].rearrange("p (h d) -> p h d", d=MP)[:, :, 0:DH],
                                            rs[:, c % 2, :].unsqueeze(2).to_broadcast([P, H, DH]), ALU.mult)\
                      .then_inc(evac_of("oT", c), 1)
                    wait_evac(dve, b, "oT", c)
                    if c >= 2:
                        wait_evac(dve, b, "st", c)
                        nc.vector.tensor_tensor(cc[:, :, :], cc[:, :, :], stt[:, :, :], ALU.add).then_inc(c_ready, 1)

                def residual(c):
                    if c == 0:
                        dve.wait_ge(x2_stored, b * 16 + 16)
                        dve.wait_ge(xb_ready, b + 1)
                    wait_full(dve, b, "proj", c)
                    nc.vector.tensor_tensor(x1[:, c, :], bank("proj", c)[:, 0:D], x_in[:, c, :], ALU.add)\
                      .then_inc(evac_of("proj", c), 1)

                features_low(0, 0)
                features_low(0, 1)
                denominator(0)
                for u in range(H // 2):
                    maxima(0, u)
                scales(0)
                for c in range(NT):
                    for s in range(H // 2):
                        if s == 1 and c:
                            context(c - 1)
                        if s == 1 and c >= 2:
                            far_features(c)
                        if s == 2 and c >= 2:
                            far_part(c)
                        if s in (3, 4) and c + 1 < NT:
                            features_low(c + 1, s - 3)
                        if s == 6 and c:
                            residual(c - 1)
                        if c + 1 < NT:
                            maxima(c + 1, s)
                        features_part(c, s)
                    if c + 1 < NT:
                        denominator(c + 1)
                        scales(c + 1)
                context(NT - 1)
                residual(NT - 1)

                wait_evac(dve, b, "proj", NT - 1)
                stats(lambda t: x1[:, t, :], NT, 0, x_free).then_inc(ln_stats, 1)
                normalize(1, lambda t: xh[:, t, :], lambda t: x1[:, t, :], NT)
                wait_full(dve, b, "gate")
                dve.wait_ge(lsig_ready, b + 1)
                link(nc.vector.tensor_scalar(rows[32:36, R_MIN, :], bank("gate")[32:36, :], fgb_sb[32:36, :], 0.0,
                                             ALU.add, ALU.min))
                link(nc.vector.tensor_tensor(rows[32:36, R_MIN, :], rows[32:36, R_MIN, :], rows[32:36, R_ABS, :], ALU.subtract))
                link(nc.vector.tensor_tensor_scan(rows[0:4, R_F, :], ones_row[32:36, :], rows[32:36, R_MIN, :], 0.0,
                                                  ALU.mult, ALU.add))
                nc.vector.scalar_tensor_tensor(rows[0:4, R_G, :], bank("gate")[0:4, :], igb_sb[:, :], rows[0:4, R_F, :],
                                               ALU.add, ALU.subtract).then_inc(evac_of("gate"), 1)
                wait_evac(dve, b, "gate")
                link(nc.vector.tensor_tensor_scan(rows[0:4, R_M, :], rows[0:4, R_G, :], rows[0:4, R_G, :], -3.0e38,
                                                  ALU.max, ALU.max))
                nc.vector.scalar_tensor_tensor(rows[0:4, R_MIN, :], rows[0:4, R_F, :], -1.0, rows[0:4, R_M, :],
                                               ALU.mult, ALU.subtract).then_inc(negm_ready, 1)
                nc.vector.tensor_scalar(rows[0:4, R_NM, :], rows[0:4, R_M, :], -1.0, None, ALU.mult).then_inc(nm_ready, 1)
                wait_full(dve, b, "rowT")
                nc.vector.tensor_copy(gT[:, :, :, :], bank("rowT")[:, 0:NT * 2 * NH].rearrange("p (t w h) -> p t w h", t=NT, w=2))\
                  .then_inc(evac_of("rowT"), 1)
                for h in range(NH):
                    for tc in range(NT):
                        n = L - tc * P
                        wait_full(dve, b, "qkm", h, tc)
                        dve.wait_ge(dmask_ready, b * NH * NT + h * NT + tc + 1)
                        nc.vector.scalar_tensor_tensor(ct(h, tc, 0, n), bank("qkm", h, tc)[:, 0:n], XD ** -0.5,
                                                       Dm[:, tc % 2, 0:n], ALU.mult, ALU.mult)\
                          .then_inc(evac_of("qkm", h, tc), 1)
                wait_evac(dve, b, "rowT")
                for sc in range(NT):
                    wait_full(dve, b, "h", sc)
                    hv = bank("h", sc)[:, 0:NH * (XD + 1)].rearrange("p (h d) -> p h d", h=NH)
                    nr = nrm[:, sc % 2, :]
                    link(nc.vector.tensor_reduce(nr, hv[:, :, XD:XD + 1], AX.X, ALU.max, apply_absolute_value=True))
                    link(nc.vector.tensor_tensor(nr, nr, gT[:, sc, 1, :], ALU.max))
                    link(nc.vector.tensor_scalar(nr, nr, X_EPS, None, ALU.add))
                    link(nc.vector.reciprocal(nr, nr))
                    nc.vector.tensor_tensor(xh[:, sc, :].rearrange("p (h d) -> p h d", h=NH), hv[:, :, 0:XD],
                                            nr.unsqueeze(2).to_broadcast([P, NH, XD]), ALU.mult)\
                      .then_inc(evac_of("h", sc), 1)
                    wait_evac(dve, b, "h", sc)
                    ins = stats(lambda h: xh[:, sc, h * XD:(h + 1) * XD], NH, sc * NH)
                ins.then_inc(ln_stats, 1)
                link(normalize(2, lambda i: xh[:, i // NH, (i % NH) * XD:(i % NH + 1) * XD],
                               lambda i: xh[:, i // NH, (i % NH) * XD:(i % NH + 1) * XD], NT * NH))
                link(nc.vector.tensor_tensor(xh[:, :, :], xh[:, :, :], onw_bc[:, :].unsqueeze(1).to_broadcast([P, NT, D]),
                                             ALU.mult))
                nc.vector.tensor_tensor(x1[:, :, :], x1[:, :, :], xh[:, :, :], ALU.add).then_inc(ctx_free, 1)
                dve.wait_ge(ctx_free, b + 2)
                stats(lambda t: x1[:, t, :], NT, 0).then_inc(ln_stats, 1)
                normalize(3, lambda t: xh[:, t, :], lambda t: x1[:, t, :], NT)
                for t in range(NT):
                    dve.wait_ge(x3h_ready, b * NT + t + 1)
                    nc.vector.tensor_tensor(x3l[:, :, t * P:(t + 1) * P],
                                            bank("x3T", t)[:, 0:D].rearrange("p (k n) -> p k n", k=KC),
                                            x3h[:, :, t * P:(t + 1) * P].bitcast(F32), ALU.subtract)\
                      .then_inc(evac_of("x3T", t), 1)
                wait_evac(dve, b, "z")
                link(nc.vector.tensor_scalar(zr[:, 1, :], zr[:, 0, :], 1.0, None, ALU.add))
                link(nc.vector.reciprocal(zr[:, 1, :], zr[:, 1, :]))
                nc.vector.scalar_tensor_tensor(zr[:, 2, :], zr[:, 1, :], 0.5, zr[:, 1, :], ALU.is_gt, ALU.mult)\
                  .then_inc(w_ready, 1)
                wait_full(dve, b, "wT")
                nc.vector.tensor_copy(wtok[:, bass.ds(b * NT, NT), :],
                                      bank("wT")[:, 0:NT * NE].rearrange("p (t e) -> p t e", t=NT))\
                  .then_inc(evac_of("wT"), 1)
                for t in range(NT):
                    wait_full(dve, b, "b2", t)
                    nc.vector.tensor_tensor(x1[:, t, :], x1[:, t, :], bank("b2", t)[:, 0:D], ALU.add)\
                      .then_inc(evac_of("b2", t), 1)
            assert n_links[0] == LINKS["dve"], ("dve", n_links)

        @block.tensor
        def _(pe):
            pe.wait_ge(consts_ready, CONSTS_READY)
            with pe.Fori(0, NB) as b:
                emitted = []

                def begin(*name):
                    emitted.append((name, BANK_OF[name]))
                    wait_bank(pe, b, *name)
                    return bank(*name)

                def end(ins, *name):
                    ins.then_inc(full_of(*name), 1)

                def turn(name, t, src, base):
                    dst = begin(name, t)
                    for k in range(KC):
                        ins = nc.tensor.transpose(dst[:, k * P:(k + 1) * P], src(k), ident[:, :])
                    end(ins, name, t)

                for t in range(NT):
                    pe.wait_ge(xhat_ready, b * 3 * NT + t + 1)
                    turn("x1T", t, lambda k: xh[:, t, k * P:(k + 1) * P], 0)

                def project(t):
                    wait_evac(pe, b, "x1T", t)
                    dst = begin("qk", t)
                    for k in range(KC):
                        ins = nc.tensor.matmul(dst[:, :], xT[:, k, t * P:(t + 1) * P], wqkv_sb[:, k, 0:2 * D],
                                               start=k == 0, stop=k == KC - 1)
                    end(ins, "qk", t)
                    dst = begin("v", t)
                    for k in range(KC):
                        ins = nc.tensor.matmul(dst[:, 0:D], xT[:, k, t * P:(t + 1) * P], wqkv_sb[:, k, 2 * D:3 * D],
                                               start=k == 0, stop=k == KC - 1)
                    end(ins, "v", t)

                def turn_qk(t):
                    wait_evac(pe, b, "qk", t)
                    dst = begin("qkT", t)
                    for j in range(4):
                        ins = nc.tensor.transpose(dst[:, j * P:(j + 1) * P], qk_tm[:, t % 2, j * P:(j + 1) * P], ident[:, :])
                    end(ins, "qkT", t)

                def random_features(t):
                    wait_evac(pe, b, "qkT", t)
                    for name, j0 in (("xdq", 0), ("xdk", 2)):
                        dst = begin(name, t)
                        for j in range(2):
                            parts = ((0, pdh), (0, pdl), (1, pdh))
                            for i, (s, w) in enumerate(parts):
                                ins = nc.tensor.matmul(dst[:, j * 256:(j + 1) * 256], qkhl[:, t % 2, s, j0 + j, :],
                                                       w[:, :, :].rearrange("p h m -> p (h m)"),
                                                       start=i == 0, stop=i == len(parts) - 1)
                        end(ins, name, t)

                for s in range(NT + 2):
                    if s < NT:
                        project(s)
                    if 1 <= s <= NT:
                        turn_qk(s - 1)
                    if 2 <= s:
                        random_features(s - 2)
                pe.wait_ge(mk_ready, b + 1)
                dst = begin("mkT")
                end(nc.tensor.transpose(dst[0:H, 0:P], mk1[:, :], ident[:, :]), "mkT")
                pe.wait_ge(kmax_diag, b + 1)
                dst = begin("mkB")
                end(nc.tensor.matmul(dst[:, 0:H], ones[0:H, :], kdg[:, :], start=True, stop=True), "mkB")

                def turn_features(c, w):
                    name, f, ready = (("qfT", qf, qf_ready), ("kfT", kf, kf_ready))[w]
                    pe.wait_ge(ready, b * NT + c + 1)
                    dst = begin(name, c)
                    for g in range(NG):
                        ins = nc.tensor.transpose(dst[:, g * P:(g + 1) * P],
                                                  f[:, c, g * HG:(g + 1) * HG, :].rearrange("p h m -> p (h m)"), ident[:, :])
                    end(ins, name, c)

                def sum_features(c):
                    dst = begin("u", c)
                    for j in range(c + 1):
                        w = wdT if j == c else wpT if j == c - 1 else ones
                        ins = nc.tensor.matmul(dst[:, :], w[:, :], kf[:, j, :, :].rearrange("p h m -> p (h m)"),
                                               start=j == 0, stop=j == c)
                    end(ins, "u", c)

                def far_keys(c):
                    dst = begin("kv", c)
                    for g in range(NG):
                        for j in range(c - 1):
                            ins = nc.tensor.matmul(dst[:, g * 64:(g + 1) * 64],
                                                   kf[:, j, g * HG:(g + 1) * HG, :].rearrange("p h m -> p (h m)"),
                                                   v_tm[:, j, g * HG:(g + 1) * HG, 0:DH], start=j == 0, stop=j == c - 2)
                    end(ins, "kv", c)

                def far_queries(c):
                    wait_evac(pe, b, "kv", c)
                    pe.wait_ge(fh_ready, b * 2 * NT + 2 * c + 1)
                    dst = begin("st", c)
                    for g in range(NG):
                        ins = nc.tensor.matmul(dst[:, g * 64:(g + 1) * 64], qf32[:, g, :], kvs[:, g, :],
                                               start=True, stop=True)
                    end(ins, "st", c)

                def scores(c, u):
                    if u % (H // 4) == 0:
                        pe.wait_ge(qs_loaded[u // (H // 4)], b * 96 * NT + 96 * (c + 1))
                    dst = begin("s", c, u)
                    nc.tensor.matmul(dst[:, :], identr[:, :],
                                     maskr[:, c % 2:c % 2 + 2, :].unsqueeze(1).to_broadcast([P, 2, 2, P]),
                                     start=True, stop=False, skip_group_check=True)
                    for i in range(2):
                        h = 2 * u + i
                        ins = nc.tensor.matmul(dst[:, i * 256:(i + 1) * 256], qs[:, h, :],
                                               ks[:, h, :, :].rearrange("p s n -> p (s n)"),
                                               start=False, stop=i == 1, skip_group_check=True)
                    end(ins, "s", c, u)

                def feature_scores(c, u):
                    if u % (H // 4) == 0:
                        pe.wait_ge(fs_loaded[u // (H // 4)], b * 96 * NT + 96 * (c + 1))
                    dst = begin("sg", c, u)
                    for i in range(2):
                        h = 2 * u + i
                        ins = nc.tensor.matmul(dst[:, i * 256:(i + 1) * 256], qfs[:, h, :],
                                               kfs[:, h, :, :].rearrange("p s n -> p (s n)"), start=True, stop=True)
                    end(ins, "sg", c, u)

                def turn_probs(c, u):
                    pe.wait_ge(p_ready, b * NT * (H // 2) + c * (H // 2) + u + 1)
                    dst = begin("pT", c, u)
                    for i in range(2):
                        for k in range(slots(c)):
                            at_ = (i * slots(c) + k) * P
                            ins = nc.tensor.transpose(dst[:, at_:at_ + P], E2[c % 2][:, 2 * u + i, k, :], ident[:, :])
                    end(ins, "pT", c, u)

                def probs_times_v(c, u):
                    wait_evac(pe, b, "pT", c, u)
                    dst = begin("pv", c) if u == 0 else bank("pv", c)
                    for i in range(2):
                        h = 2 * u + i
                        q = h % HG
                        for k in range(slots(c)):
                            chunk = c if k == c % 2 else c - 1
                            ins = nc.tensor.matmul(dst[MP * q:MP * q + MP, (h // HG) * P:(h // HG + 1) * P],
                                                   v_tm[:, chunk, h, :], PT[:, u % 2, i, k, :],
                                                   start=k == 0, stop=k == slots(c) - 1)
                    if u == H // 2 - 1:
                        end(ins, "pv", c)

                def turn_out(c):
                    wait_evac(pe, b, "pv", c)
                    dst = begin("oT", c)
                    for g in range(NG):
                        ins = nc.tensor.transpose(dst[:, g * P:(g + 1) * P], OT[:, g, :], ident[:, :])
                    end(ins, "oT", c)

                def turn_context(c):
                    if c >= 2:
                        pe.wait_ge(c_ready, b * 2 + c - 1)
                    else:
                        wait_evac(pe, b, "oT", c)
                    dst = begin("cT", c)
                    cr = cc[:, :, :].rearrange("p h d -> p (h d)")
                    for k in range(KC):
                        ins = nc.tensor.transpose(dst[:, k * P:(k + 1) * P], cr[:, k * P:(k + 1) * P], ident[:, :])
                    end(ins, "cT", c)

                def project_out(c):
                    wait_evac(pe, b, "cT", c)
                    dst = begin("proj", c)
                    for k in range(KC):
                        ins = nc.tensor.matmul(dst[:, 0:D], cT[:, k, :], wo_sb[:, k, :], start=k == 0, stop=k == KC - 1)
                    end(ins, "proj", c)

                turn_features(0, 0)
                turn_features(0, 1)
                sum_features(0)
                for u in range(H // 2):
                    scores(0, u)
                for c in range(NT):
                    for s in range(H // 2 + 3):
                        if s < H // 2:
                            if c + 1 < NT:
                                scores(c + 1, s)
                            feature_scores(c, s)
                        if 2 <= s < H // 2 + 2:
                            turn_probs(c, s - 2)
                        if s >= 3:
                            probs_times_v(c, s - 3)
                        if s == 0 and c:
                            turn_out(c - 1)
                        if s == 0 and c >= 2:
                            far_keys(c)
                        if s == 1 and c >= 2:
                            far_queries(c)
                        if s in (2, 3) and c + 1 < NT:
                            turn_features(c + 1, s - 2)
                        if s == 4 and c:
                            turn_context(c - 1)
                        if s == 5 and c:
                            project_out(c - 1)
                        if s == 6 and c + 1 < NT:
                            sum_features(c + 1)
                turn_out(NT - 1)
                turn_context(NT - 1)
                project_out(NT - 1)

                pe.wait_ge(ctx_loaded, b * 16 * (NT + 1) + 16 * (NT + 1))
                for t in range(NT):
                    turn("cxT", t, lambda k: ctx_t[:, t, k * P:(k + 1) * P], 0)
                for t in range(NT):
                    pe.wait_ge(xhat_ready, b * 3 * NT + NT + t + 1)
                    turn("x2T", t, lambda k: xh[:, t, k * P:(k + 1) * P], 0)
                for t in range(NT):
                    wait_evac(pe, b, "cxT", t)
                    wait_evac(pe, b, "x2T", t)
                dst = begin("gate")
                for k in range(2 * KC):
                    src = xT[:, k, :] if k < KC else cxT[:, k - KC, :]
                    ins = nc.tensor.matmul(dst[0:36, :], gk[:, k, :], src, start=k == 0, stop=k == 2 * KC - 1)
                end(ins, "gate")
                pe.wait_ge(expn_ready, b + 1)
                dst = begin("rowT")
                hold(pe, held["pe"])
                for t in range(NT):
                    for w, r in enumerate((R_G, R_ABS)):
                        o = (t * 2 + w) * NH
                        ins = nc.tensor.transpose(dst[:, o:o + NH], rows[0:4, r, t * P:(t + 1) * P], ident[0:4, 0:4])
                end(ins, "rowT")
                pe.wait_ge(nm_ready, b + 1)
                for h in range(NH):
                    dst = begin("mB", h)
                    end(nc.tensor.matmul(dst[:, :], sel[:, h, :], rows[0:4, R_NM, :], start=True, stop=True), "mB", h)
                    r = (h % 2) * XD
                    for tc in range(NT):
                        dst = begin("qkm", h, tc)
                        end(nc.tensor.matmul(dst[:, 0:L - tc * P], cxT[r:r + XD, h // 2, tc * P:(tc + 1) * P],
                                             xT[r:r + XD, h // 2, tc * P:L], start=True, stop=True), "qkm", h, tc)
                wait_evac(pe, b, "qkm", NH - 1, NT - 1)
                for sc in range(NT):
                    dst = begin("h", sc)
                    for h in range(NH):
                        for tc in range(sc + 1):
                            ins = nc.tensor.matmul(dst[:, h * (XD + 1):(h + 1) * (XD + 1)],
                                                   ct(h, tc, (sc - tc) * P, (sc - tc + 1) * P), ctx_in[:, tc, h, :],
                                                   start=tc == 0, stop=tc == sc)
                    end(ins, "h", sc)
                for t in range(NT):
                    pe.wait_ge(xhat_ready, b * 3 * NT + 2 * NT + t + 1)
                    turn("x3T", t, lambda k: xh[:, t, k * P:(k + 1) * P], 0)
                wait_evac(pe, b, "x3T", NT - 1)
                wait_evac(pe, b, "x3T", NT - 2)
                dst = begin("z")
                zp = [(k, a, w) for k in range(KC) for a, w in ((x3h, wgh), (x3l, wgh), (x3h, wgl))]
                for i, (k, a, w) in enumerate(zp):
                    ins = nc.tensor.matmul(dst[0:NE, :], w[:, k, :], a[:, k, :], start=i == 0, stop=i == len(zp) - 1)
                end(ins, "z")
                pe.wait_ge(w_ready, b + 1)
                dst = begin("wT")
                hold(pe, held["pe"])
                for t in range(NT):
                    ins = nc.tensor.transpose(dst[:, t * NE:(t + 1) * NE], zr[:, 2, t * P:(t + 1) * P], ident[0:NE, 0:NE])
                end(ins, "wT")
                for t in range(NT):
                    dst = begin("b2", t)
                    end(nc.tensor.matmul(dst[:, 0:D], zr[:, 2, t * P:(t + 1) * P], b2_sb[:, :], start=True, stop=True), "b2", t)
                assert emitted == GROUPS


def ffn_phase(nc, sem, banks, wtok, w1, b1, w2, x2_dram, x3_dram, out):
    w_loaded = [sem("w_loaded%d" % i) for i in range(2)]
    b1_loaded = [sem("b1_loaded%d" % i) for i in range(2)]
    held_sp, held_pool = sem("held_sp2"), sem("held_pool2")
    w_high, w_split = sem("w_high"), sem("w_split")
    group_loaded = sem("group_loaded")
    up_full, hid_ready, hid_split = sem("up_full"), sem("hid_ready"), sem("hid_split")
    down_full, gate_copied, acc_done, out_stored = sem("down_full"), sem("gate_copied"), sem("acc_done"), sem("out_stored")
    PIECES = 4
    PCOLS = KC * HID // 2
    RING = 4
    CREDIT = 2 * NGRP
    with ExitStack() as stack:
        def sb(name, shape, dt=F32):
            return stack.enter_context(nc.sbuf_tensor(name, shape, dt))

        x3 = sb("x3", [P, NGRP, 2, KC, L], F32R)
        acc = sb("acc", [P, NB * NT, D])
        wraw = sb("wraw", [P, 2, PCOLS])
        w1p = sb("w1p", [P, 2, 2, KC, HID], F32R)
        w2p = sb("w2p", [P, 2, 2, NK, D], F32R)
        b1p = sb("b1p", [P, 2, NK])
        hid = sb("hid", [P, RING, L])
        hidr = sb("hidr", [P, RING, 2, L], F32R)
        gate = sb("gate", [P, 2, NT])
        up = [banks[k] for k in ("A0", "A1", "B0", "B1")]
        down = [banks[k] for k in ("C0", "C1", "D", "E")]

        def piece(parity, part, j):
            if j < KC:
                return w1p[:, parity, part, j, :]
            j -= KC
            return w2p[:, parity, part, j * NK // 2:(j + 1) * NK // 2, :].rearrange("p k n -> p (k n)")

        def over_groups(eng, body):
            with eng.Fori(0, NGRP // 2 - 1) as j:
                body(2 * j, 0, False)
                body(2 * j + 1, 1, False)
            body(NGRP - 2, 0, False)
            body(NGRP - 1, 1, True)

        block = stack.enter_context(nc.Block())

        @block.sync
        def _(sp):
            def load_piece(e, parity, j):
                sp.wait_ge(w_split, PIECES * e + j + 1)
                hold(sp, held_sp)
                dst = wraw[:, j % 2, :]
                if j < KC:
                    src = w1[bass.ds(e, 1), j * P:(j + 1) * P, :].rearrange("o p n -> p (o n)")
                else:
                    src = w2[bass.ds(e, 1), (j - KC) * HID // 2:(j - KC + 1) * HID // 2, :]\
                        .rearrange("o (k p) n -> p (o k) n", p=P)
                    dst = dst.rearrange("p (k n) -> p k n", n=D)
                sp.dma_start(dst, src).then_inc(w_loaded[j % 2], 16)

            def load_expert(e, parity):
                load_piece(e, parity, 0)
                load_piece(e, parity, 1)
                sp.wait_ge(acc_done, NGRP * e + NGRP)
                hold(sp, held_sp)
                sp.dma_start(b1p[:, parity, :], b1[bass.ds(e, 1), :, :].rearrange("o p k -> p (o k)")).then_inc(b1_loaded[parity], 16)
                load_piece(e, parity, 2)
                load_piece(e, parity, 3)

            def load_group(g):
                for s in range(2):
                    sp.dma_start(x3[:, g, s, :, :].bitcast(F32), x3_dram[g, s, :, :, :]).then_inc(group_loaded, 16)
                sp.dma_start(acc[:, g * NT:(g + 1) * NT, :], x2_dram[g, :, :, :]).then_inc(group_loaded, 16)

            load_group(0)
            load_expert(0, 0)
            for g in range(1, NGRP):
                sp.wait_ge(group_loaded, 48 * g)
                load_group(g)
            load_expert(1, 1)
            with sp.Fori(1, NE // 2) as i:
                load_expert(2 * i, 0)
                load_expert(2 * i + 1, 1)
            with sp.Fori(0, NGRP) as g:
                sp.wait_ge(acc_done, g + (CREDIT + (NE - 1) * NGRP + 1))
                hold(sp, held_sp)
                sp.dma_start(out[bass.ds(g, 1), :, :].rearrange("o (t p) d -> p (o t) d", p=P),
                             acc[:, bass.ds(g * NT, NT), :]).then_inc(out_stored, 16)
            sp.wait_ge(out_stored, 16 * NGRP)

        @block.gpsimd
        def _(pool):
            pool.sem_inc(w_split, 2)
            pool.sem_inc(acc_done, CREDIT)
            with pool.Fori(0, NE // 2) as i:
                for parity in range(2):
                    e = 2 * i + parity
                    pool.wait_ge(acc_done, NGRP * e + NGRP)
                    for j in range(PIECES):
                        pool.wait_ge(w_loaded[j % 2], 16 * (PIECES // 2) * e + 16 * (j // 2 + 1))
                        hold(pool, held_pool)
                        high, low = piece(parity, 0, j), piece(parity, 1, j)
                        nc.gpsimd.tensor_copy(high, wraw[:, j % 2, :]).then_inc(w_high, 1)
                        pool.wait_ge(w_high, PIECES * e + j + 1)
                        nc.gpsimd.tensor_tensor(low, wraw[:, j % 2, :], high.bitcast(F32), ALU.subtract)\
                          .then_inc(w_split, 1)

        @block.scalar
        def _(act):
            with act.Fori(0, NE // 2) as i:
                for parity in range(2):
                    e = 2 * i + parity
                    act.wait_ge(b1_loaded[parity], 16 * i + 16)

                    def group(g, gp, last):
                        for k in range(NK):
                            n = (e * NGRP + g) * NK + k
                            act.wait_ge(up_full, n + 1)
                            b = b1p[:, parity, k:k + 1]
                            nc.scalar.activation(hidr[:, k % RING, 0, :], up[k % RING][:, :], ACT.Relu, bias=b)
                            nc.scalar.activation(hid[:, k % RING, :], up[k % RING][:, :], ACT.Relu, bias=b)\
                              .then_inc(hid_ready, 1)

                    over_groups(act, group)

        @block.vector
        def _(dve):
            with dve.Fori(0, NE // 2) as i:
                for parity in range(2):
                    e = 2 * i + parity

                    def group(g, gp, last):
                        nc.vector.tensor_copy(gate[:, gp, :], wtok[:, bass.ds(g * NT, NT), bass.ds(e, 1)]
                                              .rearrange("p t o -> p (t o)")).then_inc(gate_copied, 1)
                        for k in range(NK):
                            n = (e * NGRP + g) * NK + k
                            dve.wait_ge(hid_ready, n + 1)
                            nc.vector.tensor_tensor(hidr[:, k % RING, 1, :], hid[:, k % RING, :],
                                                    hidr[:, k % RING, 0, :].bitcast(F32), ALU.subtract)\
                              .then_inc(hid_split, 1)
                        dve.wait_ge(gate_copied, e * NGRP + g + 1)
                        dve.wait_ge(group_loaded, 48 * g + 48)
                        dve.wait_ge(down_full, e * NGRP + g + 1)
                        for t in range(NT):
                            a = acc[:, bass.ds(g * NT + t, 1), :].rearrange("p o d -> p (o d)")
                            ins = nc.vector.scalar_tensor_tensor(a, down[2 * gp + t // 2][:, (t % 2) * D:(t % 2 + 1) * D],
                                                                 gate[:, gp, t:t + 1], a, ALU.mult, ALU.add)
                        ins.then_inc(acc_done, 1)

                    over_groups(dve, group)

        @block.tensor
        def _(pe):
            def x3_part(g, s, k):
                return x3[:, bass.ds(g, 1), s, k, :].rearrange("p o n -> p (o n)")

            with pe.Fori(0, NE // 2) as i:
                for parity in range(2):
                    e = 2 * i + parity

                    def up_step(g, k):
                        dst = up[k % RING]
                        prods = [(s, w, c) for c in range(KC) for s, w in ((0, 0), (0, 1), (1, 0))]
                        for m, (s, w, c) in enumerate(prods):
                            ins = nc.tensor.matmul(dst[:, :], w1p[:, parity, w, c, k * P:(k + 1) * P], x3_part(g, s, c),
                                                   start=m == 0, stop=m == len(prods) - 1)
                        ins.then_inc(up_full, 1)

                    pe.wait_ge(w_split, PIECES * e + KC + 2)
                    if parity == 0:
                        pe.wait_ge(group_loaded, 48)
                    up_step(0, 0)

                    def group(g, gp, last):
                        G = e * NGRP + g
                        for k in range(NK):
                            if k + 1 < NK:
                                up_step(g, k + 1)
                            elif not last:
                                pe.wait_ge(group_loaded, 48 * (g + 1) + 48)
                                up_step(g + 1, 0)
                            pe.wait_ge(hid_split, G * NK + k + 1)
                            if k == 0:
                                pe.wait_ge(w_split, PIECES * e + PIECES + 2)
                                pe.wait_ge(acc_done, G + CREDIT - 1)
                            for t in range(NT):
                                dst = down[2 * gp + t // 2][:, (t % 2) * D:(t % 2 + 1) * D]
                                for m, (s, w) in enumerate(((0, 0), (0, 1), (1, 0))):
                                    ins = nc.tensor.matmul(dst, hidr[:, k % RING, s, t * P:(t + 1) * P], w2p[:, parity, w, k, :],
                                                           start=k == 0 and m == 0 and t % 2 == 0, stop=k == NK - 1 and m == 2,
                                                           skip_group_check=True)
                        ins.then_inc(down_full, 1)

                    over_groups(pe, group)


_OUT = (NB, L, D)


def kernel(x, ctx_1024, L0_attn_Wqkv_w, L0_attn_Wqkv_b, L0_attn_proj, L0_attn_out_w, L0_attn_out_b,
           L0_xattn_ig_kernel, L0_xattn_ig_bias, L0_xattn_fg_kernel, L0_xattn_fg_bias, L0_xattn_outnorm_weight,
           L0_ffn_Wg, L0_ffn_bg, L0_ffn_W1, L0_ffn_b1, L0_ffn_W2, L0_ffn_b2):
    import numpy as np
    import concourse.bacc as bacc
    from concourse.bass_utils import run_bass_kernel_spmd

    layout = {
        "x": x, "ctx": ctx_1024, "wqkv": np.asarray(L0_attn_Wqkv_w).T, "bqkv": L0_attn_Wqkv_b,
        "proj": np.asarray(L0_attn_proj).T, "wo": np.asarray(L0_attn_out_w).T, "bo": L0_attn_out_b,
        "igk": L0_xattn_ig_kernel, "igb": np.asarray(L0_xattn_ig_bias).reshape(NH, 1),
        "fgk": L0_xattn_fg_kernel, "fgb": np.asarray(L0_xattn_fg_bias).reshape(NH, 1),
        "onw": np.asarray(L0_xattn_outnorm_weight).reshape(D),
        "wg": L0_ffn_Wg, "bg": np.asarray(L0_ffn_bg).reshape(NE, 1), "w1": L0_ffn_W1,
        "b1": np.asarray(L0_ffn_b1).reshape(NE, NK, P).transpose(0, 2, 1), "w2": L0_ffn_W2, "b2": L0_ffn_b2,
    }
    nc = bacc.Bacc("TRN2", target_bir_lowering=False, num_devices=1)
    arrays, aps = {}, {}
    for name, a in layout.items():
        a = np.ascontiguousarray(a)
        arrays["in_" + name] = a
        aps[name] = nc.dram_tensor("in_" + name, a.shape, mybir.dt.from_np(a.dtype), kind="ExternalInput").ap()
    out = nc.dram_tensor("out_dram", _OUT, F32, kind="ExternalOutput").ap()
    decoder_kernel(nc, out=out, **aps)
    r = run_bass_kernel_spmd(nc, [arrays], core_ids=[0])
    return r.results[0]["out_dram"]
```

```python
import concourse.bass as bass
from concourse import mybir
from contextlib import ExitStack

F32 = mybir.dt.float32
F32R = mybir.dt.float32r
ALU = mybir.AluOpType
ACT = mybir.ActivationFunctionType
AX = mybir.AxisListType

P = 128
NB = 8
L = 512
D = 256
NT = L // P
KC = D // P
H = 16
DH = D // H
M = 24
MP = 32
HG = 4
NG = H // HG
QROWS = 80
FROWS = 3 * M
NH = 4
XD = D // NH
NE = 8
HID = 1024
NK = HID // P
NTOK = NB * L
NGRP = NTOK // L
SCALE = DH ** -0.5
FEAT_EPS = 1e-4
MASK_VAL = -10000.0
LN_EPS = 1e-5
X_EPS = 1e-6


def attention_groups():
    g = []
    for c in range(NT):
        for s in range(H // 2 + 3):
            if s < H // 2:
                if c + 1 < NT:
                    g.append((("s", c + 1, s), "A%d" % (s % 2)))
                g.append((("sg", c, s), "B%d" % (s % 2)))
            if 2 <= s < H // 2 + 2:
                g.append((("pT", c, s - 2), "C%d" % (s % 2)))
            if s == 3:
                g.append((("pv", c), "D"))
            if s == 0 and c:
                g.append((("oT", c - 1), "D"))
            if s == 0 and c >= 2:
                g.append((("kv", c), "E"))
            if s == 1 and c >= 2:
                g.append((("st", c), "E"))
            if c == 0 and s in CTX_STEPS:
                g.append((("cxT", CTX_STEPS.index(s)), "E"))
            if s == 2 and c + 1 < NT:
                g.append((("qfT", c + 1), "E"))
            if s == 3 and c + 1 < NT:
                g.append((("kfT", c + 1), "E"))
            if s == 4 and c:
                g.append((("cT", c - 1), "E"))
            if s == 5 and c:
                g.append((("proj", c - 1), "E"))
            if s == 6 and c + 1 < NT:
                g.append((("u", c + 1), "E"))
            if c == NT - 1 and s in X_STEPS:
                g.append((("x1T", X_STEPS.index(s)), "E"))
    return g


def mixed_groups():
    g = [(("oT", NT - 1), "D"), (("qk", 0), "C0"), (("v", 0), "C1"), (("cT", NT - 1), "A0"), (("proj", NT - 1), "A1")]
    g += [(("qk", 1), "C0"), (("v", 1), "C1"), (("gate",), "B0"), (("qkT", 0), "D")]
    g += [(("x2T", t), "A%d" % (t % 2)) for t in range(NT)]
    g += [(("qk", 2), "C0"), (("v", 2), "C1"), (("qkT", 1), "D"), (("qk", 3), "C0"), (("v", 3), "C1")]
    g += [(("rowT",), "B1")]
    for h in range(NH + 1):
        if h == NT:
            g += [(("mkT",), "C0")]
        if h < NH:
            g += [(("mB", h), "A0"), (("qkm", h, 0), "B0"), (("qkm", h, 1), "B1")]
        if h < NT:
            g += [(("xdq", h), "E"), (("xdk", h), "C1")]
        if h < NH:
            g += [(("qkm", h, 2), "B0")]
        if h < NH:
            g += [(("qkm", h, 3), "B1")]
        if h + 2 < NT:
            g += [(("qkT", h + 2), "D")]
        if h:
            g += [(("h", h - 1), "A1" if h < NH else "A0")]
    g += [(("mkB",), "C1"), (("qfT", 0), "E")]
    g += [(("s", 0, u), "A%d" % (u % 2)) for u in (0, 1)]
    g += [(("kfT", 0), "C1"), (("u", 0), "C0")]
    g += [(("s", 0, u), "A%d" % (u % 2)) for u in (2, 3)]
    g += [(("x3T", t), "B%d" % (t % 2)) for t in range(NT)]
    g += [(("z",), "B0"), (("zT",), "B1")]
    g += [(("s", 0, u), "A%d" % (u % 2)) for u in (4, 5)] + [(("wR",), "B0")]
    g += [(("s", 0, u), "A%d" % (u % 2)) for u in (6, 7)]
    g += [(("b2", t), "B%d" % ((t + 1) % 2)) for t in range(NT)]
    return g


CTX_STEPS = (0, 1, 4, 5)
X_STEPS = (6, 7, 8, 9)
NEXT = ("x1T", "qk", "v", "qkT", "xdq", "xdk", "mkT", "mkB")


def is_next(name):
    return name[0] in NEXT or name[:2] in (("qfT", 0), ("kfT", 0), ("u", 0), ("s", 0))


BANKS = ("A0", "A1", "B0", "B1", "C0", "C1", "D", "E")
GROUPS = attention_groups() + mixed_groups()
BANK_OF = dict(GROUPS)
USES = {x: [n for n, bank in GROUPS if bank == x] for x in BANKS}
FIRST = {x: sum(is_next(n) for n in USES[x]) for x in BANKS}
assert all(not n_first or all(is_next(n) for n in USES[x][-n_first:]) for x, n_first in FIRST.items())

CONST_DMA = 16 * 22
CONSTS_READY = 9

LINKS = {"dve": 49, "dve_next": 10, "act": 2, "pool": 6, "pool_next": 1}


def hold(eng, held):
    eng.sem_inc(held, 1)


def decoder_kernel(nc, x, ctx, wqkv, bqkv, proj, wo, bo, igk, igb, fgk, fgb, onw, wg, bg, w1, b1, w2, b2, out):
    assert 4 * PCOLS == H * 2 * P and 2 * PCOLS == NT * H * MP
    x2_dram = nc.dram_tensor("x2_dram", [NB, P, NT, D], F32, kind="Internal").ap()
    x3_dram = nc.dram_tensor("x3_dram", [NB, 2, P, KC, L], F32, kind="Internal").ap()
    qk_dram = nc.dram_tensor("qk_dram", [NT, 2, 4, P, P], F32, kind="Internal").ap()
    f_dram = nc.dram_tensor("f_dram", [2, 2, 2, NG, P, P], F32, kind="Internal").ap()

    with ExitStack() as stack:
        def sem(name):
            return stack.enter_context(nc.semaphore(name))

        def sb0(name, shape, dt=F32):
            return stack.enter_context(nc.sbuf_tensor(name, shape, dt))

        banks = {x: stack.enter_context(nc.psum_tensor("bank" + x, [P, 512], F32)) for x in BANKS}
        wtok = sb0("wtok", [P, NB * NT, NE])
        split0 = sb0("split0", [P, 2, 2, 2 * PCOLS], F32R)
        wraw = sb0("wraw", [P, 2, PCOLS])
        w_loaded = [sem("w_loaded%d" % i) for i in range(2)]
        w_high, w_split = sem("w_high"), sem("w_split")
        weights = (split0, wraw, w_loaded, w_high, w_split)
        attention_phase(nc, sem, banks, wtok, x, ctx, wqkv, bqkv, proj, wo, bo, igk, igb, fgk, fgb,
                        onw, wg, bg, b2, x2_dram, x3_dram, qk_dram, f_dram, w1, w2, weights)
        ffn_phase(nc, sem, banks, wtok, w1, b1, w2, x2_dram, x3_dram, out, weights)


PIECES = 4
PCOLS = KC * HID // 2


def load_piece(sp, w1, w2, wraw, w_loaded, e, j):
    dst = wraw[:, j % 2, :]
    if j < KC:
        src = w1[bass.ds(e, 1), j * P:(j + 1) * P, :].rearrange("o p n -> p (o n)")
    else:
        src = w2[bass.ds(e, 1), (j - KC) * HID // 2:(j - KC + 1) * HID // 2, :].rearrange("o (k p) n -> p (o k) n", p=P)
        dst = dst.rearrange("p (k n) -> p k n", n=D)
    sp.dma_start(dst, src).then_inc(w_loaded[j % 2], 16)


def split_piece(nc, pool, high, low, src, w_high, w_split, n):
    nc.gpsimd.tensor_copy(high, src).then_inc(w_high, 1)
    pool.wait_ge(w_high, n)
    nc.gpsimd.tensor_tensor(low, src, high.bitcast(F32), ALU.subtract).then_inc(w_split, 1)


def attention_phase(nc, sem, banks, wtok, x, ctx, wqkv, bqkv, proj, wo, bo, igk, igb, fgk, fgb,
                    onw, wg, bg, b2, x2_dram, x3_dram, qk_dram, f_dram, w1, w2, weights):
    split0, wraw, w_loaded, w_high, w_split = weights
    full = {b: sem("full_" + b) for b in BANKS}
    evac = {b: sem("evac_" + b) for b in BANKS}
    consts_loaded, consts_made, consts_ready = sem("consts_loaded"), sem("consts_made"), sem("consts_ready")
    x_loaded, x_free, xb_ready = sem("x_loaded"), sem("x_free"), sem("xb_ready")
    ln1_loaded = sem("ln1_loaded")
    ctx_loaded, ctxt_loaded, ctx_free = sem("ctx_loaded"), sem("ctxt_loaded"), sem("ctx_free")
    ln1_stats, ln1_rstd, ln1_ready = sem("ln1_stats"), sem("ln1_rstd"), sem("ln1_ready")
    ln_stats, ln_rstd, xhat_ready = sem("ln_stats"), sem("ln_rstd"), sem("xhat_ready")
    sq_ready, sq_read, qkh_ready = sem("sq_ready"), sem("sq_read"), sem("qkh_ready")
    qk_stored = [sem("qk_stored%d" % i) for i in range(NT)]
    f_stored = sem("f_stored")
    qs_loaded, fs_loaded = ([sem("%s_loaded%d" % (n, i)) for i in range(2)] for n in ("qs", "fs"))
    qf_exp, qf_ready, kf_sub, kf_exp, kf_ready = sem("qf_exp"), sem("qf_ready"), sem("kf_sub"), sem("kf_exp"), sem("kf_ready")
    mk_ready, kmax_diag = sem("mk_ready"), sem("kmax_diag")
    fh_ready = sem("fh_ready")
    nmx_ready, t_ready, e1_ready = sem("nmx_ready"), sem("t_ready"), sem("e1_ready")
    p_ready, c_ready = sem("p_ready"), sem("c_ready")
    lsig_ready, nm_ready, negm_ready, expn_ready = sem("lsig_ready"), sem("nm_ready"), sem("negm_ready"), sem("expn_ready")
    d_ready, dmask_ready = sem("d_ready"), sem("dmask_ready")
    x3h_ready, ez_ready = sem("x3h_ready"), sem("ez_ready")
    x2_stored, x3_stored = sem("x2_stored"), sem("x3_stored")
    held = {e: sem("held_" + e) for e in ("pe", "dve", "pool", "sp")}
    links = {k: sem("link_" + k) for k in LINKS}

    with ExitStack() as stack:
        def sb(name, shape, dt=F32):
            return stack.enter_context(nc.sbuf_tensor(name, shape, dt))

        wqkv_sb = sb("wqkv_sb", [P, KC, 3 * D])
        bqkv_bc = sb("bqkv_bc", [P, 3 * D])
        wo_sb = sb("wo_sb", [P, KC, D])
        bo_bc = sb("bo_bc", [P, D])
        pdh = sb("pdh", [P, H // 2, MP], F32R)
        pdl = sb("pdl", [P, H // 2, MP], F32R)
        win = sb("win", [P, 3, P])
        maskr = sb("maskr", [P, 3, P], F32R)
        ident = sb("ident", [P, P])
        identr = sb("identr", [P, P], F32R)
        wdT = sb("wdT", [P, P])
        wpT = sb("wpT", [P, P])
        ones = sb("ones", [P, P])
        blk = sb("blk", [P, HG * DH])
        gk = sb("gk", [P, 2 * KC, 36])
        gkv = sb("gkv", [P, KC, 36])
        igb_sb = sb("igb_sb", [4, 1])
        fgb_sb = sb("fgb_sb", [36, 1])
        onw_bc = sb("onw_bc", [P, D])
        selr = sb("selr", [36, NH, P], F32R)
        nmr = sb("nmr", [36, L], F32R)
        ones_row = sb("ones_row", [36, L])
        wg_sb = sb("wg_sb", [P, KC, NE])
        wgh = sb("wgh", [P, KC, NE], F32R)
        wgl = sb("wgl", [P, KC, NE], F32R)
        nbg = sb("nbg", [NE, 1])
        b2_sb = sb("b2_sb", [NE, D])
        mhalf = sb("mhalf", [P, H])

        x_in = sb("x_in", [P, NT, D])
        x1 = sb("x1", [P, NT, D])
        ctx_in = sb("ctx_in", [P, NT, NH, XD + 1])
        xh = sb("xh", [P, NT, D])
        xT = sb("xT", [P, KC, L])
        st6_n = sb("st6_n", [P, NT, 6])
        mv_n = sb("mv_n", [P, NT, 2])
        rstd_n = sb("rstd_n", [P, NT])
        rstd_in_n = sb("rstd_in_n", [P, NT])
        st6 = sb("st6", [P, NT * (NH + 1), 6])
        mv = sb("mv", [P, NT * (NH + 1), 2])
        rstd = sb("rstd", [P, NT * (NH + 1)])
        rstd_in = sb("rstd_in", [P, NT * (NH + 1)])
        qk_tm = sb("qk_tm", [P, 2, 2 * D])
        v_tm = sb("v_tm", [P, NT, H, MP])
        sqt = sb("sqt", [P, 2, 2 * D])
        sq = sb("sq", [P, NT, 2 * H])
        qkhl = sb("qkhl", [P, 2, 2, 4, P], F32R)
        qf = wraw[:, :, :].rearrange("p i (t h m) -> p (i t) h m", t=NT // 2, h=H)
        kf = sb("kf", [P, NT, H, MP])
        mq = sb("mq", [P, NT, H])
        mk = sb("mk", [P, NT, H])
        mk1 = sb("mk1", [P, H])
        kmx = sb("kmx", [H, 1])
        kdg = sb("kdg", [H, H])
        kb = sb("kb", [P, H])
        gs = sb("gs", [P, NT, H])
        fhl = sb("fhl", [P, 2, 2, NG, P], F32R)
        qf32 = sb("qf32", [P, NG, P])
        qs = sb("qs", [QROWS, H, P], F32R)
        ks, kfs = (split0[0:n, i, :, :].rearrange("p w (h s n) -> p (w h) s n", h=H // 2, s=2)
                   for i, n in ((0, QROWS), (1, FROWS)))
        qfs = sb("qfs", [FROWS, H, P], F32R)
        E2 = [sb("E%d" % i, [P, H, 2, P]) for i in range(2)]
        GP = sb("GP", [P, 2, 2, 2, 2, P])
        GW, PT = GP[:, 0, :, :, :, :], GP[:, 1, :, :, :, :]
        OT = sb("OT", [P, NG, P])
        maskf = E2[0][:, 0:2, :, :].rearrange("p h s n -> p (h s) n")[:, 0:3, :]
        pd = E2[0][:, 2, :, :].rearrange("p s n -> p (s n)").rearrange("p (h m) -> p h m", m=MP)
        self32 = E2[0][0:36, 3:5, :, :].rearrange("p a s n -> p (a s) n")
        nmx = sb("nmx", [P, H])
        sume = sb("sume", [P, H])
        gsum = sb("gsum", [P, H])
        tt = sb("tt", [P, H])
        e1 = sb("e1", [P, H])
        gps = sb("gps", [P, H])
        aa = sb("aa", [P, H])
        rs = sb("rs", [P, 2, H])
        ut = sb("ut", [P, H, M])
        kvs = sb("kvs", [P, NG, HG * DH])
        stt = sb("stt", [P, H, DH])
        cc = sb("cc", [P, H, DH])
        cT = sb("cT", [P, KC, P])
        ctx_t = sqt[:, :, :].rearrange("p a n -> p (a n)").rearrange("p (t d) -> p t d", t=NT)
        cxT = sb("cxT", [P, 2, KC, L])
        E1_row = E2[1][:, :, :, :].rearrange("p a b c -> p (a b c)")
        rows = E1_row[0:36, 0:6 * L].rearrange("p (r n) -> p r n", r=6)
        Dm = E1_row[:, 6 * L:8 * L].rearrange("p (i n) -> p i n", i=2)
        gT = sb("gT", [P, NT, 2, NH])
        zt = sb("zt", [P, 2, NT, NE])
        nrm = sb("nrm", [P, 2, NH])
        GP_row = GP[:, :, :, :, :, :].rearrange("p w a b c n -> p (w a b c n)")
        E_row = E2[0][:, :, :, :].rearrange("p a b c -> p (a b c)")
        x3h, x3l = (qkhl[:, i, :, :, :].rearrange("p s j n -> p (s j n)").rearrange("p (k n) -> p k n", k=KC)
                    for i in range(2))
        zr = rows[0:NE, 0:3, :]

        R_ABS, R_MIN, R_F, R_G, R_M, R_NM = range(6)
        CT_LEN = sum(L - tc * P for tc in range(NT))
        xT_n = E_row[:, 2 * CT_LEN:2 * CT_LEN + KC * L].rearrange("p (k n) -> p k n", k=KC)

        def ct(h, tc, a, b):
            o = (h % 2) * CT_LEN + sum(L - i * P for i in range(tc))
            return E_row[:, o + a:o + b]

        def first_piece(j, part):
            return split0[:, j // 2, part, (j % 2) * PCOLS:(j % 2 + 1) * PCOLS]

        def slots(c):
            return 1 if c == 0 else 2

        def at(b, name):
            bank = BANK_OF[name]
            n = USES[bank].index(name) + 1 + FIRST[bank]
            return b * len(USES[bank]) + (n - len(USES[bank]) if is_next(name) else n)

        def wait_full(eng, b, *name):
            eng.wait_ge(full[BANK_OF[name]], at(b, name))

        def wait_evac(eng, b, *name):
            eng.wait_ge(evac[BANK_OF[name]], at(b, name) + 1)

        def wait_bank(pe, b, *name):
            pe.wait_ge(evac[BANK_OF[name]], at(b, name))

        def bank(*name):
            return banks[BANK_OF[name]]

        def evac_of(*name):
            return evac[BANK_OF[name]]

        def full_of(*name):
            return full[BANK_OF[name]]

        def linker(eng, b, key):
            n = [0]

            def link(ins):
                n[0] += 1
                ins.then_inc(links[key], 1)
                eng.wait_ge(links[key], b * LINKS[key] + n[0])
            return link, n

        block = stack.enter_context(nc.Block())

        @block.sync
        def _(sp):
            for dst, src in (
                (wqkv_sb[:, :, :], wqkv.rearrange("(k p) n -> p k n", p=P)),
                (bqkv_bc[:, :], bqkv.partition_broadcast(P)),
                (wo_sb[:, :, :], wo.rearrange("(k p) n -> p k n", p=P)),
                (bo_bc[:, :], bo.partition_broadcast(P)),
                (igb_sb[:, :], igb), (fgb_sb[32:36, :], fgb),
                (onw_bc[:, :], onw.partition_broadcast(P)),
                (wg_sb[:, :, :], wg.rearrange("(k p) n -> p k n", p=P)),
                (nbg[:, :], bg), (b2_sb[:, :], b2),
            ):
                sp.dma_start(dst, src).then_inc(consts_loaded, 16)
            sp.wait_ge(consts_made, 3)
            for h in range(H // 2):
                sp.dma_start(pd[DH * h:DH * h + DH, h, 0:M], proj).then_inc(consts_loaded, 16)
            for (kern, at) in ((igk, 0), (fgk, 32)):
                v = kern.rearrange("(k p) n -> p k n", p=P)
                sp.dma_start(gk[:, 0:2 * KC, at:at + NH], v[:, 0:2 * KC, :]).then_inc(consts_loaded, 16)
                sp.dma_start(gkv[:, :, at:at + NH], v[:, 2 * KC:3 * KC, :]).then_inc(consts_loaded, 16)
            def load_context(b):
                sp.wait_ge(ctx_free, b + 1)
                hold(sp, held["sp"])
                for t in range(NT):
                    src = ctx[bass.ds(b, 1), t * P:(t + 1) * P, :].rearrange("o p (h d) -> p (o h) d", h=NH)
                    sp.dma_start(ctx_in[:, t, :, 0:XD], src).then_inc(ctx_loaded, 16)

            def stack_moves(b):
                def load_dots(c, half):
                    if half == 0:
                        sp.wait_ge(qk_stored[c], b * 16 + 16)
                        hold(sp, held["sp"])
                    if c:
                        wait_full(sp, b, "s", c - 1, H // 4 * (half + 1) - 1)
                    hs = slice(H // 2 * half, H // 2 * (half + 1))
                    for j, dst, parts in ((0, qs[:, hs, :], (0, 1, 0)), (2, ks[:, hs, c % 2, :], (0, 0, 1))):
                        for r, s in enumerate(parts):
                            sp.dma_start(dst[DH * r:DH * r + DH, :, :].bitcast(F32),
                                         qk_dram[c, s, j + half, :, :].rearrange("(h d) n -> d h n", d=DH))\
                              .then_inc(qs_loaded[half], 16)

                def store_features(c):
                    wait_evac(sp, b, "kfT", c)
                    for w in range(2):
                        sp.dma_start(f_dram[c % 2, w, :, :, :, :].rearrange("s g p n -> p (s g) n"),
                                     fhl[:, w, :, :, :].rearrange("p s g n -> p (s g) n").bitcast(F32)).then_inc(f_stored, 16)

                def load_features(c, half):
                    if half == 0:
                        sp.wait_ge(f_stored, b * 32 * NT + 32 * (c + 1))
                        hold(sp, held["sp"])
                    if c:
                        wait_full(sp, b, "sg", c - 1, H // 4 * (half + 1) - 1)
                    hs = slice(H // 2 * half, H // 2 * (half + 1))
                    gr = slice(NG // 2 * half, NG // 2 * (half + 1))
                    for w, dst, parts in ((0, qfs[:, hs, :], (0, 1, 0)), (1, kfs[:, hs, c % 2, :], (0, 0, 1))):
                        for r, s in enumerate(parts):
                            sp.dma_start(dst[M * r:M * r + M, :, :].bitcast(F32),
                                         f_dram[c % 2, w, s, gr, :, :].rearrange("g (h m) n -> m (g h) n", m=MP)[0:M, :, :])\
                              .then_inc(fs_loaded[half], 16)

                return load_dots, store_features, load_features

            def load_x(b):
                sp.dma_start(xh[:, :, :], x[bass.ds(b, 1), :, :].rearrange("o (t p) d -> p (o t) d", p=P))\
                  .then_inc(ln1_loaded, 16)

            def first_part(b):
                sp.wait_ge(x_free, b + 1)
                hold(sp, held["sp"])
                sp.dma_start(x_in[:, :, :], x[bass.ds(b, 1), :, :].rearrange("o (t p) d -> p (o t) d", p=P))\
                  .then_inc(x_loaded, 16)
                for t in range(NT):
                    wait_evac(sp, b, "qkT", t)
                    sp.dma_start(qk_dram[t, :, :, :, :].rearrange("s j p n -> p (s j) n"),
                                 qkhl[:, t % 2, :, :, :].rearrange("p s j n -> p (s j) n").bitcast(F32)).then_inc(qk_stored[t], 16)
                load_dots, store_features, load_features = stack_moves(b)
                load_dots(0, 0)
                load_dots(0, 1)
                sp.wait_ge(sq_read, b * NT + NT)
                hold(sp, held["sp"])
                sp.dma_start(ctx_t, ctx[bass.ds(b, 1), :, :].rearrange("o (t p) d -> p (o t) d", p=P)).then_inc(ctxt_loaded, 16)
                store_features(0)
                load_features(0, 0)
                load_dots(1, 0)
                load_features(0, 1)

            def attention(b, n):
                if n is not None:
                    load_x(n)
                load_dots, store_features, load_features = stack_moves(b)
                for c in range(NT - 1):
                    if c + 2 < NT:
                        load_dots(c + 2, 0)
                    store_features(c + 1)
                    load_features(c + 1, 0)
                    if c + 2 < NT:
                        load_dots(c + 2, 1)
                    load_features(c + 1, 1)

            def store_results(b, n):
                wait_evac(sp, b, "x3T", NT - 1)
                hold(sp, held["sp"])
                for s, part in enumerate((x3h, x3l)):
                    sp.dma_start(x3_dram[bass.ds(b, 1), s, :, :, :].rearrange("o p k n -> p (o k) n"),
                                 part.bitcast(F32)).then_inc(x3_stored, 16)
                if n is not None:
                    load_dots, store_features, load_features = stack_moves(n)
                    load_dots(1, 1)
                wait_evac(sp, b, "b2", NT - 1)
                hold(sp, held["sp"])
                sp.dma_start(x2_dram[bass.ds(b, 1), :, :, :].rearrange("o p t d -> p (o t) d"),
                             x1[:, :, :]).then_inc(x2_stored, 16)

            load_x(0)
            load_context(0)
            first_part(0)
            load_dots, store_features, load_features = stack_moves(0)
            load_dots(1, 1)
            with sp.Fori(0, NB - 1) as b:
                attention(b, b + 1)
                first_part(b + 1)
                store_results(b, b + 1)
                load_context(b + 1)
            attention(NB - 1, None)
            wait_full(sp, NB - 1, "proj", NT - 1)
            wait_evac(sp, NB - 1, "proj", NT - 1)
            load_piece(sp, w1, w2, wraw, w_loaded, 0, 0)
            load_piece(sp, w1, w2, wraw, w_loaded, 0, 1)
            for j in (2, 3):
                sp.wait_ge(w_split, j + 1)
                load_piece(sp, w1, w2, wraw, w_loaded, 0, j)
            store_results(NB - 1, None)
            sp.wait_ge(x2_stored, 16 * NB + 16)
            sp.wait_ge(x3_stored, 32 * NB + 32)

        @block.gpsimd
        def _(pool):
            def make(ins):
                ins.then_inc(consts_made, 1)
                n_made[0] += 1

            n_made = [0]
            make(nc.gpsimd.memset(pd, 0.0))
            make(nc.gpsimd.memset(gk[:, :, :], 0.0))
            make(nc.gpsimd.memset(gkv[:, :, :], 0.0))
            make(nc.gpsimd.memset(ident[:, :], 0.0))
            make(nc.gpsimd.memset(ones[:, :], 1.0))
            make(nc.gpsimd.memset(maskf, 0.0))
            make(nc.gpsimd.memset(win[:, :, :], 1.0 - SCALE))
            make(nc.gpsimd.memset(blk[:, :], 1.0))
            make(nc.gpsimd.memset(self32, 0.0))
            make(nc.gpsimd.memset(nmr[:, :].bitcast(F32), 0.0))
            make(nc.gpsimd.memset(mhalf[:, :], -0.5))
            make(nc.gpsimd.memset(ones_row[:, :], 1.0))
            make(nc.gpsimd.memset(ctx_in[:, :, :, XD:XD + 1], 1.0))
            pool.wait_ge(consts_made, n_made[0])

            def select(out, src, pattern, op, fill, base, mult):
                make(nc.gpsimd.affine_select(out=out, in_=src, pattern=pattern, compare_op=op, fill=fill,
                                             base=base, channel_multiplier=mult))
                pool.wait_ge(consts_made, n_made[0])

            select(ident[:, :], ident[:, :], [[-1, P]], ALU.not_equal, 1.0, 0, 1)
            bv = blk[:, :].rearrange("p (h d) -> p h d", h=HG)
            select(bv, bv, [[-MP, HG], [0, DH]], ALU.is_ge, 0.0, 0, 1)
            select(bv, bv, [[MP, HG], [0, DH]], ALU.is_ge, 0.0, MP - 1, -1)
            for first in (0, 32):
                select(self32, self32, [[-1, NH], [0, P]], ALU.not_equal, 1.0, -first, 1)
            for i in (0, 2):
                select(win[:, i, :], win[:, i, :], [[-1, P]], ALU.is_ge, 0.0, 0, 1)
                select(maskf[:, i, :], maskf[:, i, :], [[-1, P]], ALU.is_ge, MASK_VAL, 0, 1)
            select(win[:, 1, :], win[:, 1, :], [[1, P]], ALU.is_ge, 1.0, 0, -1)
            select(maskf[:, 1, :], maskf[:, 1, :], [[1, P]], ALU.is_ge, MASK_VAL, 0, -1)
            make(nc.gpsimd.memset(wdT[:, :], 1.0 - SCALE))
            make(nc.gpsimd.memset(wpT[:, :], 1.0 - SCALE))
            pool.wait_ge(consts_made, n_made[0])
            select(wdT[:, :], wdT[:, :], [[1, P]], ALU.is_ge, 0.0, 0, -1)
            select(wpT[:, :], wpT[:, :], [[-1, P]], ALU.is_ge, 1.0, 0, 1)
            pool.wait_ge(consts_loaded, 16 * 22)
            nc.gpsimd.tensor_tensor(gk[:, KC:2 * KC, :], gk[:, KC:2 * KC, :], gkv[:, :, :], ALU.add)\
              .then_inc(consts_ready, 1)
            nc.gpsimd.tensor_scalar(nbg[:, :], nbg[:, :], -1.0, None, ALU.mult).then_inc(consts_ready, 1)
            pool.sem_inc(x_free, 1)
            pool.sem_inc(ctx_free, 1)
            pool.sem_inc(x2_stored, 16)
            pool.sem_inc(x3_stored, 32)
            for k in BANKS:
                pool.sem_inc(evac[k], 1)

            def rsqrt(link, b, k, n, eps, stats, variance, shifted, out, done):
                pool.wait_ge(stats, k)
                hold(pool, held["pool"])
                link(nc.gpsimd.tensor_scalar(shifted, variance, eps, None, ALU.add))
                nc.gpsimd.tensor_tensor(out, shifted, mhalf[:, 0:n], ALU.pow).then_inc(done, 1)

            def rsqrt_x(link, b, k, i, eps):
                r = slice(i * NT, (i + 1) * NT)
                rsqrt(link, b, b * (NH + 2) + k, NT, eps, ln_stats, mv[:, r, 1], rstd_in[:, r], rstd[:, r], ln_rstd)

            def normalize_first(b):
                link, n_links = linker(pool, b, "pool_next")
                rsqrt(link, b, b + 1, NT, LN_EPS, ln1_stats, mv_n[:, :, 1], rstd_in_n[:, :], rstd_n[:, :], ln1_rstd)
                assert n_links[0] == LINKS["pool_next"]

            def add_out_bias(b):
                pool.wait_ge(x_loaded, b * 16 + 16)
                hold(pool, held["pool"])
                nc.gpsimd.tensor_tensor(x_in[:, :, :], x_in[:, :, :],
                                        bo_bc[:, :].unsqueeze(1).to_broadcast([P, NT, D]), ALU.add)\
                  .then_inc(xb_ready, 1)

            def squares(b, t):
                wait_evac(pool, b, "qk", t)
                if t >= 2:
                    pool.wait_ge(sq_read, b * NT + t - 1)
                nc.gpsimd.tensor_tensor(sqt[:, t % 2, :], qk_tm[:, t % 2, :], qk_tm[:, t % 2, :], ALU.mult)\
                  .then_inc(sq_ready, 1)

            def add_eps(b, t, f, made, ready):
                pool.wait_ge(made, b * NT + t + 1)
                hold(pool, held["pool"])
                nc.gpsimd.tensor_scalar(f[:, t, :, 0:M], f[:, t, :, 0:M], FEAT_EPS, None, ALU.add).then_inc(ready, 1)

            def attention(b, n):
                for c in range(NT):
                    for u in range(H // 2):
                        wait_evac(pool, b, "s", c, u)
                        wait_evac(pool, b, "sg", c, u)
                        e = E2[c % 2][:, 2 * u:2 * u + 2, 0:slots(c), :]
                        nc.gpsimd.tensor_tensor(e, e, GW[:, u % 2, :, 0:slots(c), :], ALU.add).then_inc(p_ready, 1)
                    if c == 1 and n is not None:
                        normalize_first(n)

            def diagonal(b, h, tc):
                if tc < NT - 1:
                    pool.wait_ge(d_ready, b * NH * (NT - 1) + h * (NT - 1) + tc + 1)
                else:
                    wait_evac(pool, b, "mB", h)
                hold(pool, held["pool"])
                nc.gpsimd.affine_select(out=Dm[:, tc % 2, 0:P], in_=Dm[:, tc % 2, 0:P], pattern=[[1, P]],
                                        compare_op=ALU.is_ge, fill=0.0, base=0, channel_multiplier=-1)\
                  .then_inc(dmask_ready, 1)

            def mixed(b, n, mlstm):
                if n is not None:
                    if not mlstm:
                        normalize_first(n)
                    squares(n, 0)
                if mlstm:
                    link, n_links = linker(pool, b, "pool")
                    rsqrt_x(link, b, 1, NH, LN_EPS)
                if n is not None:
                    squares(n, 1)
                for h in range(NH + 2):
                    if mlstm and h < NH:
                        diagonal(b, h, 0)
                        diagonal(b, h, 1)
                    if n is not None and h + 2 < NT:
                        squares(n, h + 2)
                    if mlstm and h < NH:
                        diagonal(b, h, 2)
                        diagonal(b, h, 3)
                    if n is not None:
                        if 1 <= h <= NT:
                            add_eps(n, h - 1, qf, qf_exp, qf_ready)
                    if mlstm and 1 <= h <= NH:
                        rsqrt_x(link, b, h + 1, h - 1, X_EPS)
                if n is not None:
                    add_eps(n, 0, kf, kf_exp, kf_ready)
                if mlstm:
                    rsqrt_x(link, b, NH + 2, NH, LN_EPS)
                    assert n_links[0] == LINKS["pool"], ("pool", n_links)
                if n is not None:
                    for t in range(1, NT):
                        add_eps(n, t, kf, kf_exp, kf_ready)
                    add_out_bias(n)

            pool.sem_inc(w_split, 2)
            mixed(None, 0, False)
            with pool.Fori(0, NB - 1) as b:
                attention(b, b + 1)
                mixed(b, b + 1, True)
            attention(NB - 1, None)
            mixed(NB - 1, None, True)

        @block.scalar
        def _(act):
            act.wait_ge(consts_ready, CONSTS_READY)

            def features_high(b, c, w, first=False):
                name = ("qfT", "kfT")[w]
                wait_full(act, b, name, c)
                src = bank(name, c)[:, :].rearrange("p (g n) -> p g n", g=NG)
                if w == 0:
                    if c or not first:
                        act.wait_ge(f_stored, b * 32 * NT + 32 * c)
                if w == 0 and c >= 2:
                    nc.scalar.activation(qf32[:, :, :], src, ACT.Copy)
                nc.scalar.activation(fhl[:, w, 0, :, :], src, ACT.Copy).then_inc(fh_ready, 1)

            def scores_exp(b, c, u):
                act.wait_ge(nmx_ready, b * NT * (H // 2) + c * (H // 2) + u + 1)
                if c >= 2:
                    wait_full(act, b, "pT", c - 2, u)
                for i in range(2):
                    h = 2 * u + i
                    src = bank("s", c, u)[:, i * 2 * P:(i + 1) * 2 * P].rearrange("p (s n) -> p s n", s=2)
                    ins = nc.scalar.activation(E2[c % 2][:, h, 0:slots(c), :], src[:, 0:slots(c), :],
                                               ACT.Exp, bias=nmx[:, h:h + 1], accum_out=sume[:, h:h + 1])
                ins.then_inc(evac_of("s", c, u), 1)

            def copy_xT(b, name, dst, t):
                wait_full(act, b, name, t)
                src = bank(name, t)[:, 0:D].rearrange("p (k n) -> p k n", k=KC)
                nc.scalar.activation(dst[:, :, t * P:(t + 1) * P], src, ACT.Copy).then_inc(evac_of(name, t), 1)

            def copy_context(b, c):
                wait_full(act, b, "cT", c)
                nc.scalar.activation(cT[:, :, :], bank("cT", c)[:, 0:D].rearrange("p (k n) -> p k n", k=KC), ACT.Copy)\
                  .then_inc(evac_of("cT", c), 1)

            def qk_high(b, t):
                wait_full(act, b, "qkT", t)
                if t >= 2:
                    wait_full(act, b, "xdk", t - 2)
                    act.wait_ge(qk_stored[t - 2], b * 16 + 16)
                nc.scalar.activation(qkhl[:, t % 2, 0, :, :], bank("qkT", t)[:, :].rearrange("p (j n) -> p j n", j=4),
                                     ACT.Copy, scale=SCALE ** 0.5).then_inc(qkh_ready, 1)

            def q_exp(b, t):
                wait_evac(act, b, "xdq", t)
                nc.scalar.activation(qf[:, t, :, 0:M], qf[:, t, :, 0:M], ACT.Exp).then_inc(qf_exp, 1)

            def decay(b, h, tc):
                n = L - tc * P
                if tc == 0:
                    wait_full(act, b, "mB", h)
                if tc >= 2:
                    wait_evac(act, b, "qkm", h, tc - 2)
                elif h:
                    wait_evac(act, b, "qkm", h - 1, tc + 2)
                ins = nc.scalar.activation(Dm[:, tc % 2, 0:n], bank("mB", h)[:, tc * P:L], ACT.Exp,
                                           bias=gT[:, tc, 0, h:h + 1])
                ins.then_inc(d_ready if tc < NT - 1 else evac_of("mB", h), 1)

            def attention(b, n):
                def scale_exp(c):
                    act.wait_ge(t_ready, b * NT + c + 1)
                    nc.scalar.activation(e1[:, :], tt[:, :], ACT.Exp).then_inc(e1_ready, 1)

                def copy_ctx(t):
                    wait_full(act, b, "cxT", t)
                    for i in range(2):
                        r = slice(i * XD, (i + 1) * XD)
                        ins = nc.scalar.activation(cxT[r, i, :, t * P:(t + 1) * P],
                                                   bank("cxT", t)[r, 0:D].rearrange("p (k n) -> p k n", k=KC), ACT.Copy)
                    ins.then_inc(evac_of("cxT", t), 1)

                scale_exp(0)
                for c in range(NT):
                    for s in range(H // 2 + 3):
                        if s in (3, 4) and c + 1 < NT:
                            features_high(b, c + 1, s - 3)
                        if s == 5 and c:
                            copy_context(b, c - 1)
                        if c == NT - 1 and s - 1 in X_STEPS and n is not None:
                            copy_xT(n, "x1T", xT_n, X_STEPS.index(s - 1))
                        if c == 0 and s - 1 in CTX_STEPS:
                            copy_ctx(CTX_STEPS.index(s - 1))
                        if 2 <= s < H // 2 + 2:
                            wait_full(act, b, "pT", c, s - 2)
                            a = slots(c)
                            src = bank("pT", c, s - 2)[:, 0:2 * a * P].rearrange("p (h s n) -> p h s n", h=2, s=a)
                            nc.scalar.activation(PT[:, s % 2, :, 0:a, :], src, ACT.Copy)\
                              .then_inc(evac_of("pT", c, s - 2), 1)
                        if s < H // 2 and c + 1 < NT:
                            scores_exp(b, c + 1, s)
                    if c + 1 < NT:
                        scale_exp(c + 1)
                    wait_full(act, b, "pv", c)
                    nc.scalar.activation(OT[:, :, :], bank("pv", c)[:, :].rearrange("p (g n) -> p g n", g=NG), ACT.Copy)\
                      .then_inc(evac_of("pv", c), 1)

            def mixed(b, n, mlstm):
                if mlstm:
                    copy_context(b, NT - 1)
                    act.wait_ge(x3_stored, b * 32 + 32)
                else:
                    for t in range(NT):
                        copy_xT(n, "x1T", xT_n, t)
                if n is not None:
                    qk_high(n, 0)
                if mlstm:
                    link, n_links = linker(act, b, "act")
                    for t in range(NT):
                        copy_xT(b, "x2T", xT, t)
                    wait_full(act, b, "gate")
                    r = rows[32:36, R_ABS, :]
                    link(nc.scalar.activation(r, bank("gate")[32:36, :], ACT.Abs, bias=fgb_sb[32:36, :]))
                    link(nc.scalar.activation(r, r, ACT.Exp, scale=-1.0))
                    nc.scalar.activation(r, r, ACT.Ln, bias=1.0).then_inc(lsig_ready, 1)
                    assert n_links[0] == LINKS["act"], ("act", n_links)
                    act.wait_ge(negm_ready, b + 1)
                    nc.scalar.activation(rows[0:4, R_ABS, :], rows[0:4, R_MIN, :], ACT.Exp).then_inc(expn_ready, 1)
                if n is not None:
                    qk_high(n, 1)
                if mlstm:
                    wait_evac(act, b, "rowT")
                for h in range(NH):
                    if mlstm:
                        for tc in range(NT):
                            decay(b, h, tc)
                    if n is not None:
                        if h + 2 < NT:
                            qk_high(n, h + 2)
                        q_exp(n, h)
                    elif h < PIECES:
                        act.wait_ge(w_loaded[h % 2], 16 * (h // 2 + 1))
                        nc.scalar.activation(first_piece(h, 0), wraw[:, h % 2, :], ACT.Copy).then_inc(w_high, 1)
                if n is not None:
                    first = not mlstm
                    for t in range(NT):
                        act.wait_ge(kf_sub, n * NT + t + 1)
                        nc.scalar.activation(kf[:, t, :, 0:M], kf[:, t, :, 0:M], ACT.Exp).then_inc(kf_exp, 1)
                        if t == 0:
                            features_high(n, 0, 0, first)
                    for u in (0, 1):
                        scores_exp(n, 0, u)
                if mlstm:
                    if n is not None:
                        for stored in qk_stored[NT - 2:]:
                            act.wait_ge(stored, n * 16 + 16)
                    for t in range(NT):
                        wait_full(act, b, "x3T", t)
                        nc.scalar.activation(x3h[:, :, t * P:(t + 1) * P],
                                             bank("x3T", t)[:, 0:D].rearrange("p (k n) -> p k n", k=KC), ACT.Copy)\
                          .then_inc(x3h_ready, 1)
                if n is not None:
                    features_high(n, 0, 1)
                for u in range(2, H // 2):
                    if u == 4 and mlstm:
                        wait_full(act, b, "zT")
                        nc.scalar.activation(zt[:, 0, :, :], bank("zT")[:, 0:NT * NE].rearrange("p (t e) -> p t e", t=NT),
                                             ACT.Exp).then_inc(ez_ready, 1)
                    if u == 6 and mlstm:
                        wait_full(act, b, "wR")
                        nc.scalar.activation(zr[:, 1, :], bank("wR")[0:NE, :], ACT.Copy).then_inc(evac_of("wR"), 1)
                    if n is not None:
                        scores_exp(n, 0, u)

            mixed(None, 0, False)
            with act.Fori(0, NB - 1) as b:
                attention(b, b + 1)
                mixed(b, b + 1, True)
            attention(NB - 1, None)
            mixed(NB - 1, None, True)

        @block.vector
        def _(dve):
            for t in (v_tm[:, :, :, :], qf[:, :, :, :], kf[:, :, :, :], qs[:, :, :].bitcast(F32),
                      ks[:, :, :, :].bitcast(F32), kfs[:, :, :, :].bitcast(F32), cxT[:, :, :, :]):
                nc.vector.memset(t, 0.0)
            dve.wait_ge(consts_ready, 2)
            dve.wait_ge(consts_loaded, CONST_DMA)
            for hi, lo, src in ((pdh, pdl, pd), (wgh, wgl, wg_sb[:, :, :])):
                nc.vector.tensor_copy(hi[:, :, :], src).then_inc(consts_ready, 1)
                dve.wait_ge(consts_ready, 3 if hi is pdh else 5)
                nc.vector.tensor_tensor(lo[:, :, :], src, hi[:, :, :].bitcast(F32), ALU.subtract)\
                  .then_inc(consts_ready, 1)
            nc.vector.tensor_copy(identr[:, :], ident[:, :]).then_inc(consts_ready, 1)
            nc.vector.tensor_copy(maskr[:, :, :], maskf).then_inc(consts_ready, 1)
            nc.vector.tensor_copy(selr[:, :, :], self32).then_inc(consts_ready, 1)
            dve.wait_ge(consts_ready, CONSTS_READY)

            def features_low(b, c, w):
                name = ("qfT", "kfT")[w]
                dve.wait_ge(fh_ready, b * 2 * NT + 2 * c + w + 1)
                nc.vector.tensor_tensor(fhl[:, w, 1, :, :], bank(name, c)[:, :].rearrange("p (g n) -> p g n", g=NG),
                                        fhl[:, w, 0, :, :].bitcast(F32), ALU.subtract)\
                  .then_inc(evac_of(name, c), 1)

            def denominator(b, c):
                wait_full(dve, b, "u", c)
                nc.vector.tensor_tensor(ut[:, :, :], bank("u", c)[:, :].rearrange("p (h m) -> p h m", m=MP)[:, :, 0:M],
                                        qf[:, c, :, 0:M], ALU.mult).then_inc(evac_of("u", c), 1)
                wait_evac(dve, b, "u", c)
                nc.vector.tensor_reduce(gsum[:, :], ut[:, :, :], AX.X, ALU.add)

            def maxima(b, c, u):
                wait_full(dve, b, "s", c, u)
                src = bank("s", c, u)[:, :].rearrange("p (h n) -> p h n", h=2)[:, :, 0:slots(c) * P]
                nc.vector.tensor_reduce(nmx[:, 2 * u:2 * u + 2], src, AX.X, ALU.max, negate=True).then_inc(nmx_ready, 1)

            def context(b, c):
                wait_full(dve, b, "oT", c)
                nc.vector.tensor_tensor(cc[:, :, :], bank("oT", c)[:, :].rearrange("p (h d) -> p h d", d=MP)[:, :, 0:DH],
                                        rs[:, c % 2, :].unsqueeze(2).to_broadcast([P, H, DH]), ALU.mult)\
                  .then_inc(evac_of("oT", c), 1)
                wait_evac(dve, b, "oT", c)
                if c >= 2:
                    wait_evac(dve, b, "st", c)
                    nc.vector.tensor_tensor(cc[:, :, :], cc[:, :, :], stt[:, :, :], ALU.add).then_inc(c_ready, 1)

            def residual(b, c):
                if c == 0:
                    dve.wait_ge(x2_stored, b * 16 + 16)
                    dve.wait_ge(xb_ready, b + 1)
                wait_full(dve, b, "proj", c)
                nc.vector.tensor_tensor(x1[:, c, :], bank("proj", c)[:, 0:D], x_in[:, c, :], ALU.add)\
                  .then_inc(evac_of("proj", c), 1)

            def first_part(b):
                link, n_links = linker(dve, b, "dve_next")

                def stats_first():
                    dve.wait_ge(ln1_loaded, b * 16 + 16)
                    for t in range(NT):
                        ins = nc.vector.bn_stats(st6_n[:, t, :], xh[:, t, :])
                    link(ins)
                    hold(dve, held["dve"])
                    for t in range(NT):
                        ins = nc.vector.bn_aggr(mv_n[:, t, :], st6_n[:, t, :])
                    ins.then_inc(ln1_stats, 1)

                def normalize_first(t):
                    dve.wait_ge(ln1_rstd, b + 1)
                    nc.vector.tensor_scalar(xh[:, t, :], xh[:, t, :], mv_n[:, t, 0:1], rstd_n[:, t:t + 1],
                                            ALU.subtract, ALU.mult).then_inc(ln1_ready, 1)

                def add_bias(t):
                    wait_full(dve, b, "qk", t)
                    if t >= 2:
                        dve.wait_ge(sq_ready, b * NT + t - 1)
                        wait_full(dve, b, "qkT", t - 2)
                    nc.vector.tensor_tensor(qk_tm[:, t % 2, :], bank("qk", t)[:, :], bqkv_bc[:, 0:2 * D], ALU.add)\
                      .then_inc(evac_of("qk", t), 1)
                    wait_full(dve, b, "v", t)
                    nc.vector.tensor_tensor(v_tm[:, t, :, 0:DH], bank("v", t)[:, 0:D].rearrange("p (h d) -> p h d", h=H),
                                            bqkv_bc[:, 2 * D:3 * D].rearrange("p (h d) -> p h d", h=H), ALU.add)\
                      .then_inc(evac_of("v", t), 1)

                def qk_low(t):
                    dve.wait_ge(qkh_ready, b * NT + t + 1)
                    nc.vector.scalar_tensor_tensor(
                        qkhl[:, t % 2, 1, :, :], bank("qkT", t)[:, :].rearrange("p (j n) -> p j n", j=4), SCALE ** 0.5,
                        qkhl[:, t % 2, 0, :, :].bitcast(F32), ALU.mult, ALU.subtract).then_inc(evac_of("qkT", t), 1)
                    dve.wait_ge(sq_ready, b * NT + t + 1)
                    nc.vector.tensor_reduce(sq[:, t, :], sqt[:, t % 2, :].rearrange("p (h d) -> p h d", d=DH),
                                            AX.X, ALU.add).then_inc(sq_read, 1)

                def logits(t):
                    xq = bank("xdq", t)[:, :].rearrange("p (h m) -> p h m", m=MP)[:, :, 0:M]
                    xk = bank("xdk", t)[:, :].rearrange("p (h m) -> p h m", m=MP)[:, :, 0:M]
                    wait_full(dve, b, "xdq", t)
                    link(nc.vector.tensor_reduce(mq[:, t, :], xq, AX.X, ALU.max))
                    nc.vector.tensor_tensor(qf[:, t, :, 0:M], xq, mq[:, t, :].unsqueeze(2).to_broadcast([P, H, M]),
                                            ALU.subtract).then_inc(evac_of("xdq", t), 1)
                    wait_full(dve, b, "xdk", t)
                    dve.wait_ge(sq_read, b * NT + t + 1)
                    nc.vector.scalar_tensor_tensor(kf[:, t, :, 0:M],
                                                   sq[:, t, H:2 * H].unsqueeze(2).to_broadcast([P, H, M]), -0.5 * SCALE,
                                                   xk, ALU.mult, ALU.add).then_inc(evac_of("xdk", t), 1)
                    nc.vector.scalar_tensor_tensor(gs[:, t, :], sq[:, t, 0:H], -0.5 * SCALE, mq[:, t, :],
                                                   ALU.mult, ALU.add)
                    wait_evac(dve, b, "xdk", t)
                    link(nc.vector.tensor_reduce(mk[:, t, :], kf[:, t, :, 0:M], AX.X, ALU.max))

                def keys_maximum(step):
                    if step == 0:
                        nc.vector.tensor_reduce(mk1[:, :], mk[:, :, :].rearrange("p t h -> p h t"), AX.X, ALU.max)\
                          .then_inc(mk_ready, 1)
                    if step == 1:
                        wait_full(dve, b, "mkT")
                        nc.vector.tensor_reduce(kmx[:, :], bank("mkT")[0:H, 0:P], AX.X, ALU.max).then_inc(evac_of("mkT"), 1)
                        wait_evac(dve, b, "mkT")
                        nc.vector.tensor_scalar(kdg[:, :], ident[0:H, 0:H], kmx[:, 0:1], None, ALU.mult).then_inc(kmax_diag, 1)
                    if step == 2:
                        wait_full(dve, b, "mkB")
                        nc.vector.tensor_copy(kb[:, :], bank("mkB")[:, 0:H]).then_inc(evac_of("mkB"), 1)
                        wait_evac(dve, b, "mkB")
                        for t in range(NT):
                            nc.vector.tensor_tensor(kf[:, t, :, 0:M], kf[:, t, :, 0:M],
                                                    kb[:, :].unsqueeze(2).to_broadcast([P, H, M]), ALU.subtract)\
                              .then_inc(kf_sub, 1)
                        link(nc.vector.tensor_tensor(gs[:, :, :], gs[:, :, :], kb[:, :].unsqueeze(1).to_broadcast([P, NT, H]),
                                                     ALU.add))
                        assert n_links[0] == LINKS["dve_next"], n_links

                return stats_first, normalize_first, add_bias, qk_low, logits, keys_maximum

            def attention(b, first):
                link, n_links = linker(dve, b, "dve")
                def scales(c):
                    dve.wait_ge(nmx_ready, b * NT * (H // 2) + (c + 1) * (H // 2))
                    nc.vector.scalar_tensor_tensor(tt[:, :], nmx[:, :], -1.0, gs[:, c, :], ALU.mult, ALU.subtract)\
                      .then_inc(t_ready, 1)
                    dve.wait_ge(e1_ready, b * NT + c + 1)
                    wait_evac(dve, b, "s", c, H // 2 - 1)
                    wait_evac(dve, b, "s", c, H // 2 - 2)
                    link(nc.vector.tensor_tensor(tt[:, :], e1[:, :], sume[:, :], ALU.mult))
                    link(nc.vector.scalar_tensor_tensor(tt[:, :], gsum[:, :], 1e-24, tt[:, :], ALU.max, ALU.add))
                    link(nc.vector.reciprocal(gps[:, :], tt[:, :]))
                    nc.vector.reciprocal(rs[:, c % 2, :], sume[:, :])
                    link(nc.vector.tensor_tensor(aa[:, :], gps[:, :], sume[:, :], ALU.mult))

                def features_part(c, u):
                    wait_full(dve, b, "sg", c, u)
                    if u >= 2:
                        dve.wait_ge(p_ready, b * NT * (H // 2) + c * (H // 2) + u - 1)
                    for i in range(2):
                        h = 2 * u + i
                        src = bank("sg", c, u)[:, i * 2 * P:(i + 1) * 2 * P].rearrange("p (s n) -> p s n", s=2)
                        ins = nc.vector.scalar_tensor_tensor(
                            GW[:, u % 2, i, 0:slots(c), :], src[:, 0:slots(c), :],
                            aa[:, h:h + 1], win[:, c % 2:c % 2 + slots(c), :], ALU.mult, ALU.mult)
                    ins.then_inc(evac_of("sg", c, u), 1)

                def far_features(c):
                    wait_full(dve, b, "kv", c)
                    nc.vector.tensor_tensor(kvs[:, :, :], bank("kv", c)[:, 0:NG * HG * DH].rearrange("p (g n) -> p g n", g=NG),
                                            blk[:, :].unsqueeze(1).to_broadcast([P, NG, HG * DH]), ALU.mult)\
                      .then_inc(evac_of("kv", c), 1)

                def far_part(c):
                    wait_full(dve, b, "st", c)
                    nc.vector.tensor_tensor(stt[:, :, :], bank("st", c)[:, 0:D].rearrange("p (h d) -> p h d", h=H),
                                            gps[:, :].unsqueeze(2).to_broadcast([P, H, DH]), ALU.mult)\
                      .then_inc(evac_of("st", c), 1)

                scales(0)
                for c in range(NT):
                    for s in range(H // 2):
                        if s == 1 and c:
                            context(b, c - 1)
                        if s == 1 and c >= 2:
                            far_features(c)
                        if s == 2 and c >= 2:
                            far_part(c)
                        if s in (3, 4) and c + 1 < NT:
                            features_low(b, c + 1, s - 3)
                        if c == 1 and s == 5 and first:
                            first[0]()
                        if c == 2 and s >= NT and first:
                            first[1](s - NT)
                        if s == 6 and c:
                            residual(b, c - 1)
                        if c + 1 < NT:
                            maxima(b, c + 1, s)
                        features_part(c, s)
                    if c + 1 < NT:
                        denominator(b, c + 1)
                        scales(c + 1)
                return link, n_links

            def mlstm_part(b, link):
                def stats(src, n, first, done=None):
                    for i in range(n):
                        ins = nc.vector.bn_stats(st6[:, first + i, :], src(i))
                        if i == 0 and done is not None:
                            ins.then_inc(done, 1)
                    link(ins)
                    hold(dve, held["dve"])
                    for i in range(n):
                        ins = nc.vector.bn_aggr(mv[:, first + i, :], st6[:, first + i, :])
                    return ins

                def normalize(k, dst, src, n):
                    dve.wait_ge(ln_rstd, b * (NH + 2) + k)
                    for i in range(n):
                        nc.vector.tensor_scalar(dst(i), src(i), mv[:, NH * NT + i, 0:1], rstd[:, NH * NT + i:NH * NT + i + 1],
                                                ALU.subtract, ALU.mult).then_inc(xhat_ready, 1)

                def gates():
                    wait_full(dve, b, "gate")
                    dve.wait_ge(lsig_ready, b + 1)
                    link(nc.vector.tensor_scalar(rows[32:36, R_MIN, :], bank("gate")[32:36, :], fgb_sb[32:36, :], 0.0,
                                                 ALU.add, ALU.min))
                    link(nc.vector.tensor_tensor(rows[32:36, R_MIN, :], rows[32:36, R_MIN, :], rows[32:36, R_ABS, :], ALU.subtract))
                    link(nc.vector.tensor_tensor_scan(rows[0:4, R_F, :], ones_row[32:36, :], rows[32:36, R_MIN, :], 0.0,
                                                      ALU.mult, ALU.add))
                    nc.vector.scalar_tensor_tensor(rows[0:4, R_G, :], bank("gate")[0:4, :], igb_sb[:, :], rows[0:4, R_F, :],
                                                   ALU.add, ALU.subtract).then_inc(evac_of("gate"), 1)
                    wait_evac(dve, b, "gate")
                    link(nc.vector.tensor_tensor_scan(rows[0:4, R_M, :], rows[0:4, R_G, :], rows[0:4, R_G, :], -3.0e38,
                                                      ALU.max, ALU.max))
                    nc.vector.scalar_tensor_tensor(rows[0:4, R_MIN, :], rows[0:4, R_F, :], -1.0, rows[0:4, R_M, :],
                                                   ALU.mult, ALU.subtract).then_inc(negm_ready, 1)
                    link(nc.vector.tensor_scalar(nmr[0:4, :], rows[0:4, R_M, :], -1.0, None, ALU.mult))
                    nc.vector.scalar_tensor_tensor(nmr[32:36, :], rows[0:4, R_M, :], -1.0, nmr[0:4, :].bitcast(F32),
                                                   ALU.mult, ALU.subtract).then_inc(nm_ready, 1)

                def copy_gates():
                    wait_full(dve, b, "rowT")
                    nc.vector.tensor_copy(gT[:, :, :, :], bank("rowT")[:, 0:NT * 2 * NH].rearrange("p (t w h) -> p t w h", t=NT, w=2))\
                      .then_inc(evac_of("rowT"), 1)

                def weigh(h, tc):
                    n = L - tc * P
                    wait_full(dve, b, "qkm", h, tc)
                    dve.wait_ge(dmask_ready, b * NH * NT + h * NT + tc + 1)
                    nc.vector.scalar_tensor_tensor(ct(h, tc, 0, n), bank("qkm", h, tc)[:, 0:n], XD ** -0.5,
                                                   Dm[:, tc % 2, 0:n], ALU.mult, ALU.mult)\
                      .then_inc(evac_of("qkm", h, tc), 1)

                def head_out(h):
                    wait_full(dve, b, "h", h)
                    hv = bank("h", h)[:, 0:NT * (XD + 1)].rearrange("p (t d) -> p t d", t=NT)
                    nr = nrm[:, h % 2, :]
                    link(nc.vector.tensor_reduce(nr, hv[:, :, XD:XD + 1], AX.X, ALU.max, apply_absolute_value=True))
                    if h == 0:
                        wait_evac(dve, b, "rowT")
                    link(nc.vector.tensor_tensor(nr, nr, gT[:, :, 1, h], ALU.max))
                    link(nc.vector.tensor_scalar(nr, nr, X_EPS, None, ALU.add))
                    link(nc.vector.reciprocal(nr, nr))
                    nc.vector.tensor_tensor(xh[:, :, h * XD:(h + 1) * XD], hv[:, :, 0:XD],
                                            nr.unsqueeze(2).to_broadcast([P, NT, XD]), ALU.mult)\
                      .then_inc(evac_of("h", h), 1)
                    wait_evac(dve, b, "h", h)
                    stats(lambda t: xh[:, t, h * XD:(h + 1) * XD], NT, h * NT).then_inc(ln_stats, 1)

                def normalize_head(h):
                    dve.wait_ge(ln_rstd, b * (NH + 2) + h + 2)
                    r = slice(h * XD, (h + 1) * XD)
                    for t in range(NT):
                        ins = nc.vector.scalar_tensor_tensor(xh[:, t, r], xh[:, t, r], mv[:, h * NT + t, 0:1], onw_bc[:, r],
                                                             ALU.subtract, ALU.mult)
                    link(ins)
                    for t in range(NT):
                        ins = nc.vector.scalar_tensor_tensor(x1[:, t, r], xh[:, t, r], rstd[:, h * NT + t:h * NT + t + 1],
                                                             x1[:, t, r], ALU.mult, ALU.add)
                    return ins

                def stats_last():
                    dve.wait_ge(ctx_free, b + 2)
                    stats(lambda t: x1[:, t, :], NT, NH * NT).then_inc(ln_stats, 1)

                def normalize_last():
                    normalize(NH + 2, lambda t: xh[:, t, :], lambda t: x1[:, t, :], NT)

                def x3_low():
                    for t in range(NT):
                        dve.wait_ge(x3h_ready, b * NT + t + 1)
                        nc.vector.tensor_tensor(x3l[:, :, t * P:(t + 1) * P],
                                                bank("x3T", t)[:, 0:D].rearrange("p (k n) -> p k n", k=KC),
                                                x3h[:, :, t * P:(t + 1) * P].bitcast(F32), ALU.subtract)\
                          .then_inc(evac_of("x3T", t), 1)

                def copy_z():
                    wait_full(dve, b, "z")
                    nc.vector.tensor_scalar(zr[:, 0, :], bank("z")[0:NE, :], -1.0, nbg[:, :], ALU.mult, ALU.add)\
                      .then_inc(evac_of("z"), 1)

                def expert_gates():
                    dve.wait_ge(ez_ready, b + 1)
                    link(nc.vector.tensor_scalar(zt[:, 0, :, :], zt[:, 0, :, :], 1.0, None, ALU.add))
                    link(nc.vector.reciprocal(zt[:, 0, :, :], zt[:, 0, :, :]))
                    nc.vector.scalar_tensor_tensor(zt[:, 1, :, :], zt[:, 0, :, :], 0.5, zt[:, 0, :, :], ALU.is_gt, ALU.mult)\
                      .then_inc(evac_of("zT"), 1)
                    wait_evac(dve, b, "zT")
                    hold(dve, held["dve"])
                    nc.vector.tensor_copy(wtok[:, bass.ds(b * NT, NT), :], zt[:, 1, :, :])

                def add_b2():
                    for t in range(NT):
                        wait_full(dve, b, "b2", t)
                        nc.vector.tensor_tensor(x1[:, t, :], x1[:, t, :], bank("b2", t)[:, 0:D], ALU.add)\
                          .then_inc(evac_of("b2", t), 1)

                return (stats, normalize, gates, copy_gates, weigh, head_out, normalize_head, stats_last, normalize_last,
                        x3_low, copy_z, expert_gates, add_b2)

            def mixed(b, n, first, link, n_links):
                mlstm = b is not None
                if mlstm:
                    (stats, normalize, gates, copy_gates, weigh, head_out, normalize_head, stats_last, normalize_last,
                     x3_low, copy_z, expert_gates, add_b2) = mlstm_part(b, link)
                    context(b, NT - 1)
                if n is not None:
                    stats_first, normalize_first, add_bias, qk_low, logits, keys_maximum = first
                    if not mlstm:
                        stats_first()
                        for t in range(NT):
                            normalize_first(t)
                    add_bias(0)
                if mlstm:
                    residual(b, NT - 1)
                    wait_evac(dve, b, "proj", NT - 1)
                    stats(lambda t: x1[:, t, :], NT, NH * NT, x_free).then_inc(ln_stats, 1)
                if n is not None:
                    add_bias(1)
                if mlstm:
                    normalize(1, lambda t: xh[:, t, :], lambda t: x1[:, t, :], NT)
                if n is not None:
                    qk_low(0)
                    add_bias(2)
                if mlstm:
                    gates()
                if n is not None:
                    qk_low(1)
                if mlstm:
                    copy_gates()
                if n is not None:
                    add_bias(3)
                for h in range(NH + 1):
                    if mlstm and h < NH:
                        weigh(h, 0)
                        weigh(h, 1)
                    if n is not None and h < NT:
                        logits(h)
                    if mlstm and h < NH:
                        weigh(h, 2)
                    if mlstm and h < NH:
                        weigh(h, 3)
                    if n is not None and h + 2 < NT:
                        qk_low(h + 2)
                    if n is not None and h == NT - 1:
                        keys_maximum(0)
                    if mlstm and h:
                        head_out(h - 1)
                        if n is None:
                            dve.wait_ge(w_high, h)
                            nc.vector.tensor_tensor(first_piece(h - 1, 1), wraw[:, (h - 1) % 2, :],
                                                    first_piece(h - 1, 0).bitcast(F32), ALU.subtract).then_inc(w_split, 1)
                    if n is not None and h == NT:
                        keys_maximum(1)
                    if mlstm and h >= 2:
                        normalize_head(h - 2)
                if n is not None:
                    keys_maximum(2)
                if mlstm:
                    normalize_head(NH - 1).then_inc(ctx_free, 1)
                    stats_last()
                if n is not None:
                    features_low(n, 0, 0)
                    maxima(n, 0, 0)
                if mlstm:
                    normalize_last()
                if n is not None:
                    maxima(n, 0, 1)
                if mlstm:
                    x3_low()
                if n is not None:
                    features_low(n, 0, 1)
                    denominator(n, 0)
                if mlstm:
                    copy_z()
                for u in range(2, H // 2):
                    if u == 4 and mlstm:
                        expert_gates()
                    if n is not None:
                        maxima(n, 0, u)
                if mlstm:
                    add_b2()
                    assert n_links[0] == LINKS["dve"], ("dve", n_links)

            mixed(None, 0, first_part(0), None, None)
            with dve.Fori(0, NB - 1) as b:
                first = first_part(b + 1)
                mixed(b, b + 1, first, *attention(b, first))
            mixed(NB - 1, None, None, *attention(NB - 1, None))

        @block.tensor
        def _(pe):
            pe.wait_ge(consts_ready, CONSTS_READY)
            emitted = []

            def begin(b, *name):
                emitted.append((name, BANK_OF[name]))
                wait_bank(pe, b, *name)
                return bank(*name)

            def end(ins, *name):
                ins.then_inc(full_of(*name), 1)

            def turn(b, name, t, src):
                dst = begin(b, name, t)
                for k in range(KC):
                    ins = nc.tensor.transpose(dst[:, k * P:(k + 1) * P], src(k), ident[:, :])
                end(ins, name, t)

            def turn_features(b, c, w):
                name, f, ready = (("qfT", qf, qf_ready), ("kfT", kf, kf_ready))[w]
                pe.wait_ge(ready, b * NT + c + 1)
                dst = begin(b, name, c)
                for g in range(NG):
                    ins = nc.tensor.transpose(dst[:, g * P:(g + 1) * P],
                                              f[:, c, g * HG:(g + 1) * HG, :].rearrange("p h m -> p (h m)"), ident[:, :])
                end(ins, name, c)

            def sum_features(b, c):
                dst = begin(b, "u", c)
                for j in range(c + 1):
                    w = wdT if j == c else wpT if j == c - 1 else ones
                    ins = nc.tensor.matmul(dst[:, :], w[:, :], kf[:, j, :, :].rearrange("p h m -> p (h m)"),
                                           start=j == 0, stop=j == c)
                end(ins, "u", c)

            def scores(b, c, u):
                if u % (H // 4) == 0:
                    pe.wait_ge(qs_loaded[u // (H // 4)], b * 96 * NT + 96 * (c + 1))
                dst = begin(b, "s", c, u)
                nc.tensor.matmul(dst[:, :], identr[:, :],
                                 maskr[:, c % 2:c % 2 + 2, :].unsqueeze(1).to_broadcast([P, 2, 2, P]),
                                 start=True, stop=False, skip_group_check=True)
                for i in range(2):
                    h = 2 * u + i
                    ins = nc.tensor.matmul(dst[:, i * 256:(i + 1) * 256], qs[:, h, :],
                                           ks[:, h, :, :].rearrange("p s n -> p (s n)"),
                                           start=False, stop=i == 1, skip_group_check=True)
                end(ins, "s", c, u)

            def turn_x(b, t):
                if b is None:
                    return
                pe.wait_ge(ln1_ready, b * NT + t + 1)
                turn(b, "x1T", t, lambda k: xh[:, t, k * P:(k + 1) * P])

            def turn_out(b, c):
                wait_evac(pe, b, "pv", c)
                dst = begin(b, "oT", c)
                for g in range(NG):
                    ins = nc.tensor.transpose(dst[:, g * P:(g + 1) * P], OT[:, g, :], ident[:, :])
                end(ins, "oT", c)

            def turn_context(b, c):
                if c >= 2:
                    pe.wait_ge(c_ready, b * 2 + c - 1)
                else:
                    wait_evac(pe, b, "oT", c)
                dst = begin(b, "cT", c)
                cr = cc[:, :, :].rearrange("p h d -> p (h d)")
                for k in range(KC):
                    ins = nc.tensor.transpose(dst[:, k * P:(k + 1) * P], cr[:, k * P:(k + 1) * P], ident[:, :])
                end(ins, "cT", c)

            def project_out(b, c):
                wait_evac(pe, b, "cT", c)
                dst = begin(b, "proj", c)
                for k in range(KC):
                    ins = nc.tensor.matmul(dst[:, 0:D], cT[:, k, :], wo_sb[:, k, :], start=k == 0, stop=k == KC - 1)
                end(ins, "proj", c)

            def first_part(b):
                def project(t):
                    wait_evac(pe, b, "x1T", t)
                    dst = begin(b, "qk", t)
                    for k in range(KC):
                        ins = nc.tensor.matmul(dst[:, :], xT_n[:, k, t * P:(t + 1) * P], wqkv_sb[:, k, 0:2 * D],
                                               start=k == 0, stop=k == KC - 1)
                    end(ins, "qk", t)
                    dst = begin(b, "v", t)
                    for k in range(KC):
                        ins = nc.tensor.matmul(dst[:, 0:D], xT_n[:, k, t * P:(t + 1) * P], wqkv_sb[:, k, 2 * D:3 * D],
                                               start=k == 0, stop=k == KC - 1)
                    end(ins, "v", t)

                def turn_qk(t):
                    wait_evac(pe, b, "qk", t)
                    dst = begin(b, "qkT", t)
                    for j in range(4):
                        ins = nc.tensor.transpose(dst[:, j * P:(j + 1) * P], qk_tm[:, t % 2, j * P:(j + 1) * P], ident[:, :])
                    end(ins, "qkT", t)

                def random_features(t):
                    wait_evac(pe, b, "qkT", t)
                    for name, j0 in (("xdq", 0), ("xdk", 2)):
                        dst = begin(b, name, t)
                        for j in range(2):
                            parts = ((0, pdh), (0, pdl), (1, pdh))
                            for i, (s, w) in enumerate(parts):
                                ins = nc.tensor.matmul(dst[:, j * 256:(j + 1) * 256], qkhl[:, t % 2, s, j0 + j, :],
                                                       w[:, :, :].rearrange("p h m -> p (h m)"),
                                                       start=i == 0, stop=i == len(parts) - 1)
                        end(ins, name, t)

                return project, turn_qk, random_features

            def attention(b, n):
                def far_keys(c):
                    dst = begin(b, "kv", c)
                    for g in range(NG):
                        for j in range(c - 1):
                            ins = nc.tensor.matmul(dst[:, g * 64:(g + 1) * 64],
                                                   kf[:, j, g * HG:(g + 1) * HG, :].rearrange("p h m -> p (h m)"),
                                                   v_tm[:, j, g * HG:(g + 1) * HG, 0:DH], start=j == 0, stop=j == c - 2)
                    end(ins, "kv", c)

                def far_queries(c):
                    wait_evac(pe, b, "kv", c)
                    pe.wait_ge(fh_ready, b * 2 * NT + 2 * c + 1)
                    dst = begin(b, "st", c)
                    for g in range(NG):
                        ins = nc.tensor.matmul(dst[:, g * 64:(g + 1) * 64], qf32[:, g, :], kvs[:, g, :],
                                               start=True, stop=True)
                    end(ins, "st", c)

                def feature_scores(c, u):
                    if u % (H // 4) == 0:
                        pe.wait_ge(fs_loaded[u // (H // 4)], b * 96 * NT + 96 * (c + 1))
                    dst = begin(b, "sg", c, u)
                    for i in range(2):
                        h = 2 * u + i
                        ins = nc.tensor.matmul(dst[:, i * 256:(i + 1) * 256], qfs[:, h, :],
                                               kfs[:, h, :, :].rearrange("p s n -> p (s n)"), start=True, stop=True)
                    end(ins, "sg", c, u)

                def turn_probs(c, u):
                    pe.wait_ge(p_ready, b * NT * (H // 2) + c * (H // 2) + u + 1)
                    dst = begin(b, "pT", c, u)
                    for i in range(2):
                        for k in range(slots(c)):
                            at_ = (i * slots(c) + k) * P
                            ins = nc.tensor.transpose(dst[:, at_:at_ + P], E2[c % 2][:, 2 * u + i, k, :], ident[:, :])
                    end(ins, "pT", c, u)

                def probs_times_v(c, u):
                    wait_evac(pe, b, "pT", c, u)
                    dst = begin(b, "pv", c) if u == 0 else bank("pv", c)
                    for i in range(2):
                        h = 2 * u + i
                        q = h % HG
                        for k in range(slots(c)):
                            chunk = c if k == c % 2 else c - 1
                            ins = nc.tensor.matmul(dst[MP * q:MP * q + MP, (h // HG) * P:(h // HG + 1) * P],
                                                   v_tm[:, chunk, h, :], PT[:, u % 2, i, k, :],
                                                   start=k == 0, stop=k == slots(c) - 1)
                    if u == H // 2 - 1:
                        end(ins, "pv", c)

                for c in range(NT):
                    for s in range(H // 2 + 3):
                        if s < H // 2:
                            if c + 1 < NT:
                                scores(b, c + 1, s)
                            feature_scores(c, s)
                        if 2 <= s < H // 2 + 2:
                            turn_probs(c, s - 2)
                        if s >= 3:
                            probs_times_v(c, s - 3)
                        if s == 0 and c:
                            turn_out(b, c - 1)
                        if s == 0 and c >= 2:
                            far_keys(c)
                        if s == 1 and c >= 2:
                            far_queries(c)
                        if c == 0 and s in CTX_STEPS:
                            if s == 0:
                                pe.wait_ge(ctxt_loaded, b * 16 + 16)
                            t = CTX_STEPS.index(s)
                            turn(b, "cxT", t, lambda k: ctx_t[:, t, k * P:(k + 1) * P])
                        if s in (2, 3) and c + 1 < NT:
                            turn_features(b, c + 1, s - 2)
                        if s == 4 and c:
                            turn_context(b, c - 1)
                        if s == 5 and c:
                            project_out(b, c - 1)
                        if s == 6 and c + 1 < NT:
                            sum_features(b, c + 1)
                        if c == NT - 1 and s in X_STEPS:
                            turn_x(n, X_STEPS.index(s))

            def mlstm_products(b, h, tc):
                dst = begin(b, "qkm", h, tc)
                end(nc.tensor.matmul(dst[:, 0:L - tc * P], cxT[:, h % 2, h // 2, tc * P:(tc + 1) * P],
                                     xT[:, h // 2, tc * P:L], start=True, stop=True), "qkm", h, tc)

            def mlstm_values(b, h):
                wait_evac(pe, b, "qkm", h, NT - 1)
                wait_evac(pe, b, "qkm", h, NT - 2)
                if h == 0:
                    pe.wait_ge(ctx_loaded, b * 16 * NT + 16 * NT)
                dst = begin(b, "h", h)
                for sc in range(NT):
                    for tc in range(sc + 1):
                        ins = nc.tensor.matmul(dst[:, sc * (XD + 1):(sc + 1) * (XD + 1)],
                                               ct(h, tc, (sc - tc) * P, (sc - tc + 1) * P), ctx_in[:, tc, h, :],
                                               start=tc == 0, stop=tc == sc)
                end(ins, "h", h)

            def mixed(b, n):
                mlstm = b is not None
                if mlstm:
                    turn_out(b, NT - 1)
                if n is not None:
                    project, turn_qk, random_features = first_part(n)
                    if not mlstm:
                        for t in range(NT):
                            turn_x(n, t)
                    project(0)
                if mlstm:
                    turn_context(b, NT - 1)
                    project_out(b, NT - 1)
                if n is not None:
                    project(1)
                if mlstm:
                    gate = begin(b, "gate")
                    srcs = [(KC + k, cxT[:, i, k, :]) for k in range(KC) for i in range(2)] + [(k, xT[:, k, :]) for k in range(KC)]

                    def add_gates(first, last):
                        for m in range(first, last):
                            k, src = srcs[m]
                            ins = nc.tensor.matmul(gate[0:36, :], gk[:, k, :], src, start=m == 0, stop=m == len(srcs) - 1)
                        return ins

                    add_gates(0, 2 * KC)
                if n is not None:
                    turn_qk(0)
                if mlstm:
                    for t in range(NT):
                        pe.wait_ge(xhat_ready, b * 2 * NT + t + 1)
                        turn(b, "x2T", t, lambda k: xh[:, t, k * P:(k + 1) * P])
                    wait_evac(pe, b, "x2T", NT - 1)
                    wait_evac(pe, b, "x2T", NT - 2)
                    end(add_gates(2 * KC, 3 * KC), "gate")
                if n is not None:
                    project(2)
                    turn_qk(1)
                    project(3)
                if mlstm:
                    pe.wait_ge(expn_ready, b + 1)
                    dst = begin(b, "rowT")
                    hold(pe, held["pe"])
                    for t in range(NT):
                        for w, r in enumerate((R_G, R_ABS)):
                            o = (t * 2 + w) * NH
                            ins = nc.tensor.transpose(dst[:, o:o + NH], rows[0:4, r, t * P:(t + 1) * P], ident[0:4, 0:4])
                    end(ins, "rowT")
                    pe.wait_ge(nm_ready, b + 1)
                for h in range(NH + 1):
                    if n is not None and h == NT:
                        pe.wait_ge(mk_ready, n + 1)
                        dst = begin(n, "mkT")
                        end(nc.tensor.transpose(dst[0:H, 0:P], mk1[:, :], ident[:, :]), "mkT")
                    if mlstm and h < NH:
                        dst = begin(b, "mB", h)
                        end(nc.tensor.matmul(dst[:, :], selr[:, h, :], nmr[:, :], start=True, stop=True), "mB", h)
                        mlstm_products(b, h, 0)
                        mlstm_products(b, h, 1)
                    if n is not None and h < NT:
                        random_features(h)
                    if mlstm and h < NH:
                        mlstm_products(b, h, 2)
                    if mlstm and h < NH:
                        mlstm_products(b, h, 3)
                    if n is not None and h + 2 < NT:
                        turn_qk(h + 2)
                    if mlstm and h:
                        mlstm_values(b, h - 1)
                if n is not None:
                    pe.wait_ge(kmax_diag, n + 1)
                    dst = begin(n, "mkB")
                    end(nc.tensor.matmul(dst[:, 0:H], ones[0:H, :], kdg[:, :], start=True, stop=True), "mkB")
                    turn_features(n, 0, 0)
                    for u in (0, 1):
                        scores(n, 0, u)
                    turn_features(n, 0, 1)
                    sum_features(n, 0)
                    for u in (2, 3):
                        scores(n, 0, u)
                if mlstm:
                    for t in range(NT):
                        pe.wait_ge(xhat_ready, b * 2 * NT + NT + t + 1)
                        turn(b, "x3T", t, lambda k: xh[:, t, k * P:(k + 1) * P])
                if mlstm:
                    wait_evac(pe, b, "x3T", NT - 1)
                    wait_evac(pe, b, "x3T", NT - 2)
                    dst = begin(b, "z")
                    zp = [(k, a, w) for k in range(KC) for a, w in ((x3h, wgh), (x3l, wgh), (x3h, wgl))]
                    for i, (k, a, w) in enumerate(zp):
                        ins = nc.tensor.matmul(dst[0:NE, :], w[:, k, :], a[:, k, :], start=i == 0, stop=i == len(zp) - 1)
                    end(ins, "z")
                for u in range(4, H // 2):
                    if u == 4 and mlstm:
                        wait_evac(pe, b, "z")
                        dst = begin(b, "zT")
                        hold(pe, held["pe"])
                        for t in range(NT):
                            ins = nc.tensor.transpose(dst[:, t * NE:(t + 1) * NE], zr[:, 0, t * P:(t + 1) * P], ident[0:NE, 0:NE])
                        end(ins, "zT")
                    if u == 6 and mlstm:
                        wait_evac(pe, b, "zT")
                        dst = begin(b, "wR")
                        for t in range(NT):
                            ins = nc.tensor.transpose(dst[0:NE, t * P:(t + 1) * P], zt[:, 1, t, :], ident[:, :])
                        end(ins, "wR")
                    if n is not None:
                        scores(n, 0, u)
                if mlstm:
                    wait_evac(pe, b, "wR")
                    for t in range(NT):
                        dst = begin(b, "b2", t)
                        end(nc.tensor.matmul(dst[:, 0:D], zr[:, 1, t * P:(t + 1) * P], b2_sb[:, :], start=True, stop=True), "b2", t)


            mixed(None, 0)
            emitted.clear()
            with pe.Fori(0, NB - 1) as b:
                attention(b, b + 1)
                mixed(b, b + 1)
            assert emitted == GROUPS, [x for x in zip(emitted, GROUPS) if x[0] != x[1]][:2]
            attention(NB - 1, None)
            mixed(NB - 1, None)


def ffn_phase(nc, sem, banks, wtok, w1, b1, w2, x2_dram, x3_dram, out, weights):
    split0, wraw, w_loaded, w_high, w_split = weights
    b1_loaded = [sem("b1_loaded%d" % i) for i in range(2)]
    held_sp, held_pool = sem("held_sp2"), sem("held_pool2")
    group_loaded, x2_loaded = sem("group_loaded"), sem("x2_loaded")
    up_full, hid_ready, hid_split = sem("up_full"), sem("hid_ready"), sem("hid_split")
    down_full, gate_copied, acc_done, out_stored = sem("down_full"), sem("gate_copied"), sem("acc_done"), sem("out_stored")
    RING = 4
    CREDIT = 2 * NGRP
    with ExitStack() as stack:
        def sb(name, shape, dt=F32):
            return stack.enter_context(nc.sbuf_tensor(name, shape, dt))

        x3 = sb("x3", [P, NGRP, 2, KC, L], F32R)
        acc = sb("acc", [P, NB * NT, D])
        split = [split0, sb("split1", [P, 2, 2, 2 * PCOLS], F32R)]
        w1p = [w[:, 0, :, :].rearrange("p w (c n) -> p w c n", c=KC) for w in split]
        w2p = [w[:, 1, :, :].rearrange("p w (k n) -> p w k n", k=NK) for w in split]
        b1p = sb("b1p", [P, 2, NK])
        hid = sb("hid", [P, RING, L])
        hidr = sb("hidr", [P, RING, 2, L], F32R)
        gate = sb("gate", [P, 2, NT])
        up = [banks[k] for k in ("A0", "A1", "B0", "B1")]
        down = [banks[k] for k in ("C0", "C1", "D", "E")]

        def piece(parity, part, j):
            return split[parity][:, j // 2, part, (j % 2) * PCOLS:(j % 2 + 1) * PCOLS]

        def over_groups(eng, body):
            body(0, 0, True, False)
            with eng.Fori(0, NGRP // 2 - 1) as j:
                body(2 * j + 1, 1, False, False)
                body(2 * j + 2, 0, False, False)
            body(NGRP - 1, 1, False, True)

        block = stack.enter_context(nc.Block())

        @block.sync
        def _(sp):
            def next_piece(e, j):
                sp.wait_ge(w_split, PIECES * e + j + 1)
                hold(sp, held_sp)
                load_piece(sp, w1, w2, wraw, w_loaded, e, j)

            def load_biases(e, parity):
                sp.dma_start(b1p[:, parity, :], b1[bass.ds(e, 1), :, :].rearrange("o p k -> p (o k)")).then_inc(b1_loaded[parity], 16)

            def load_expert(e, parity):
                next_piece(e, 0)
                next_piece(e, 1)
                sp.wait_ge(acc_done, NGRP * e + NGRP)
                hold(sp, held_sp)
                load_biases(e, parity)
                next_piece(e, 2)
                next_piece(e, 3)

            def load_group(g):
                for s in range(2):
                    sp.dma_start(x3[:, g, s, :, :].bitcast(F32), x3_dram[g, s, :, :, :]).then_inc(group_loaded, 16)
                sp.dma_start(acc[:, g * NT:(g + 1) * NT, :], x2_dram[g, :, :, :]).then_inc(x2_loaded, 16)

            load_group(0)
            load_biases(0, 0)
            for g in range(1, NGRP):
                sp.wait_ge(group_loaded, 32 * g)
                sp.wait_ge(x2_loaded, 16 * g)
                load_group(g)
            load_expert(1, 1)
            with sp.Fori(1, NE // 2) as i:
                load_expert(2 * i, 0)
                load_expert(2 * i + 1, 1)
            with sp.Fori(0, NGRP) as g:
                sp.wait_ge(acc_done, g + (CREDIT + (NE - 1) * NGRP + 1))
                hold(sp, held_sp)
                sp.dma_start(out[bass.ds(g, 1), :, :].rearrange("o (t p) d -> p (o t) d", p=P),
                             acc[:, bass.ds(g * NT, NT), :]).then_inc(out_stored, 16)
            sp.wait_ge(out_stored, 16 * NGRP)

        @block.gpsimd
        def _(pool):
            pool.sem_inc(acc_done, CREDIT)

            def split_expert(e, parity):
                pool.wait_ge(acc_done, NGRP * e + NGRP)
                for j in range(PIECES):
                    pool.wait_ge(w_loaded[j % 2], 16 * (PIECES // 2) * e + 16 * (j // 2 + 1))
                    hold(pool, held_pool)
                    split_piece(nc, pool, piece(parity, 0, j), piece(parity, 1, j), wraw[:, j % 2, :],
                                w_high, w_split, PIECES * e + j + 1)

            split_expert(1, 1)
            with pool.Fori(1, NE // 2) as i:
                split_expert(2 * i, 0)
                split_expert(2 * i + 1, 1)

        @block.scalar
        def _(act):
            with act.Fori(0, NE // 2) as i:
                for parity in range(2):
                    e = 2 * i + parity
                    act.wait_ge(b1_loaded[parity], 16 * i + 16)

                    def group(g, gp, first, last):
                        for k in range(NK):
                            n = (e * NGRP + g) * NK + k
                            act.wait_ge(up_full, n + 1)
                            b = b1p[:, parity, k:k + 1]
                            nc.scalar.activation(hidr[:, k % RING, 0, :], up[k % RING][:, :], ACT.Relu, bias=b)
                            nc.scalar.activation(hid[:, k % RING, :], up[k % RING][:, :], ACT.Relu, bias=b)\
                              .then_inc(hid_ready, 1)

                    over_groups(act, group)

        @block.vector
        def _(dve):
            with dve.Fori(0, NE // 2) as i:
                for parity in range(2):
                    e = 2 * i + parity

                    def accumulate(g, gp):
                        dve.wait_ge(gate_copied, e * NGRP + g + 1)
                        dve.wait_ge(x2_loaded, 16 * g + 16)
                        dve.wait_ge(down_full, e * NGRP + g + 1)
                        for t in range(NT):
                            a = acc[:, bass.ds(g * NT + t, 1), :].rearrange("p o d -> p (o d)")
                            ins = nc.vector.scalar_tensor_tensor(a, down[2 * gp + t // 2][:, (t % 2) * D:(t % 2 + 1) * D],
                                                                 gate[:, gp, t:t + 1], a, ALU.mult, ALU.add)
                        ins.then_inc(acc_done, 1)

                    def group(g, gp, first, last):
                        nc.vector.tensor_copy(gate[:, gp, :], wtok[:, bass.ds(g * NT, NT), bass.ds(e, 1)]
                                              .rearrange("p t o -> p (t o)")).then_inc(gate_copied, 1)
                        for k in range(NK):
                            n = (e * NGRP + g) * NK + k
                            dve.wait_ge(hid_ready, n + 1)
                            nc.vector.tensor_tensor(hidr[:, k % RING, 1, :], hid[:, k % RING, :],
                                                    hidr[:, k % RING, 0, :].bitcast(F32), ALU.subtract)\
                              .then_inc(hid_split, 1)
                            if k == 1 and not first:
                                accumulate(g - 1, 1 - gp)
                        if last:
                            accumulate(g, gp)

                    over_groups(dve, group)

        @block.tensor
        def _(pe):
            def x3_part(g, s, k):
                return x3[:, bass.ds(g, 1), s, k, :].rearrange("p o n -> p (o n)")

            with pe.Fori(0, NE // 2) as i:
                for parity in range(2):
                    e = 2 * i + parity

                    def up_step(g, k):
                        dst = up[k % RING]
                        prods = [(s, w, c) for c in range(KC) for s, w in ((0, 0), (0, 1), (1, 0))]
                        for m, (s, w, c) in enumerate(prods):
                            ins = nc.tensor.matmul(dst[:, :], w1p[parity][:, w, c, k * P:(k + 1) * P], x3_part(g, s, c),
                                                   start=m == 0, stop=m == len(prods) - 1)
                        ins.then_inc(up_full, 1)

                    pe.wait_ge(w_split, PIECES * e + KC + 2)
                    if parity == 0:
                        pe.wait_ge(group_loaded, 32)
                    up_step(0, 0)

                    def group(g, gp, first, last):
                        G = e * NGRP + g
                        for k in range(NK):
                            if k + 1 < NK:
                                up_step(g, k + 1)
                            elif not last:
                                pe.wait_ge(group_loaded, 32 * (g + 1) + 32)
                                up_step(g + 1, 0)
                            pe.wait_ge(hid_split, G * NK + k + 1)
                            if k == 0:
                                pe.wait_ge(w_split, PIECES * e + PIECES + 2)
                                pe.wait_ge(acc_done, G + CREDIT - 1)
                            for t in range(NT):
                                dst = down[2 * gp + t // 2][:, (t % 2) * D:(t % 2 + 1) * D]
                                for m, (s, w) in enumerate(((0, 0), (0, 1), (1, 0))):
                                    ins = nc.tensor.matmul(dst, hidr[:, k % RING, s, t * P:(t + 1) * P], w2p[parity][:, w, k, :],
                                                           start=k == 0 and m == 0 and t % 2 == 0, stop=k == NK - 1 and m == 2,
                                                           skip_group_check=True)
                        ins.then_inc(down_full, 1)

                    over_groups(pe, group)


_OUT = (NB, L, D)


def kernel(x, ctx_1024, L0_attn_Wqkv_w, L0_attn_Wqkv_b, L0_attn_proj, L0_attn_out_w, L0_attn_out_b,
           L0_xattn_ig_kernel, L0_xattn_ig_bias, L0_xattn_fg_kernel, L0_xattn_fg_bias, L0_xattn_outnorm_weight,
           L0_ffn_Wg, L0_ffn_bg, L0_ffn_W1, L0_ffn_b1, L0_ffn_W2, L0_ffn_b2):
    import numpy as np
    import concourse.bacc as bacc
    from concourse.bass_utils import run_bass_kernel_spmd

    layout = {
        "x": x, "ctx": ctx_1024, "wqkv": np.asarray(L0_attn_Wqkv_w).T, "bqkv": L0_attn_Wqkv_b,
        "proj": np.asarray(L0_attn_proj).T, "wo": np.asarray(L0_attn_out_w).T, "bo": L0_attn_out_b,
        "igk": L0_xattn_ig_kernel, "igb": np.asarray(L0_xattn_ig_bias).reshape(NH, 1),
        "fgk": L0_xattn_fg_kernel, "fgb": np.asarray(L0_xattn_fg_bias).reshape(NH, 1),
        "onw": np.asarray(L0_xattn_outnorm_weight).reshape(D),
        "wg": L0_ffn_Wg, "bg": np.asarray(L0_ffn_bg).reshape(NE, 1), "w1": L0_ffn_W1,
        "b1": np.asarray(L0_ffn_b1).reshape(NE, NK, P).transpose(0, 2, 1), "w2": L0_ffn_W2, "b2": L0_ffn_b2,
    }
    nc = bacc.Bacc("TRN2", target_bir_lowering=False, num_devices=1)
    arrays, aps = {}, {}
    for name, a in layout.items():
        a = np.ascontiguousarray(a)
        arrays["in_" + name] = a
        aps[name] = nc.dram_tensor("in_" + name, a.shape, mybir.dt.from_np(a.dtype), kind="ExternalInput").ap()
    out = nc.dram_tensor("out_dram", _OUT, F32, kind="ExternalOutput").ap()
    decoder_kernel(nc, out=out, **aps)
    r = run_bass_kernel_spmd(nc, [arrays], core_ids=[0])
    return r.results[0]["out_dram"]
```
